# Optimizing a Trainium2 kernel written in Bass

```python
import numpy as np
import jax
import jax.numpy as jnp

def _softmax(x, axis=-1):
    return jax.nn.softmax(x, axis=axis)

def _gelu(x):
    return jax.nn.gelu(x, approximate=True)

def _silu(x):
    return jax.nn.silu(x)

def _sigmoid(x):
    return jax.nn.sigmoid(x)

def _layernorm(x, axis=-1, eps=1e-05):
    m = jnp.mean(x, axis=axis, keepdims=True)
    v = jnp.var(x, axis=axis, keepdims=True)
    return (x - m) / jnp.sqrt(v + eps)

def _scatter_add(tgt, idx, src, axis=0):
    return tgt.at[idx].add(src)

def _segment_sum(src, seg, n):
    return jax.ops.segment_sum(src, seg, n)
kernel_name = 'mk_gps_d2_gnn_r32_a1d1ba'

def setup_inputs(seed: int=0):
    np.random.seed(seed)
    _w = jnp.asarray

    def _rec_inputs():
        import jax
        import jax.numpy as jnp
        _gk = jax.random.key(seed)
        x = -0.0003713 + 1 * jax.random.normal(jax.random.fold_in(_gk, 1), (3125, 256), jnp.float32)
        src = jax.random.randint(jax.random.fold_in(_gk, 2), (50000,), 0, 3125, jnp.int32)
        dst = jnp.minimum((3125 * jax.random.uniform(jax.random.fold_in(_gk, 3), (50000,)) ** 2.0).astype(jnp.int32), 99999)
        _o = jnp.argsort(dst, stable=True)
        src = src[_o]
        dst = dst[_o]
        edge_attr_3 = -1.09012e-05 + 0.99985 * jax.random.normal(jax.random.fold_in(_gk, 11), (50000, 3), jnp.float32)
        return (x, src, dst, edge_attr_3)
    x, src, dst, edge_attr_3 = _rec_inputs()

    def _L0_gnn_setup():
        import jax, jax.numpy as jnp
        import numpy as np
        N = 50000
        E = 12500
        IN = 256
        H = 8
        D = 32
        EF = 3
        key = jax.random.key(seed)
        ks = jax.random.split(key, 8)
        x = jax.random.normal(ks[0], (N, IN), dtype=jnp.float32)
        edge_index = jax.random.randint(ks[1], (2, E), 0, N, dtype=jnp.int64)
        edge_attr = jax.random.normal(ks[2], (E, EF), dtype=jnp.float32)
        W = jax.random.normal(ks[3], (H * D, IN), dtype=jnp.float32) * np.float32(np.sqrt(2.0 / (IN + H * D)))
        a_src = jax.random.normal(ks[4], (H, D), dtype=jnp.float32) * np.float32(np.sqrt(2.0 / (H + D)))
        a_dst = jax.random.normal(ks[5], (H, D), dtype=jnp.float32) * np.float32(np.sqrt(2.0 / (H + D)))
        edge_W = jax.random.normal(ks[6], (H * D, EF), dtype=jnp.float32) * np.float32(np.sqrt(2.0 / (EF + H * D)))
        edge_b = jnp.zeros((H * D,), dtype=jnp.float32)
        bias = jnp.zeros((H * D,), dtype=jnp.float32)
        return {'x': x, 'W': W, 'a_src': a_src, 'a_dst': a_dst, 'edge_W': edge_W, 'edge_b': edge_b, 'bias': bias, 'edge_attr': edge_attr, 'edge_index': edge_index}
    _L0_gnn_all = _L0_gnn_setup()
    _L0_gnn_in = {k: v for k, v in _L0_gnn_all.items() if k in ('W', 'a_src', 'a_dst', 'edge_W', 'edge_b', 'bias')}
    del _L0_gnn_all

    def _L0_mix_setup():
        import jax, jax.numpy as jnp
        import numpy as np
        import math
        EMBED = 256
        HEADS = 4
        HEAD_DIM = EMBED // HEADS
        OUT_DIM = 256
        LN_EPS = 1e-05

        def _qkv_init(key):
            spread = math.sqrt(3.0 / EMBED)
            gain, delta = (0.01, 0.01)
            w = jax.random.uniform(key, (EMBED, EMBED), minval=-spread, maxval=spread) * gain
            return w + delta * jnp.eye(EMBED, dtype=w.dtype)

        def _layer_norm(x, g, b):
            mu = jnp.mean(x, axis=-1, keepdims=True)
            var = jnp.mean(jnp.square(x - mu), axis=-1, keepdims=True)
            return (x - mu) * jax.lax.rsqrt(var + LN_EPS) * g + b

        def _split_heads(x, B, S):
            return x.reshape(B, S, HEADS, HEAD_DIM).transpose(0, 2, 1, 3)
        key = jax.random.key(seed)
        ks = jax.random.split(key, 6)
        seq = jax.random.normal(ks[0], (4, 256, EMBED), dtype=jnp.float32)
        wq = _qkv_init(ks[1])
        wk = _qkv_init(ks[2])
        wv = _qkv_init(ks[3])
        bound = 1.0 / math.sqrt(EMBED)
        wo = jax.random.uniform(ks[4], (OUT_DIM, EMBED), minval=-bound, maxval=bound)
        bo = jax.random.uniform(ks[5], (OUT_DIM,), minval=-bound, maxval=bound)
        ln_k_g = jnp.ones((HEAD_DIM,), jnp.float32)
        ln_k_b = jnp.zeros((HEAD_DIM,), jnp.float32)
        ln_v_g = jnp.ones((HEAD_DIM,), jnp.float32)
        ln_v_b = jnp.zeros((HEAD_DIM,), jnp.float32)
        return {'seq': seq, 'wq': wq, 'wk': wk, 'wv': wv, 'wo': wo, 'bo': bo, 'ln_k_g': ln_k_g, 'ln_k_b': ln_k_b, 'ln_v_g': ln_v_g, 'ln_v_b': ln_v_b}
    _L0_mix_all = _L0_mix_setup()
    _L0_mix_in = {k: v for k, v in _L0_mix_all.items() if k in ('wq', 'wk', 'wv', 'wo', 'bo', 'ln_k_g', 'ln_k_b', 'ln_v_g', 'ln_v_b')}
    del _L0_mix_all

    def _L0_ffn_setup():
        import math
        import jax, jax.numpy as jnp
        import numpy as np
        CAPACITY_FACTOR = 1.25
        key = jax.random.key(seed)
        ks = jax.random.split(key, 5)
        B, L, D, F, E = (8, 256, 256, 1024, 8)
        h = jax.random.normal(ks[0], (B, L, D), dtype=jnp.float32)
        gate_w = jax.random.normal(ks[1], (D, E), dtype=jnp.float32) * 0.02
        gate_b = jnp.zeros((E,), dtype=jnp.float32)
        w1 = jax.random.normal(ks[2], (E, D, F), dtype=jnp.float32) * (1.0 / math.sqrt(D))
        b1 = jnp.zeros((E, F), dtype=jnp.float32)
        w2 = jax.random.normal(ks[3], (E, F, D), dtype=jnp.float32) * (1.0 / math.sqrt(F))
        b2 = jnp.zeros((E, D), dtype=jnp.float32)
        return {'h': h, 'gate_w': gate_w, 'gate_b': gate_b, 'w1': w1, 'b1': b1, 'w2': w2, 'b2': b2}
    _L0_ffn_all = _L0_ffn_setup()
    _L0_ffn_in = {k: v for k, v in _L0_ffn_all.items() if k in ('gate_w', 'gate_b', 'w1', 'b1', 'w2', 'b2')}
    del _L0_ffn_all

    def _L1_gnn_setup():
        import jax, jax.numpy as jnp
        import numpy as np
        NEG_SLOPE = 0.2

        def gat_conv(x, edge_index, W, att_src, att_dst, bias, heads, out_c, concat):
            N = x.shape[0]
            loop = jnp.arange(N, dtype=edge_index.dtype)
            src = jnp.concatenate([edge_index[0], loop])
            dst = jnp.concatenate([edge_index[1], loop])
            h = (x @ W).reshape(N, heads, out_c)
            a_src = jnp.einsum('nhc,hc->nh', h, att_src)
            a_dst = jnp.einsum('nhc,hc->nh', h, att_dst)
            e = jax.nn.leaky_relu(a_src[src] + a_dst[dst], NEG_SLOPE)
            emax = jax.ops.segment_max(e, dst, num_segments=N)
            e = jnp.exp(e - emax[dst])
            denom = jax.ops.segment_sum(e, dst, num_segments=N)
            alpha = e / denom[dst]
            msg = h[src] * alpha[:, :, None]
            out = jax.ops.segment_sum(msg, dst, num_segments=N)
            out = out.reshape(N, heads * out_c) if concat else out.mean(axis=1)
            return out + bias
        key = jax.random.key(seed)
        ks = jax.random.split(key, 10)
        N, E, Fin, Hc, H, Out = (625, 10000, 256, 128, 4, 256)
        s = lambda k, shp: jax.random.normal(k, shp, dtype=jnp.float32) * 0.05
        return {'x': jax.random.normal(ks[0], (N, Fin), dtype=jnp.float32), 'edge_index': jax.random.randint(ks[1], (2, E), 0, N, dtype=jnp.int64), 'W1': s(ks[2], (Fin, H * Hc)), 'att_src1': s(ks[3], (H, Hc)), 'att_dst1': s(ks[4], (H, Hc)), 'b1': s(ks[5], (H * Hc,)), 'W2': s(ks[6], (H * Hc, Out)), 'att_src2': s(ks[7], (1, Out)), 'att_dst2': s(ks[8], (1, Out)), 'b2': s(ks[9], (Out,))}
    _L1_gnn_all = _L1_gnn_setup()
    _L1_gnn_in = {k: v for k, v in _L1_gnn_all.items() if k in ('W1', 'att_src1', 'att_dst1', 'b1', 'W2', 'att_src2', 'att_dst2', 'b2')}
    del _L1_gnn_all

    def _L1_mix_setup():
        import jax, jax.numpy as jnp
        import numpy as np
        HEADS = 4
        DIM_HEAD = 32
        key = jax.random.key(seed)
        k1, k2, k3 = jax.random.split(key, 3)
        B, L, D = (16, 256, 256)
        hidden = HEADS * DIM_HEAD
        x = jax.random.normal(k1, (B, L, D), dtype=jnp.float32)
        W_qkv = jax.random.normal(k2, (D, 3 * hidden), dtype=jnp.float32) * D ** (-0.5)
        W_out = jax.random.normal(k3, (hidden, D), dtype=jnp.float32) * hidden ** (-0.5)
        b_out = jnp.zeros((D,), dtype=jnp.float32)
        return {'x': x, 'W_qkv': W_qkv, 'W_out': W_out, 'b_out': b_out}
    _L1_mix_all = _L1_mix_setup()
    _L1_mix_in = {k: v for k, v in _L1_mix_all.items() if k in ('W_qkv', 'W_out', 'b_out')}
    del _L1_mix_all

    def _L1_ffn_setup():
        import jax, jax.numpy as jnp
        import numpy as np
        B, K, D = (512, 16, 256)
        E = 32
        H = int(D * 0.25)
        key = jax.random.key(seed)
        ks = jax.random.split(key, 7)
        d_rs = D ** (-0.5)
        h_rs = H ** (-0.5)
        x = jax.random.normal(ks[0], (B, K, D), dtype=jnp.float32)
        router_w = jax.random.uniform(ks[1], (E, D), jnp.float32, -d_rs, d_rs)
        router_b = jax.random.uniform(ks[2], (E,), jnp.float32, -d_rs, d_rs)
        W1 = jax.random.uniform(ks[3], (E, D, H), jnp.float32, -h_rs, h_rs)
        b1 = jax.random.uniform(ks[4], (E, H), jnp.float32, -h_rs, h_rs)
        W2 = jax.random.uniform(ks[5], (E, H, D), jnp.float32, -d_rs, d_rs)
        b2 = jax.random.uniform(ks[6], (E, D), jnp.float32, -d_rs, d_rs)
        return {'x': x, 'router_w': router_w, 'router_b': router_b, 'W1': W1, 'b1': b1, 'W2': W2, 'b2': b2}
    _L1_ffn_all = _L1_ffn_setup()
    _L1_ffn_in = {k: v for k, v in _L1_ffn_all.items() if k in ('router_w', 'router_b', 'W1', 'b1', 'W2', 'b2')}
    del _L1_ffn_all
    return {'x': x, 'src': src, 'dst': dst, 'edge_attr_3': edge_attr_3, 'L0_gnn_W': _L0_gnn_in['W'], 'L0_gnn_a_src': _L0_gnn_in['a_src'], 'L0_gnn_a_dst': _L0_gnn_in['a_dst'], 'L0_gnn_edge_W': _L0_gnn_in['edge_W'], 'L0_gnn_edge_b': _L0_gnn_in['edge_b'], 'L0_gnn_bias': _L0_gnn_in['bias'], 'L0_mix_wq': _L0_mix_in['wq'], 'L0_mix_wk': _L0_mix_in['wk'], 'L0_mix_wv': _L0_mix_in['wv'], 'L0_mix_wo': _L0_mix_in['wo'], 'L0_mix_bo': _L0_mix_in['bo'], 'L0_mix_ln_k_g': _L0_mix_in['ln_k_g'], 'L0_mix_ln_k_b': _L0_mix_in['ln_k_b'], 'L0_mix_ln_v_g': _L0_mix_in['ln_v_g'], 'L0_mix_ln_v_b': _L0_mix_in['ln_v_b'], 'L0_ffn_gate_w': _L0_ffn_in['gate_w'], 'L0_ffn_gate_b': _L0_ffn_in['gate_b'], 'L0_ffn_w1': _L0_ffn_in['w1'], 'L0_ffn_b1': _L0_ffn_in['b1'], 'L0_ffn_w2': _L0_ffn_in['w2'], 'L0_ffn_b2': _L0_ffn_in['b2'], 'L1_gnn_W1': _L1_gnn_in['W1'], 'L1_gnn_att_src1': _L1_gnn_in['att_src1'], 'L1_gnn_att_dst1': _L1_gnn_in['att_dst1'], 'L1_gnn_b1': _L1_gnn_in['b1'], 'L1_gnn_W2': _L1_gnn_in['W2'], 'L1_gnn_att_src2': _L1_gnn_in['att_src2'], 'L1_gnn_att_dst2': _L1_gnn_in['att_dst2'], 'L1_gnn_b2': _L1_gnn_in['b2'], 'L1_mix_W_qkv': _L1_mix_in['W_qkv'], 'L1_mix_W_out': _L1_mix_in['W_out'], 'L1_mix_b_out': _L1_mix_in['b_out'], 'L1_ffn_router_w': _L1_ffn_in['router_w'], 'L1_ffn_router_b': _L1_ffn_in['router_b'], 'L1_ffn_W1': _L1_ffn_in['W1'], 'L1_ffn_b1': _L1_ffn_in['b1'], 'L1_ffn_W2': _L1_ffn_in['W2'], 'L1_ffn_b2': _L1_ffn_in['b2']}

def reference(x, src, dst, edge_attr_3, L0_gnn_W, L0_gnn_a_src, L0_gnn_a_dst, L0_gnn_edge_W, L0_gnn_edge_b, L0_gnn_bias, L0_mix_wq, L0_mix_wk, L0_mix_wv, L0_mix_wo, L0_mix_bo, L0_mix_ln_k_g, L0_mix_ln_k_b, L0_mix_ln_v_g, L0_mix_ln_v_b, L0_ffn_gate_w, L0_ffn_gate_b, L0_ffn_w1, L0_ffn_b1, L0_ffn_w2, L0_ffn_b2, L1_gnn_W1, L1_gnn_att_src1, L1_gnn_att_dst1, L1_gnn_b1, L1_gnn_W2, L1_gnn_att_src2, L1_gnn_att_dst2, L1_gnn_b2, L1_mix_W_qkv, L1_mix_W_out, L1_mix_b_out, L1_ffn_router_w, L1_ffn_router_b, L1_ffn_W1, L1_ffn_b1, L1_ffn_W2, L1_ffn_b2):
    import jax
    import jax.numpy as jnp

    def _L0_gnn_ref(x, W, a_src, a_dst, edge_W, edge_b, bias, edge_attr, edge_index):
        import jax, jax.numpy as jnp
        import numpy as np
        N = 50000
        E = 12500
        IN = 256
        H = 8
        D = 32
        EF = 3
        n = x.shape[0]
        h = (x @ W.T).reshape(n, H, D)
        src, dst = (edge_index[0], edge_index[1])
        h_src = h[src]
        h_dst = h[dst]
        alpha = jnp.einsum('ehd,hd->eh', h_src, a_src) + jnp.einsum('ehd,hd->eh', h_dst, a_dst)
        enc = jax.nn.relu(edge_attr @ edge_W.T + edge_b).reshape(-1, H, D)
        alpha = alpha + jnp.sum(enc * h_dst, axis=-1)
        alpha = jnp.where(alpha >= 0, alpha, 0.2 * alpha)
        amax = jax.ops.segment_max(alpha, dst, num_segments=n)
        ex = jnp.exp(alpha - amax[dst])
        denom = jax.ops.segment_sum(ex, dst, num_segments=n)
        attn = ex / jnp.maximum(denom[dst], 1e-10)
        out = jax.ops.segment_sum(h_src * attn[..., None], dst, num_segments=n)
        return out.reshape(n, H * D) + bias

    def _L0_mix_ref(seq, wq, wk, wv, wo, bo, ln_k_g, ln_k_b, ln_v_g, ln_v_b):
        import jax, jax.numpy as jnp
        import numpy as np
        import math
        EMBED = 256
        HEADS = 4
        HEAD_DIM = EMBED // HEADS
        OUT_DIM = 256
        LN_EPS = 1e-05

        def _qkv_init(key):
            spread = math.sqrt(3.0 / EMBED)
            gain, delta = (0.01, 0.01)
            w = jax.random.uniform(key, (EMBED, EMBED), minval=-spread, maxval=spread) * gain
            return w + delta * jnp.eye(EMBED, dtype=w.dtype)

        def _layer_norm(x, g, b):
            mu = jnp.mean(x, axis=-1, keepdims=True)
            var = jnp.mean(jnp.square(x - mu), axis=-1, keepdims=True)
            return (x - mu) * jax.lax.rsqrt(var + LN_EPS) * g + b

        def _split_heads(x, B, S):
            return x.reshape(B, S, HEADS, HEAD_DIM).transpose(0, 2, 1, 3)
        B, S, _ = seq.shape
        q = _split_heads(seq @ wq.T, B, S)
        k = _split_heads(seq @ wk.T, B, S)
        v = _split_heads(seq @ wv.T, B, S)
        k = _layer_norm(k, ln_k_g, ln_k_b)
        v = _layer_norm(v, ln_v_g, ln_v_b)
        kv = jnp.einsum('bhsd,bhse->bhde', k, v) / S
        ga = jnp.einsum('bhsd,bhde->bhse', q, kv)
        ga = ga.transpose(0, 2, 1, 3).reshape(B, S, EMBED)
        return ga @ wo.T + bo

    def _L0_ffn_ref(h, gate_w, gate_b, w1, b1, w2, b2):
        import math
        import jax, jax.numpy as jnp
        import numpy as np
        CAPACITY_FACTOR = 1.25
        B, L, D = h.shape
        E = gate_w.shape[1]
        T = B * L
        C = max(1, math.ceil(CAPACITY_FACTOR * T / E))
        x = h.reshape(T, D)
        logits = x @ gate_w + gate_b
        probs = jax.nn.softmax(logits, axis=-1)
        idx = jnp.argmax(probs, axis=-1)
        prb = jnp.take_along_axis(probs, idx[:, None], axis=1)[:, 0]
        one_hot = jax.nn.one_hot(idx, E, dtype=jnp.float32)
        pos = (jnp.cumsum(one_hot, axis=0) * one_hot).sum(-1).astype(jnp.int32) - 1
        kept = pos < C
        pos_safe = jnp.where(kept, pos, C)
        buf = jnp.zeros((E, C, D), dtype=h.dtype).at[idx, pos_safe].set(x, mode='drop')
        hmid = jax.nn.relu(jnp.einsum('ecd,edf->ecf', buf, w1) + b1[:, None, :])
        ybuf = jnp.einsum('ecf,efd->ecd', hmid, w2) + b2[:, None, :]
        pos_g = jnp.minimum(pos, C - 1)
        y_tok = ybuf[idx, pos_g] * (prb * kept)[:, None]
        y = y_tok.reshape(B, L, D)
        y = jnp.nan_to_num(y, nan=0.0, posinf=10000.0, neginf=-10000.0)
        return y

    def _L1_gnn_ref(x, edge_index, W1, att_src1, att_dst1, b1, W2, att_src2, att_dst2, b2):
        import jax, jax.numpy as jnp
        import numpy as np
        NEG_SLOPE = 0.2

        def gat_conv(x, edge_index, W, att_src, att_dst, bias, heads, out_c, concat):
            N = x.shape[0]
            loop = jnp.arange(N, dtype=edge_index.dtype)
            src = jnp.concatenate([edge_index[0], loop])
            dst = jnp.concatenate([edge_index[1], loop])
            h = (x @ W).reshape(N, heads, out_c)
            a_src = jnp.einsum('nhc,hc->nh', h, att_src)
            a_dst = jnp.einsum('nhc,hc->nh', h, att_dst)
            e = jax.nn.leaky_relu(a_src[src] + a_dst[dst], NEG_SLOPE)
            emax = jax.ops.segment_max(e, dst, num_segments=N)
            e = jnp.exp(e - emax[dst])
            denom = jax.ops.segment_sum(e, dst, num_segments=N)
            alpha = e / denom[dst]
            msg = h[src] * alpha[:, :, None]
            out = jax.ops.segment_sum(msg, dst, num_segments=N)
            out = out.reshape(N, heads * out_c) if concat else out.mean(axis=1)
            return out + bias
        h = gat_conv(x, edge_index, W1, att_src1, att_dst1, b1, heads=4, out_c=128, concat=True)
        h = jax.nn.gelu(h, approximate=False)
        out = gat_conv(h, edge_index, W2, att_src2, att_dst2, b2, heads=1, out_c=256, concat=False)
        return out

    def _L1_mix_ref(x, W_qkv, W_out, b_out):
        import jax, jax.numpy as jnp
        import numpy as np
        HEADS = 4
        DIM_HEAD = 32
        B, L, D = x.shape
        scale = DIM_HEAD ** (-0.5)
        qkv = jnp.einsum('bld,df->blf', x, W_qkv)
        qkv = qkv.reshape(B, L, 3, HEADS, DIM_HEAD)
        q = jnp.transpose(qkv[:, :, 0], (0, 2, 1, 3)) * scale
        k = jax.nn.softmax(jnp.transpose(qkv[:, :, 1], (0, 2, 1, 3)), axis=2)
        v = jnp.transpose(qkv[:, :, 2], (0, 2, 1, 3))
        context = jnp.einsum('bhld,bhle->bhde', k, v)
        out = jnp.einsum('bhde,bhld->bhle', context, q)
        out = jnp.transpose(out, (0, 2, 1, 3)).reshape(B, L, HEADS * DIM_HEAD)
        return jnp.einsum('blf,fd->bld', out, W_out) + b_out

    def _L1_ffn_ref(x, router_w, router_b, W1, b1, W2, b2):
        import jax, jax.numpy as jnp
        import numpy as np
        B, K, D = (512, 16, 256)
        E = 32
        H = int(D * 0.25)
        xf = x.reshape(-1, D)
        logits = xf @ router_w.T + router_b
        idx = jnp.argmax(logits, axis=-1)
        w1t = jnp.take(W1, idx, axis=0)
        h = jnp.einsum('nd,ndh->nh', xf, w1t) + jnp.take(b1, idx, axis=0)
        h = jax.nn.relu(h)
        w2t = jnp.take(W2, idx, axis=0)
        out = jnp.einsum('nh,nhd->nd', h, w2t) + jnp.take(b2, idx, axis=0)
        out = jax.nn.relu(out)
        return out.reshape(x.shape)
    edge_index = jnp.stack([src, dst])
    xn = _layernorm(x, axis=-1)
    x = x + _L0_gnn_ref(xn, L0_gnn_W, L0_gnn_a_src, L0_gnn_a_dst, L0_gnn_edge_W, L0_gnn_edge_b, L0_gnn_bias, edge_attr_3, edge_index) + _L0_mix_ref(xn[None], L0_mix_wq, L0_mix_wk, L0_mix_wv, L0_mix_wo, L0_mix_bo, L0_mix_ln_k_g, L0_mix_ln_k_b, L0_mix_ln_v_g, L0_mix_ln_v_b)[0]
    x = x + _L0_ffn_ref(_layernorm(x, axis=-1)[None], L0_ffn_gate_w, L0_ffn_gate_b, L0_ffn_w1, L0_ffn_b1, L0_ffn_w2, L0_ffn_b2)[0]
    xn = _layernorm(x, axis=-1)
    x = x + _L1_gnn_ref(xn, edge_index, L1_gnn_W1, L1_gnn_att_src1, L1_gnn_att_dst1, L1_gnn_b1, L1_gnn_W2, L1_gnn_att_src2, L1_gnn_att_dst2, L1_gnn_b2) + _L1_mix_ref(xn[None], L1_mix_W_qkv, L1_mix_W_out, L1_mix_b_out)[0]
    x = x + _L1_ffn_ref(_layernorm(x, axis=-1)[None], L1_ffn_router_w, L1_ffn_router_b, L1_ffn_W1, L1_ffn_b1, L1_ffn_W2, L1_ffn_b2)[0]
    return x

_drawn_inputs = setup_inputs


def setup_inputs(seed=0):
    import zlib

    import numpy as np

    out = dict(_drawn_inputs(seed))
    spreads = {'L0_gnn_edge_b': (0.0, 0.1),
     'L0_gnn_bias': (0.0, 0.1),
     'L0_mix_ln_k_g': (1.0, 0.6),
     'L0_mix_ln_k_b': (0.0, 0.8),
     'L0_mix_ln_v_g': (1.0, 0.6),
     'L0_mix_ln_v_b': (0.0, 0.8),
     'L0_ffn_gate_b': (0.0, 0.1),
     'L0_ffn_b1': (0.0, 0.414),
     'L0_ffn_b2': (0.0, 0.285),
     'L1_mix_b_out': (0.0, 0.1)}
    factors = {'L0_mix_wq': 4.309,
     'L0_mix_wk': 3.808,
     'L0_mix_wv': 3.992,
     'L0_mix_wo': 3.929,
     'L1_gnn_att_dst1': 22.4,
     'L1_gnn_att_src2': 8.0,
     'L1_gnn_att_dst2': 42.525,
     'L1_ffn_b1': 6.521,
     'L1_ffn_b2': 3.163}
    for name, (base, spread) in spreads.items():
        noise = np.random.default_rng([zlib.crc32(name.encode()), seed]).standard_normal(out[name].shape)
        drawn = base * np.exp(spread * noise) if base else spread * noise
        out[name] = jnp.asarray(drawn.astype(out[name].dtype))
    for name, factor in factors.items():
        out[name] = (out[name] * factor).astype(out[name].dtype)
    return out
```

```python
from contextlib import ExitStack

import concourse.bass as bass
from concourse import mybir

F32 = mybir.dt.float32
BF16 = mybir.dt.bfloat16
I32 = mybir.dt.int32
ALU = mybir.AluOpType
ACT = mybir.ActivationFunctionType
AX = mybir.AxisListType.X

P = 128
N = 3125
D = 256
E = 50000
NT = -(-N // P)
NLAST = N - (NT - 1) * P
NPAD = NT * P
U = 5
EB = 256
NB = -(-E // EB)
W = NB + NT - 1
SUB = EB // P
WS = W * SUB
WC = 2
WP = W // WC
BIG = 1.0e30
NEG_SLOPE = 0.2
LN_EPS = 1e-5

H0, DH0 = 8, 32
MH, MD = 4, 64
E0, F0 = 8, 1024
CAP = -(-5 * N // (4 * E0))
H1, DH1 = 4, 128
E1, F1 = 32, 64
LH, LD = 4, 32


class Program:

    def __init__(self, nc, stack):
        self.nc, self.stack, self.used = nc, stack, []

    def sbuf(self, name, shape, dt=F32):
        return self.stack.enter_context(self.nc.sbuf_tensor(name, shape, dt))

    def dram(self, name, shape, dt=F32):
        return self.nc.dram_tensor(name, shape, dt, kind="Internal").ap()


class Stage:
    def __init__(self, prog, name):
        self.prog, self.nc, self.name = prog, prog.nc, name
        self.stack = ExitStack()
        self.sems = []
        self.stale = prog.used

    def sem(self, name):
        s = self.nc.alloc_semaphore(f"{self.name}_{name}")
        self.sems.append(s)
        return s

    def sem_sw(self, name):
        return self.nc.alloc_semaphore(f"{self.name}_{name}")

    def sbuf(self, name, shape, dt=F32):
        return self.stack.enter_context(self.nc.sbuf_tensor(f"{self.name}_{name}", shape, dt))

    def psum(self, name, shape, dt=F32):
        return self.stack.enter_context(self.nc.psum_tensor(f"{self.name}_{name}", shape, dt))

    def block(self):
        return self.stack.enter_context(self.nc.Block())

    def clear_stale(self, pool):
        for s in self.stale:
            pool.sem_clear(s)

    def __enter__(self):
        return self

    def __exit__(self, *exc):
        self.stack.__exit__(*exc)
        for s in self.stale:
            self.nc.release_semaphore(s)
        self.prog.used = self.sems
        return False


def edge_items(prog, K, x, src, dst, attr):
    nc = prog.nc
    with Stage(prog, "items") as st:
        def carve(i):
            rows = K.xn[0:WP, :, :].rearrange("p t d -> p (t d)")[:, i * WC * EB:(i + 1) * WC * EB]
            return rows.rearrange("p (c e) -> p c e", c=WC)

        edges = st.sbuf("edges", [P, NB * EB // P], I32)
        edges_f = st.sbuf("edges_f", [P, NB * EB // P])
        below = st.sbuf("below", [P, NB * EB // P])
        count = st.sbuf("count", [P, NT - 1])
        ones = st.sbuf("ones", [P, P])
        t_step = st.sbuf("t_step", [P, NT - 1])
        key_t = st.sbuf("key_t", [P, NT - 1])
        w_row = st.sbuf("w_row", [P, W])
        w_col = st.sbuf("w_col", [WP, WC])
        w_id = st.sbuf("w_id", [WP, WC])
        passed = K.arena_a[:, 0:W * (NT - 1)].rearrange("p (w t) -> p w t", w=W)
        passed_c = st.sbuf("passed_c", [WP, WC, NT - 1])
        t_f = st.sbuf("t_f", [P, W])
        t_c = st.sbuf("t_c", [WP, WC])
        t_first = st.sbuf("t_first", [WP, WC])
        b_col = st.sbuf("b_col", [WP, WC], I32)
        gsrc = st.sbuf("gsrc", [WP, WC, EB], I32)
        gdst = st.sbuf("gdst", [WP, WC, EB], I32)
        gattr = K.arena_b[0:WP, 0:WC * 3 * EB].rearrange("p (c a e) -> p c a e", c=WC, a=3)
        src_f = carve(0)
        dst_f = carve(1)
        rel = carve(2)
        inside = carve(3)
        inside2 = carve(4)
        key = carve(5)
        clip = st.sbuf("clip", [WP, WC, EB], BF16)
        key_prev = carve(6)
        key_next = carve(7)
        first = carve(8)
        last = carve(9)
        pen_p = carve(10)
        pen_n = carve(11)
        guard = st.sbuf("guard", [1, 1])
        zeros = K.arena_a[:, W * (NT - 1):W * (NT - 1) + E0 * CAP * D // P // 4]
        ps_total = st.psum("ps_total", [P, NT - 1])
        ps_turn = st.psum("ps_turn", [P, 4, WP])

        s_const = st.sem("const")
        s_ident = st.sem("ident")
        s_edges = st.sem("edges")
        s_dve = st.sem("dve")
        s_xpad = st.sem("xpad")
        s_x = st.sem("x")
        s_count = st.sem("count")
        s_total = st.sem("total")
        s_gather = st.sem_sw("gather")
        s_rows = st.sem("rows")
        s_key = st.sem("key")
        s_store = st.sem("store")
        s_shift = st.sem("shift")
        s_pen = st.sem("pen")
        s_turn = st.sem("turn")
        s_turned = st.sem("turned")
        s_srcf = st.sem("srcf")
        s_zero = st.sem("zero")
        key_flat = K.key_flat
        block = st.block()

        @block.sync
        def _(sp):
            sp.dma_start(edges[:, :], dst.rearrange("b e -> (b e)").rearrange("(p j) -> p j", p=P)).then_inc(s_edges, 16)
            sp.dma_start(K.x[:, 0:NT - 1, :], x[0:(NT - 1) * P, :].rearrange("(t p) d -> p t d", p=P)).then_inc(s_x, 16)
            sp.wait_ge(s_xpad, 2)
            sp.dma_start(K.x[0:NLAST, NT - 1, :], x[(NT - 1) * P:N, :]).then_inc(s_x, 16)
            sp.wait_ge(s_zero, 1)
            zrows = K.slots.rearrange("s d -> (s d)").rearrange("(q p j) -> q p j", q=4, p=P)
            for q in range(4):
                sp.dma_start(zrows[q], zeros[:, :]).then_inc(s_store, 16)
            sp.dma_start(key_flat[0:1].unsqueeze(0), guard[:, :]).then_inc(s_shift, 16)
            sp.dma_start(key_flat[1 + WS * P:2 + WS * P].unsqueeze(0), guard[:, :]).then_inc(s_shift, 16)
            sp.wait_ge(s_gather, 16 * 3 * WC)
            for c in range(3):
                sp.dma_start(K.attr_rows[c].rearrange("(c p) e -> p c e", c=WC), gattr[:, :, c, :]).then_inc(s_store, 16)
            sp.wait_ge(s_key, 1)
            sp.dma_start(key_flat[1:1 + WS * P].rearrange("(c p e) -> p c e", c=WC, p=WP), key[:, :, :]).then_inc(s_shift, 16)
            sp.wait_ge(s_shift, 48)
            sp.dma_start(key_prev[:, :, :], key_flat[0:WS * P].rearrange("(c p e) -> p c e", c=WC, p=WP)).then_inc(s_rows, 16)
            sp.dma_start(key_next[:, :, :], key_flat[2:2 + WS * P].rearrange("(c p e) -> p c e", c=WC, p=WP)).then_inc(s_rows, 16)
            sp.wait_ge(s_key, 2)
            sp.dma_start(K.rel_rows.rearrange("(c p) e -> p c e", c=WC), clip[:, :, :]).then_inc(s_store, 16)
            sp.wait_ge(s_pen, 2)
            sp.dma_start(K.pen_prev.rearrange("(c p e) -> p c e", c=WC, p=WP), pen_p[:, :, :]).then_inc(s_store, 16)
            sp.dma_start(K.pen_next.rearrange("(c p e) -> p c e", c=WC, p=WP), pen_n[:, :, :]).then_inc(s_store, 16)
            sp.wait_ge(s_store, 16 * 10)
            sp.wait_ge(s_x, 32)

        @block.gpsimd
        def _(pool):
            pool.memset(zeros[:, :], 0.0).then_inc(s_zero, 1)
            pool.iota(w_row[:, :], [[EB, W]], base=EB, channel_multiplier=0, allow_small_or_imprecise_dtypes=True).then_inc(s_const, 1)
            pool.iota(w_col[:, :], [[EB * WP, WC]], base=EB, channel_multiplier=EB, allow_small_or_imprecise_dtypes=True).then_inc(s_const, 1)
            pool.iota(w_id[:, :], [[WP, WC]], base=0, channel_multiplier=1, allow_small_or_imprecise_dtypes=True).then_inc(s_const, 1)
            pool.iota(t_step[:, :], [[EB, NT - 1]], base=EB, channel_multiplier=0, allow_small_or_imprecise_dtypes=True).then_inc(s_const, 1)
            pool.iota(K.iota_row[:, :], [[1, P]], base=0, channel_multiplier=0, allow_small_or_imprecise_dtypes=True).then_inc(s_const, 1)
            pool.iota(K.iota_part[:, :], [[0, 1]], base=0, channel_multiplier=1, allow_small_or_imprecise_dtypes=True).then_inc(s_const, 1)
            pool.memset(K.ident[:, :], 0.0).then_inc(s_ident, 1)
            pool.wait_ge(s_ident, 1)
            pool.affine_select(out=K.ident[:, :], in_=K.ident[:, :], compare_op=ALU.not_equal, fill=1.0, base=0,
                               pattern=[[-1, P]], channel_multiplier=1).then_inc(s_ident, 1)
            pool.wait_ge(s_count, 2)
            for c in range(WC):
                at = bass.IndirectOffsetOnAxis(ap=b_col[:, c:c + 1], axis=0)
                pool.indirect_dma_start(gdst[:, c, :], None, dst, at).then_inc(s_gather, 16)
                pool.indirect_dma_start(gsrc[:, c, :], None, src, at).then_inc(s_gather, 16)
                pool.indirect_dma_start(gattr[:, c, :, :].rearrange("p a e -> p (a e)"), None, attr, at).then_inc(s_gather, 16)
            pool.wait_ge(s_gather, 16 * 3 * WC)

        @block.vector
        def _(dve):
            n = [0]

            def step(ins):
                n[0] += 1
                ins.then_inc(s_dve, 1)
                dve.wait_ge(s_dve, n[0])

            dve.memset(K.x[:, NT - 1, :], 0.0).then_inc(s_xpad, 1)
            dve.memset(guard[:, :], -7.0).then_inc(s_xpad, 1)
            dve.memset(K.eps[:, :], LN_EPS)
            dve.memset(K.one[:, :], 1.0)
            step(dve.memset(ones[:, :], 1.0))
            dve.wait_ge(s_edges, 16)
            step(dve.tensor_copy(edges_f[:, :], edges[:, :]))
            for t in range(NT - 1):
                step(dve.tensor_scalar(below[:, :], edges_f[:, :], float(P * (t + 1)), 0.0, ALU.is_lt, ALU.add,
                                       accum_out=count[:, t:t + 1]))
            dve.sem_inc(s_count, 1)
            dve.wait_ge(s_const, 6)
            dve.wait_ge(s_total, 1)
            step(dve.tensor_tensor(key_t[:, :], ps_total[:, :], t_step[:, :], ALU.add))
            dve.tensor_tensor(passed_c[:, :, :], w_col[:, :].unsqueeze(2).broadcast_to([WP, WC, NT - 1]),
                              key_t[0:WP, :].unsqueeze(1).broadcast_to([WP, WC, NT - 1]), ALU.is_gt)
            step(dve.tensor_tensor(passed[:, :, :], w_row[:, :].unsqueeze(2).broadcast_to([P, W, NT - 1]),
                                   key_t[:, :].unsqueeze(1).broadcast_to([P, W, NT - 1]), ALU.is_gt))
            step(dve.tensor_reduce(t_c[:, :], passed_c[:, :, :], AX, ALU.add))
            dve.tensor_tensor(b_col[:, :], w_id[:, :], t_c[:, :], ALU.subtract).then_inc(s_count, 1)
            step(dve.tensor_scalar(t_first[:, :], t_c[:, :], float(P), None, ALU.mult))
            step(dve.tensor_reduce(t_f[:, :], passed[:, :, :], AX, ALU.add))
            step(dve.tensor_copy(K.window[:, :], t_f[:, :]))
            dve.wait_ge(s_gather, 16 * 3 * WC)
            dve.tensor_copy(src_f[:, :, :], gsrc[:, :, :]).then_inc(s_srcf, 1)
            step(dve.tensor_copy(dst_f[:, :, :], gdst[:, :, :]))
            for c in range(WC):
                ins = dve.tensor_scalar(rel[:, c, :], dst_f[:, c, :], t_first[:, c:c + 1], None, ALU.subtract)
            ins.then_inc(s_srcf, 1)
            dve.wait_ge(s_srcf, 2)
            step(dve.tensor_scalar(inside[:, :, :], rel[:, :, :], 0.0, None, ALU.is_ge))
            step(dve.scalar_tensor_tensor(inside2[:, :, :], rel[:, :, :], float(P - 1), inside[:, :, :], ALU.is_le, ALU.mult))
            dve.scalar_tensor_tensor(key[:, :, :], dst_f[:, :, :], 1.0, inside2[:, :, :], ALU.add, ALU.mult).then_inc(s_key, 1)
            dve.tensor_scalar(clip[:, :, :], rel[:, :, :], -1.0, float(P), ALU.max, ALU.min).then_inc(s_key, 1)
            dve.wait_ge(s_key, 1)
            dve.wait_ge(s_rows, 32)
            dve.tensor_tensor(last[:, :, :], key[:, :, :], key_next[:, :, :], ALU.not_equal).then_inc(s_srcf, 1)
            step(dve.tensor_tensor(first[:, :, :], key[:, :, :], key_prev[:, :, :], ALU.not_equal))
            dve.wait_ge(s_srcf, 3)
            dve.tensor_scalar(pen_p[:, :, :], first[:, :, :], -BIG, None, ALU.mult).then_inc(s_pen, 1)
            dve.tensor_scalar(pen_n[:, :, :], last[:, :, :], -BIG, None, ALU.mult).then_inc(s_pen, 1)
            for r, out in enumerate((K.src_col, K.rel_col, K.last_col)):
                dve.wait_ge(s_turn, r + 1)
                ins = dve.tensor_copy(out[:, :].rearrange("e (c p s) -> e c p s", c=WC, s=SUB),
                                      ps_turn[:, :, :].rearrange("e (c s) p -> e c p s", c=WC)).then_inc(s_turned, 1)
            dve.wait_ge(s_pen, 2)

        @block.tensor
        def _(pe):
            pe.wait_ge(s_count, 1)
            pe.wait_ge(s_dve, 1)
            pe.matmul(ps_total[:, :], lhsT=ones[:, :], rhs=count[:, :], start=True, stop=True).then_inc(s_total, 1)
            pe.wait_ge(s_ident, 2)
            for r, rows in enumerate((src_f, rel, last)):
                pe.wait_ge(s_srcf, r + 1)
                if r:
                    pe.wait_ge(s_turned, r)
                for c in range(WC):
                    for s in range(SUB):
                        ins = pe.transpose(ps_turn[:, c * SUB + s, :], rows[:, c, s * P:(s + 1) * P], K.ident[0:WP, 0:WP])
                ins.then_inc(s_turn, 1)


def layer_norm(prog, K, name):
    with Stage(prog, name) as st:
        stats = st.sbuf("stats", [P, NT, 6])
        total, gap, within = (st.sbuf(n, [P, NT]) for n in ("total", "gap", "within"))
        mean, gap2, within2, var = (st.sbuf(n, [P, NT]) for n in ("mean", "gap2", "within2", "var"))
        std = st.sbuf("std", [P, NT])
        rstd = st.sbuf("rstd", [P, NT])
        ps = st.psum("ps", [P, U, 4, P])
        s_stats, s_mom, s_std, s_rstd = st.sem("stats"), st.sem("mom"), st.sem("std"), st.sem("rstd")
        s_xn, s_turn, s_free = st.sem("xn"), st.sem("turn"), st.sem("free")
        block = st.block()

        @block.gpsimd
        def _(pool):
            st.clear_stale(pool)

        @block.vector
        def _(dve):
            with dve.Fori(0, NT) as t:
                dve.bn_stats(stats[:, t, :], K.x[:, t, :]).then_inc(s_stats, 1)
            dve.wait_ge(s_stats, NT)
            dve.tensor_tensor(total[:, :], stats[:, :, 1], stats[:, :, 4], ALU.add).then_inc(s_mom, 1)
            dve.tensor_tensor(gap[:, :], stats[:, :, 1], stats[:, :, 4], ALU.subtract).then_inc(s_mom, 1)
            dve.tensor_tensor(within[:, :], stats[:, :, 2], stats[:, :, 5], ALU.add).then_inc(s_mom, 1)
            dve.wait_ge(s_mom, 3)
            dve.tensor_scalar(mean[:, :], total[:, :], 0.5, None, ALU.mult).then_inc(s_mom, 1)
            dve.tensor_tensor(gap2[:, :], gap[:, :], gap[:, :], ALU.mult).then_inc(s_mom, 1)
            dve.tensor_scalar(within2[:, :], within[:, :], 1.0 / D, None, ALU.mult).then_inc(s_mom, 1)
            dve.wait_ge(s_mom, 6)
            dve.scalar_tensor_tensor(var[:, :], gap2[:, :], 0.25, within2[:, :], ALU.mult, ALU.add).then_inc(s_mom, 1)
            dve.wait_ge(s_std, 1)
            dve.reciprocal(rstd[:, :], std[:, :]).then_inc(s_rstd, 1)
            dve.wait_ge(s_rstd, 1)
            with dve.Fori(0, NT) as t:
                dve.tensor_scalar(K.xn[:, t, :], K.x[:, t, :], mean[:, bass.ds(t, 1)], rstd[:, bass.ds(t, 1)],
                                  ALU.subtract, ALU.mult).then_inc(s_xn, 1)

        @block.scalar
        def _(act):
            act.wait_ge(s_mom, 7)
            act.activation(std[:, :], var[:, :], ACT.Sqrt, bias=K.eps[:, 0:1]).then_inc(s_std, 1)
            with act.Fori(0, NT // U) as i:
                for j in range(U):
                    t = i * U + j
                    act.wait_ge(s_turn, t + 1)
                    act.activation(K.xn_t[:, :, bass.ds(t * P, P)], ps[:, j, 0:2, :], ACT.Copy).then_inc(s_free, 1)

        @block.tensor
        def _(pe):
            for t in range(NT):
                pe.wait_ge(s_xn, t + 1)
                if t >= U:
                    pe.wait_ge(s_free, t - U + 1)
                pe.transpose(ps[:, t % U, 0, :], K.xn[:, t, 0:P], K.ident[:, :])
                pe.transpose(ps[:, t % U, 1, :], K.xn[:, t, P:D], K.ident[:, :]).then_inc(s_turn, 1)


def load_rows(sp, sem, dst, rows):
    return sp.dma_start(dst, rows.partition_broadcast(P).rearrange("p a d -> p (a d)")).then_inc(sem, 16)


def project_l0(prog, K, A):
    R = DH0 + 1
    with Stage(prog, "proj0") as st:
        kv = K.arena_a[:, 0:NT * 2 * D].rearrange("p (t d) -> p t d", t=NT)
        w = st.sbuf("w", [P, 2, D + 2 * H0])
        wkv = st.sbuf("wkv", [P, 2, 2 * D])
        wot = st.sbuf("wot", [P, 2, D])
        wq = st.sbuf("wq", [P, 2, D])
        att = st.sbuf("att", [P, 2, D])
        att_w = K.xn[:, 10:12, :]
        att_w2 = K.xn[:, 12:14, :]
        gain = st.sbuf("gain", [P, 2, 64])
        shift = st.sbuf("shift", [P, 2, 64])
        groups = U * 2 * MH
        gsum = st.sbuf("gsum", [P, groups])
        gmean = st.sbuf("gmean", [P, groups])
        gsq = st.sbuf("gsq", [P, groups])
        gstd = st.sbuf("gstd", [P, groups])
        grstd = st.sbuf("grstd", [P, groups])
        square = K.xn[:, 0:2 * U, :].rearrange("p (t a) d -> p t (a d)", a=2)
        kv_t = st.sbuf("kv_t", [P, 2, P])
        kvo = st.sbuf("kvo", [P, 2, D])
        ps_h = st.psum("ps_h", [P, 2, 512])
        ps_kv = st.psum("ps_kv", [P, 2, 512])
        ps_c = st.psum("ps_c", [P, 2, 512])
        ps_m = st.psum("ps_m", [P, 2, 512])
        s_w, s_wa, s_h, s_kv = st.sem("w"), st.sem("wa"), st.sem("h"), st.sem("kv")
        s_hout, s_adout, s_kvout, s_table = st.sem("hout"), st.sem("adout"), st.sem("kvout"), st.sem("table")
        s_dve, s_cen, s_sq, s_var, s_std, s_norm, s_gain, s_shift = (
            st.sem(n) for n in ("dve", "cen", "sq", "var", "std", "norm", "gain", "shift"))
        s_c, s_bd, s_kvo, s_kvos, s_m, s_ones = (st.sem(n) for n in ("c", "bd", "kvo", "kvos", "m", "ones"))
        block = st.block()

        @block.sync
        def _(sp):
            sp.dma_start(w[:, :, 0:D], A["g0_wt"].rearrange("(k p) n -> p k n", p=P)).then_inc(s_w, 16)
            load_rows(sp, s_w, att[:, 0, :], A["g0_as"])
            load_rows(sp, s_w, att[:, 1, :], A["g0_ad"])
            sp.dma_start(wkv[:, :, 0:D], A["m0_wkt"].rearrange("(k p) n -> p k n", p=P)).then_inc(s_w, 16)
            sp.dma_start(wkv[:, :, D:2 * D], A["m0_wvt"].rearrange("(k p) n -> p k n", p=P)).then_inc(s_w, 16)
            sp.dma_start(wot[:, :, :], A["m0_wot"].rearrange("(k p) n -> p k n", p=P)).then_inc(s_w, 16)
            sp.dma_start(wq[:, :, :], A["m0_wq"].rearrange("(k p) n -> p k n", p=P)).then_inc(s_w, 16)
            load_rows(sp, s_w, gain[:, 0, :], A["m0_kg"])
            load_rows(sp, s_w, gain[:, 1, :], A["m0_vg"])
            load_rows(sp, s_w, shift[:, 0, :], A["m0_kb"])
            load_rows(sp, s_w, shift[:, 1, :], A["m0_vb"])
            sp.wait_ge(s_ones, 1)
            with sp.Fori(0, NT) as t:
                sp.wait_ge(s_hout, t + 1)
                sp.dma_start(K.table0[bass.ds(t * P, P), :], K.tab0[:, t, :]).then_inc(s_table, 16)
            sp.wait_ge(s_adout, NT)
            sp.dma_start(K.att_table[H0].rearrange("(t p) h -> p t h", p=P), K.att_n[:, :, 0:H0]).then_inc(s_table, 16)
            sp.wait_ge(s_table, 16 * (NT + 1))

        @block.gpsimd
        def _(pool):
            st.clear_stale(pool)
            pool.memset(K.tab0[:, :, :].rearrange("p t (h r) -> p (t h) r", r=R)[:, :, DH0:R], 1.0).then_inc(s_ones, 1)
            pool.wait_ge(s_w, 16 * 11)
            for c in range(NT // U):
                view = kv[:, c * U:(c + 1) * U, :].rearrange("p t (a h d) -> p t a h d", a=2, h=MH)
                pool.wait_ge(s_norm, c + 1)
                for t in range(U):
                    ins = pool.tensor_tensor(view[:, t], view[:, t], gain[:, :, :].unsqueeze(2).broadcast_to([P, 2, MH, MD]), ALU.mult)
                ins.then_inc(s_gain, 1)
                pool.wait_ge(s_gain, c + 1)
                for t in range(U):
                    ins = pool.tensor_tensor(view[:, t], view[:, t], shift[:, :, :].unsqueeze(2).broadcast_to([P, 2, MH, MD]), ALU.add)
                ins.then_inc(s_shift, 1)

        @block.tensor
        def _(pe):
            pe.wait_ge(s_w, 16 * 11)
            pe.wait_ge(s_wa, 2)
            for t in range(NT):
                if t >= 2:
                    pe.wait_ge(s_adout, t - 1)
                    pe.wait_ge(s_kvout, t - 1)
                for k in range(2):
                    ins = pe.matmul(ps_h[:, t % 2, 0:D + 2 * H0], lhsT=K.xn_t[:, k, t * P:(t + 1) * P], rhs=w[:, k, :],
                                    start=(k == 0), stop=(k == 1))
                ins.then_inc(s_h, 1)
                for k in range(2):
                    ins = pe.matmul(ps_kv[:, t % 2, :], lhsT=K.xn_t[:, k, t * P:(t + 1) * P], rhs=wkv[:, k, :],
                                    start=(k == 0), stop=(k == 1))
                ins.then_inc(s_kv, 1)
            for t in range(NT):
                if t % U == 0:
                    pe.wait_ge(s_shift, t // U + 1)
                rows = P if t < NT - 1 else NLAST
                for c in range(2):
                    ins = pe.matmul(ps_c[:, c, 0:P], lhsT=kv[0:rows, t, D + c * P:D + (c + 1) * P],
                                    rhs=kv[0:rows, t, c * P:(c + 1) * P], start=(t == 0), stop=(t == NT - 1))
            ins.then_inc(s_c, 1)
            pe.wait_ge(s_bd, 1)
            for c in range(2):
                ins = pe.matmul(ps_m[:, c, 0:D], lhsT=kv_t[:, c, :], rhs=wot[:, c, :], start=True, stop=True)
            ins.then_inc(s_kvo, 1)
            pe.wait_ge(s_kvos, 1)
            for c in range(2):
                for k in range(2):
                    ins = pe.matmul(ps_c[:, c, 0:D], lhsT=wq[:, k, c * P:(c + 1) * P], rhs=kvo[:, k, :],
                                    start=(k == 0), stop=(k == 1))
            ins.then_inc(s_m, 1)

        @block.scalar
        def _(act):
            with act.Fori(0, (NT - 1) // 2) as i:
                for j in range(2):
                    t = 2 * i + j
                    act.wait_ge(s_h, t + 1)
                    act.activation(K.tab0[:, t, :].rearrange("p (h r) -> p h r", r=R)[:, :, 0:DH0],
                                   ps_h[:, j, 0:D].rearrange("p (h d) -> p h d", d=DH0), ACT.Copy).then_inc(s_hout, 1)
                    act.activation(K.att_n[:, t, :], ps_h[:, j, D:D + 2 * H0], ACT.Copy).then_inc(s_adout, 1)
            t = NT - 1
            act.wait_ge(s_h, NT)
            act.activation(K.tab0[:, t, :].rearrange("p (h r) -> p h r", r=R)[:, :, 0:DH0],
                           ps_h[:, 0, 0:D].rearrange("p (h d) -> p h d", d=DH0), ACT.Copy).then_inc(s_hout, 1)
            act.activation(K.att_n[:, t, :], ps_h[:, 0, D:D + 2 * H0], ACT.Copy).then_inc(s_adout, 1)
            for c in range(NT // U):
                act.wait_ge(s_cen, c + 1)
                act.activation(square[:, :, :], kv[:, c * U:(c + 1) * U, :], ACT.Square).then_inc(s_sq, 1)
                act.wait_ge(s_var, c + 1)
                act.activation(gstd[:, :], gsq[:, :], ACT.Sqrt, scale=1.0 / MD, bias=K.eps[:, 0:1]).then_inc(s_std, 1)

        @block.vector
        def _(dve):
            n = [0]

            def step(ins):
                n[0] += 1
                ins.then_inc(s_dve, 1)
                dve.wait_ge(s_dve, n[0])

            dve.wait_ge(s_w, 16 * 11)
            for a, tmp in ((0, att_w), (1, att_w2)):
                step(dve.tensor_tensor(tmp[:, :, :], w[:, :, 0:D], att[:, a, :].unsqueeze(1).broadcast_to([P, 2, D]), ALU.mult))
                dve.tensor_reduce(w[:, :, D + a * H0:D + (a + 1) * H0], tmp[:, :, :].rearrange("p k (h d) -> p k h d", h=H0),
                                  AX, ALU.add).then_inc(s_wa, 1)
            with dve.Fori(0, (NT - 1) // 2) as i:
                for j in range(2):
                    dve.wait_ge(s_kv, 2 * i + j + 1)
                    dve.tensor_copy(kv[:, 2 * i + j, :], ps_kv[:, j, :]).then_inc(s_kvout, 1)
            dve.wait_ge(s_kv, NT)
            dve.tensor_copy(kv[:, NT - 1, :], ps_kv[:, 0, :]).then_inc(s_kvout, 1)
            dve.wait_ge(s_kvout, NT)
            for c in range(NT // U):
                part = kv[:, c * U:(c + 1) * U, :].rearrange("p t (g d) -> p (t g) d", d=MD)
                step(dve.tensor_reduce(gsum[:, :], part, AX, ALU.add))
                step(dve.tensor_scalar(gmean[:, :], gsum[:, :], 1.0 / MD, None, ALU.mult))
                dve.tensor_tensor(part, part, gmean[:, :].unsqueeze(2).broadcast_to([P, groups, MD]), ALU.subtract).then_inc(s_cen, 1)
                dve.wait_ge(s_sq, c + 1)
                dve.tensor_reduce(gsq[:, :], square[:, :, :].rearrange("p t (g d) -> p (t g) d", d=MD), AX, ALU.add).then_inc(s_var, 1)
                dve.wait_ge(s_std, c + 1)
                step(dve.reciprocal(grstd[:, :], gstd[:, :]))
                dve.tensor_tensor(part, part, grstd[:, :].unsqueeze(2).broadcast_to([P, groups, MD]), ALU.mult).then_inc(s_norm, 1)
            step(dve.memset(kv_t[:, :, :], 0.0))
            dve.wait_ge(s_c, 1)
            for h in range(2):
                ins = dve.tensor_scalar(kv_t[h * MD:(h + 1) * MD, :, h * MD:(h + 1) * MD],
                                        ps_c[h * MD:(h + 1) * MD, :, h * MD:(h + 1) * MD], 1.0 / N, None, ALU.mult)
            ins.then_inc(s_bd, 1)
            dve.wait_ge(s_kvo, 1)
            dve.tensor_copy(kvo[:, :, :], ps_m[:, :, 0:D]).then_inc(s_kvos, 1)
            dve.wait_ge(s_m, 1)
            dve.tensor_copy(K.mix[:, :, :], ps_c[:, :, 0:D]).then_inc(s_kvos, 1)
            dve.wait_ge(s_kvos, 2)


def edge_scores(prog, K, name, H, C, A=None):
    with Stage(prog, name) as st:
        Q, U2 = 4, 2
        al = K.al[:, 0:WS * H].rearrange("p (s h) -> p s h", h=H)
        rel = st.sbuf("rel", [P, Q, EB], BF16)
        hot = st.sbuf("hot", [P, Q, EB])
        asg = st.sbuf("asg", [P, Q, SUB, max(H, 2)])
        idx = st.sbuf("idx", [P, Q, SUB], I32)
        s_idx = st.sem("idx")
        ps_ad = st.psum("ps_ad", [P, U2, 512])
        s_load = [st.sem(f"load{q}") for q in range(Q)]
        s_gath, gathered = K.gath, K.gathered
        s_hot, s_ad, s_al, s_fin = (st.sem(n) for n in ("hot", "ad", "al", "fin"))
        if A:
            al2 = K.arena_a[:, 0:WS * H].rearrange("p (s h) -> p s h", h=H)
            attr = st.sbuf("attr", [4, Q, EB])
            enc_w = st.sbuf("enc_w", [4, D])
            enc = st.sbuf("enc", [P, U2, SUB * D])
            prod = st.sbuf("prod", [P, U2, SUB * D])
            ps_en = st.psum("ps_en", [P, U2, 512])
            ps_hd = st.psum("ps_hd", [P, U2, 512])
            s_one, s_encw, s_en, s_hd, s_enc, s_prod, s_red = (
                st.sem(n) for n in ("one", "encw", "en", "hd", "enc", "prod", "red"))
        block = st.block()

        @block.sync
        def _(sp):
            if A:
                sp.dma_start(enc_w[0:3, :], A["g0_ewt"]).then_inc(s_encw, 16)
                sp.dma_start(enc_w[3:4, :], A["g0_eb"]).then_inc(s_encw, 16)
                sp.wait_ge(s_one, 1)
            with sp.Fori(0, W // Q) as i:
                for q in range(Q):
                    w = i * Q + q
                    sp.wait_ge(s_ad, w + 1)
                    sp.dma_start(rel[:, q, :], K.rel_rows[bass.ds(w, 1), :].partition_broadcast(P).rearrange("p a e -> p (a e)")).then_inc(s_load[q], 16)
                    if A:
                        sp.dma_start(attr[0:3, q, :], K.attr_rows[:, w, :]).then_inc(s_load[q], 16)

        @block.gpsimd
        def _(pool):
            st.clear_stale(pool)
            with pool.Fori(0, W // Q) as i:
                for q in range(Q):
                    w = i * Q + q
                    pool.wait_ge(s_idx, w + 1)
                    pool.nop(nofuse=True)
                    for s in range(SUB):
                        pool.indirect_dma_start(asg[:, q, s, :], None, K.att_table[H][:, :],
                                                bass.IndirectOffsetOnAxis(ap=idx[:, q, s:s + 1], axis=0)).then_inc(s_gath[q], 16)

        @block.tensor
        def _(pe):
            pe.sem_inc(s_ad, Q)
            if A:
                pe.wait_ge(s_encw, 32)
            with pe.Fori(0, W // Q) as i:
                for q in range(Q):
                    w = i * Q + q
                    window = pe.value_load(K.window[0:1, bass.ds(w, 1)], min_val=0, max_val=NT - 1)
                    pe.wait_ge(s_hot, w + 1)
                    if A:
                        pe.wait_ge(s_load[q], 32 * (i + 1))
                        pe.wait_ge(s_enc, w + 1)
                        for s in range(SUB):
                            ins = pe.matmul(ps_en[:, q % U2, s * D:(s + 1) * D], lhsT=attr[:, q, s * P:(s + 1) * P], rhs=enc_w[:, :], start=True, stop=True)
                        ins.then_inc(s_en, 1)
                        pe.wait_ge(s_prod, w + 1)
                        for s in range(SUB):
                            ins = pe.matmul(ps_hd[:, q % U2, s * D:(s + 1) * D], lhsT=hot[:, q, s * P:(s + 1) * P],
                                            rhs=K.tab0[:, window, :].rearrange("p (h r) -> p h r", h=H0)[:, :, 0:DH0], start=True, stop=True)
                        ins.then_inc(s_hd, 1)
                    pe.wait_ge(s_al, w + 3)
                    for s in range(SUB):
                        ins = pe.matmul(ps_ad[:, q % U2, s * H:(s + 1) * H], lhsT=hot[:, q, s * P:(s + 1) * P],
                                        rhs=K.att_n[:, window, H:2 * H], start=True, stop=True)
                    ins.then_inc(s_ad, 1)

        @block.scalar
        def _(act):
            def sources(q, w):
                act.wait_ge(s_al, w + 1)
                act.activation(idx[:, q, :], K.src_col[:, bass.ds(w * SUB, SUB)], ACT.Copy).then_inc(s_idx, 1)

            def encode(q, w):
                if A:
                    act.wait_ge(s_en, w + 1)
                    act.wait_ge(s_prod, w + 1)
                    act.activation(enc[:, q % U2, :], ps_en[:, q % U2, :], ACT.Relu).then_inc(s_enc, 1)

            if A:
                act.sem_inc(s_enc, U2)
            sources(0, 0)
            sources(1, 1)
            with act.Fori(0, W // Q - 1) as i:
                for q in range(Q):
                    sources((q + 2) % Q, i * Q + q + 2)
                    encode(q, i * Q + q)
            for q in range(Q):
                if q + 2 < Q:
                    sources(q + 2, W - Q + q + 2)
                encode(q, W - Q + q)

        @block.vector
        def _(dve):
            def one_hot(i, q, w):
                dve.wait_ge(s_load[q], (32 if A else 16) * (i + 1))
                dve.wait_ge(s_ad, w + 1)
                dve.tensor_scalar(hot[:, q, :], rel[:, q, :], K.iota_part[:, 0:1], None, ALU.is_equal).then_inc(s_hot, 1)

            def scores(i, q, w):
                if A:
                    dve.wait_ge(s_hd, w + 1)
                    dve.wait_ge(s_enc, w + 3)
                    dve.wait_ge(s_red, w + 1)
                    dve.tensor_tensor(prod[:, q % U2, :], enc[:, q % U2, :], ps_hd[:, q % U2, :], ALU.mult).then_inc(s_prod, 1)
                dve.wait_ge(s_ad, w + 1 + Q)
                dve.wait_ge(s_gath[q], gathered + 32 * (i + 1))
                out = al2 if A else al
                dve.tensor_tensor(out[:, bass.ds(w * SUB, SUB), :], ps_ad[:, q % U2, 0:SUB * H].rearrange("p (s h) -> p s h", h=H),
                                  asg[:, q, :, 0:H], ALU.add).then_inc(s_al, 1)
                if A:
                    dve.wait_ge(s_prod, w + 3)
                    dve.tensor_reduce(al[:, bass.ds(w * SUB, SUB), :], prod[:, q % U2, :].rearrange("p (s h d) -> p s h d", s=SUB, d=DH0),
                                      AX, ALU.add).then_inc(s_red, 1)

            dve.sem_inc(s_al, Q)
            if A:
                dve.sem_inc(s_prod, U2)
                dve.sem_inc(s_red, U2)
                dve.memset(attr[:, :, :], 1.0).then_inc(s_one, 1)
            one_hot(0, 0, 0)
            one_hot(0, 1, 1)
            with dve.Fori(0, W // Q - 1) as i:
                for q in range(Q):
                    one_hot(i + (q + 2) // Q, (q + 2) % Q, i * Q + q + 2)
                    scores(i, q, i * Q + q)
            i = W // Q - 1
            for q in range(Q):
                if q + 2 < Q:
                    one_hot(i, q + 2, i * Q + q + 2)
                scores(i, q, i * Q + q)
            dve.wait_ge(s_al, W + Q)
            if A:
                dve.wait_ge(s_red, W + U2)
                dve.tensor_tensor(al[:, :, :], al[:, :, :], al2[:, :, :], ALU.add).then_inc(s_fin, 1)
            else:
                dve.sem_inc(s_fin, 1)
            dve.wait_ge(s_fin, 1)
            turn = K.xn[:, :, :].rearrange("p t d -> p (t d)")[:, 0:WS * H].rearrange("p (j c h) -> p j c h", c=C, h=H)
            view = al.rearrange("p (c j) h -> p j c h", c=C)
            for c in range(C):
                ins = dve.scalar_tensor_tensor(turn[:, :, c, :], view[:, :, c, :], NEG_SLOPE, view[:, :, c, :], ALU.mult, ALU.max)
            ins.then_inc(s_fin, 1)
            dve.wait_ge(s_fin, 2)

        K.gathered += 32 * (W // Q)


def segment_softmax(prog, K, name, H, C, keep_max=None):
    J = WS // C
    R, L = C * H, J * P
    G = min(4, 512 // P)
    with Stage(prog, name) as st:
        al = K.al[:, 0:WS * H].rearrange("p (s h) -> p s h", h=H)
        turn = K.xn[:, :, :].rearrange("p t d -> p (t d)")[:, 0:WS * H]
        pen_p = K.arena_a[0:R, 0:L]
        pen_n = K.arena_a[0:R, L:2 * L]
        score = st.sbuf("score", [R, L])
        run = st.sbuf("run", [R, L]) if H == 1 else K.arena_b[0:R, 0:L]
        back = pen_p
        ends = st.sbuf("ends", [R, 2, 2])
        ends_row = st.sbuf("ends_row", [1, 2, 2, C, H])
        carry_row = st.sbuf("carry_row", [1, 2, C + 2, H])
        carry = st.sbuf("carry", [R, 2])
        ps_in = st.psum("ps_in", [P, 2, 512])
        ps_row = st.psum("ps_row", [P, 2, 512])
        s_pen, s_turn, s_score, s_step, s_end, s_endrow = (st.sem(n) for n in ("pen", "turn", "score", "step", "end", "endrow"))
        s_carry, s_carried, s_diff, s_exp, s_back, s_out = (st.sem(n) for n in ("carry", "carried", "diff", "exp", "back", "out"))
        turns = J // G
        block = st.block()

        @block.sync
        def _(sp):
            for pen, rows in ((pen_p, K.pen_prev), (pen_n, K.pen_next)):
                sp.dma_start(pen,
                             bass.AP(tensor=rows.tensor, offset=0, ap=[[L, C], [0, H], [1, L]])).then_inc(s_pen, 16)

        @block.gpsimd
        def _(pool):
            st.clear_stale(pool)

        @block.tensor
        def _(pe):
            for g in range(turns):
                if g >= 2:
                    pe.wait_ge(s_score, g - 1)
                for j in range(G):
                    ins = pe.transpose(ps_in[0:R, g % 2, j * P:(j + 1) * P],
                                       turn[:, (g * G + j) * R:(g * G + j + 1) * R], K.ident[:, :])
                ins.then_inc(s_turn, 1)
            for d in range(2):
                pe.wait_ge(s_end, d + 1)
                pe.transpose(ps_row[0:1, 0, 0:R], ends[:, d, 0:1], K.ident[0:R, 0:R])
                pe.transpose(ps_row[0:1, 0, R:2 * R], ends[:, d, 1:2], K.ident[0:R, 0:R]).then_inc(s_endrow, 1)
                pe.wait_ge(s_carry, d + 1)
                first = 0 if d == 0 else 2
                pe.transpose(ps_row[0:R, 1, 0:1], carry_row[:, d, first:first + C, :].rearrange("p c h -> p (c h)"),
                             K.ident[0:1, 0:1]).then_inc(s_carried, 1)
            for g in range(turns):
                pe.wait_ge(s_exp, 1)
                if g >= 2:
                    pe.wait_ge(s_out, g - 1)
                for j in range(G):
                    ins = pe.transpose(ps_in[:, g % 2, j * R:(j + 1) * R], score[:, (g * G + j) * P:(g * G + j + 1) * P],
                                       K.ident[0:R, 0:R])
                ins.then_inc(s_back, 1)
            if keep_max is not None:
                for g in range(turns):
                    pe.wait_ge(s_diff, 3)
                    b = turns + g
                    if b >= 2:
                        pe.wait_ge(s_out, b - 1)
                    for j in range(G):
                        ins = pe.transpose(ps_in[:, b % 2, j * R:(j + 1) * R], run[:, (g * G + j) * P:(g * G + j + 1) * P],
                                           K.ident[0:R, 0:R])
                    ins.then_inc(s_back, 1)

        @block.scalar
        def _(act):
            for g in range(turns):
                act.wait_ge(s_turn, g + 1)
                act.activation(score[:, g * G * P:(g + 1) * G * P], ps_in[0:R, g % 2, 0:G * P], ACT.Copy).then_inc(s_score, 1)
            act.wait_ge(s_diff, 1)
            act.activation(score[:, :], score[:, :], ACT.Exp).then_inc(s_exp, 1)

            def put(out, b):
                act.activation(out, ps_in[:, b % 2, 0:G * R].rearrange("p (j c h) -> p c j h", j=G, h=H), ACT.Copy).then_inc(s_out, 1)

            for g in range(turns):
                act.wait_ge(s_back, g + 1)
                put(al.rearrange("p (c j) h -> p c j h", j=J)[:, :, g * G:(g + 1) * G, :], g)
            if keep_max is not None:
                kept = keep_max.rearrange("p (c j) h -> p c j h", j=J)
                for g in range(turns):
                    act.wait_ge(s_back, turns + g + 1)
                    put(kept[:, :, g * G:(g + 1) * G, 0:H], turns + g)
                act.activation(keep_max[:, :, H], K.last_col[:, :], ACT.Copy).then_inc(s_out, 1)
                act.wait_ge(s_out, 2 * turns + 1)

        @block.vector
        def _(dve):
            n = [0]

            def step(ins):
                n[0] += 1
                ins.then_inc(s_step, 1)
                dve.wait_ge(s_step, n[0])

            dve.memset(carry_row[:, :, :, :], -BIG)
            dve.wait_ge(s_pen, 32)
            dve.tensor_reduce(ends[:, 0, 1:2], pen_p, AX, ALU.min)
            step(dve.tensor_reduce(ends[:, 1, 1:2], pen_n, AX, ALU.min))
            dve.wait_ge(s_score, turns)
            for d, (out, pen, data, last) in enumerate(((run[:, :], pen_p, score[:, :], L - 1),
                                                        (back[:, ::-1], pen_n[:, ::-1], run[:, ::-1], 0))):
                step(dve.tensor_tensor_scan(out, pen, data, -BIG, ALU.add, ALU.max))
                whole = (run if d == 0 else back)
                dve.tensor_copy(ends[:, d, 0:1], whole[:, last:last + 1]).then_inc(s_end, 1)
                dve.wait_ge(s_endrow, d + 1)
                step(dve.tensor_copy(ends_row[:, d, :, :, :].rearrange("p a c h -> p (a c h)"), ps_row[0:1, 0, 0:2 * R]))
                order = slice(None) if d == 0 else slice(None, None, -1)
                for h in range(H):
                    ins = dve.tensor_tensor_scan(carry_row[:, d, 1:C + 1, h][:, order], ends_row[:, d, 1, :, h][:, order],
                                                 ends_row[:, d, 0, :, h][:, order], -BIG, ALU.add, ALU.max)
                ins.then_inc(s_carry, 1)
                dve.wait_ge(s_carried, d + 1)
                step(dve.tensor_copy(carry[:, d:d + 1], ps_row[0:R, 1, 0:1]))
                step(dve.tensor_tensor_scan(out, pen, data, carry[:, d:d + 1], ALU.add, ALU.max))
            dve.tensor_tensor(score[:, :], score[:, :], back, ALU.subtract).then_inc(s_diff, 1)
            if keep_max is not None:
                dve.wait_ge(s_diff, 1)
                dve.tensor_scalar(pen_n, pen_n, -1.0 / BIG, None, ALU.mult).then_inc(s_diff, 1)
                dve.wait_ge(s_diff, 2)
                dve.tensor_tensor(run[:, :], back, pen_n, ALU.mult).then_inc(s_diff, 1)
                dve.wait_ge(s_diff, 3)


def aggregate(prog, K, name, H, RW, table, acc, width, extra=None):
    B = 1 if RW <= 512 else 2
    part = RW // B
    X = 0 if extra is None else width - part
    with Stage(prog, name) as st:
        Q, U2 = 4, 2
        al = K.al[:, 0:WS * H].rearrange("p (s h) -> p s h", h=H)
        rows = st.sbuf("rows", [P, Q, SUB, RW])
        hot = st.sbuf("hot", [P, Q, SUB, P])
        idx = st.sbuf("idx", [P, Q, SUB], I32)
        s_idx = st.sem("idx")
        ps = st.psum("ps", [P, U2, B, 512])
        s_gath, gathered = K.gath, K.gathered
        s_hot, s_msg, s_sum, s_acc, s_zero = (st.sem(n) for n in ("hot", "msg", "sum", "acc", "zero"))
        block = st.block()

        @block.gpsimd
        def _(pool):
            st.clear_stale(pool)
            pool.memset(acc, 0.0).then_inc(s_zero, 1)
            with pool.Fori(0, W // Q) as i:
                for q in range(Q):
                    w = i * Q + q
                    pool.wait_ge(s_idx, w + 1)
                    pool.nop(nofuse=True)
                    for s in range(SUB):
                        pool.indirect_dma_start(rows[:, q, s, :], None, table,
                                                bass.IndirectOffsetOnAxis(ap=idx[:, q, s:s + 1], axis=0)).then_inc(s_gath[q], 16)

        @block.scalar
        def _(act):
            with act.Fori(0, W // Q) as i:
                for q in range(Q):
                    w = i * Q + q
                    act.wait_ge(s_sum, w + 1)
                    act.activation(idx[:, q, :], K.src_col[:, bass.ds(w * SUB, SUB)], ACT.Copy).then_inc(s_idx, 1)

        @block.tensor
        def _(pe):
            pe.sem_inc(s_sum, Q)
            with pe.Fori(0, W // Q) as i:
                for q in range(Q):
                    w = i * Q + q
                    pe.wait_ge(s_hot, w + 1)
                    pe.wait_ge(s_msg, w + 1)
                    pe.wait_ge(s_acc, w + 1)
                    for s in range(SUB):
                        for b in range(B):
                            ins = pe.matmul(ps[:, q % U2, b, 0:part], lhsT=hot[:, q, s, :], rhs=rows[:, q, s, b * part:(b + 1) * part],
                                            start=(s == 0), stop=(s == SUB - 1))
                    if X:
                        for b in range(B):
                            for s in range(SUB):
                                ins = pe.matmul(ps[:, q % U2, b, part:width], lhsT=hot[:, q, s, :], rhs=extra[:, w * SUB + s, :],
                                                start=(s == 0), stop=(s == SUB - 1))
                    ins.then_inc(s_sum, 1)

        @block.vector
        def _(dve):
            def message(i, q, w):
                dve.wait_ge(s_sum, w + 1)
                for s in range(SUB):
                    ins = dve.tensor_scalar(hot[:, q, s, :], K.iota_row[:, :], K.rel_col[:, bass.ds(w * SUB + s, 1)], None, ALU.is_equal)
                ins.then_inc(s_hot, 1)
                dve.wait_ge(s_gath[q], gathered + 32 * (i + 1))
                view = rows[:, q, :, :].rearrange("p s (h r) -> p (s h) r", h=H)
                dve.tensor_tensor(view, view, al[:, bass.ds(w * SUB, SUB), :].rearrange("p s h -> p (s h)").unsqueeze(2).broadcast_to([P, SUB * H, RW // H]),
                                  ALU.mult).then_inc(s_msg, 1)

            def add(q, w, wait_last):
                window = dve.value_load(K.window[0:1, bass.ds(w, 1)], min_val=0, max_val=NT - 1)
                dve.wait_ge(s_sum, w + 1 + Q)
                dve.wait_ge(s_acc, w + 2)
                out = acc[:, window, :].rearrange("p (b c) -> p b c", b=B)
                dve.tensor_tensor(out, out, ps[:, q % U2, :, 0:width], ALU.add).then_inc(s_acc, 1)

            dve.sem_inc(s_acc, U2)
            dve.wait_ge(s_zero, 1)
            message(0, 0, 0)
            with dve.Fori(0, W // Q - 1) as i:
                for q in range(Q):
                    message(i + (q + 1) // Q, (q + 1) % Q, i * Q + q + 1)
                    add(q, i * Q + q, True)
            i = W // Q - 1
            for q in range(Q):
                if q + 1 < Q:
                    message(i, q + 1, i * Q + q + 1)
                add(q, i * Q + q, True)
            dve.wait_ge(s_acc, W + U2)

        K.gathered += 32 * (W // Q)


def finish_l0(prog, K, A):
    R = DH0 + 1
    with Stage(prog, "fin0") as st:
        den = st.sbuf("den", [P, NT, H0])
        rden = st.sbuf("rden", [P, NT, H0])
        bias = st.sbuf("bias", [P, 3, D])
        ps = st.psum("ps", [P, 4, 512])
        s_b, s_dve, s_mm, s_add, s_gnn = (st.sem(n) for n in ("b", "dve", "mm", "add", "gnn"))
        acc = K.acc0[:, :, :].rearrange("p t (h r) -> p t h r", r=R)
        block = st.block()

        @block.sync
        def _(sp):
            load_rows(sp, s_b, bias[:, 0, :], A["g0_b"])
            load_rows(sp, s_b, bias[:, 1, :], A["m0_bo"])

        @block.gpsimd
        def _(pool):
            st.clear_stale(pool)

        @block.tensor
        def _(pe):
            for t in range(NT):
                if t >= 4:
                    pe.wait_ge(s_add, t - 3)
                for k in range(2):
                    ins = pe.matmul(ps[:, t % 4, 0:D], lhsT=K.xn_t[:, k, t * P:(t + 1) * P], rhs=K.mix[:, k, :], start=(k == 0), stop=(k == 1))
                ins.then_inc(s_mm, 1)

        @block.vector
        def _(dve):
            n = [0]

            def step(ins):
                n[0] += 1
                ins.then_inc(s_dve, 1)
                dve.wait_ge(s_dve, n[0])

            step(dve.tensor_scalar(den[:, :, :], acc[:, :, :, DH0], 1e-10, None, ALU.max))
            step(dve.reciprocal(rden[:, :, :], den[:, :, :]))
            dve.wait_ge(s_b, 32)
            step(dve.tensor_tensor(bias[:, 2, :], bias[:, 0, :], bias[:, 1, :], ALU.add))
            step(dve.tensor_tensor(acc[:, :, :, 0:DH0], acc[:, :, :, 0:DH0], rden[:, :, :].unsqueeze(3).broadcast_to([P, NT, H0, DH0]), ALU.mult))
            step(dve.tensor_tensor(K.x[:, :, :], K.x[:, :, :], bias[:, 2, :].unsqueeze(1).broadcast_to([P, NT, D]), ALU.add))
            step(dve.tensor_tensor(K.x[:, :, :].rearrange("p t (h d) -> p t h d", h=H0), K.x[:, :, :].rearrange("p t (h d) -> p t h d", h=H0),
                                   acc[:, :, :, 0:DH0], ALU.add))
            for t in range(NT):
                dve.wait_ge(s_mm, t + 1)
                dve.tensor_tensor(K.x[:, t, :], K.x[:, t, :], ps[:, t % 4, 0:D], ALU.add).then_inc(s_add, 1)
            dve.wait_ge(s_add, NT)


def first_best(dve, step, logits, bias, code, EX, tmp, best, hot, pick):
    shape = [P, NT, EX]
    step(dve.tensor_tensor(logits, logits, bias.unsqueeze(1).broadcast_to(shape), ALU.add))
    step(dve.tensor_reduce(best, logits, AX, ALU.max))
    step(dve.tensor_tensor(tmp, logits, best.unsqueeze(2).broadcast_to(shape), ALU.is_lt))
    step(dve.scalar_tensor_tensor(tmp, tmp, float(EX), code.unsqueeze(1).broadcast_to(shape), ALU.mult, ALU.add))
    step(dve.tensor_reduce(pick, tmp, AX, ALU.min))
    step(dve.tensor_tensor(hot, code.unsqueeze(1).broadcast_to(shape), pick.unsqueeze(2).broadcast_to(shape), ALU.is_equal))


def route_l0(prog, K, A):
    FAR = 1.0e6
    with Stage(prog, "route0") as st:
        gw = st.sbuf("gw", [P, 2, E0])
        gb = st.sbuf("gb", [P, E0])
        code = st.sbuf("code", [P, E0])
        node = st.sbuf("node", [P, NT])
        tri = st.sbuf("tri", [P, P])
        ones = st.sbuf("ones", [P, P])
        logits, tmp, hot, before, placed = (st.sbuf(n, [P, NT, E0]) for n in ("logits", "tmp", "hot", "before", "placed"))
        total, upto = st.sbuf("total", [P, NT, E0]), st.sbuf("upto", [P, NT, E0])
        best, pick, esum, prob, place, kept, slot, far, away = (
            st.sbuf(n, [P, NT]) for n in ("best", "pick", "esum", "prob", "place", "kept", "slot", "far", "away"))
        ps_l = st.psum("ps_l", [P, 512])
        ps_c = st.psum("ps_c", [P, 2, 512])
        s_w, s_const, s_logits, s_dve, s_hot, s_count = (st.sem(n) for n in ("w", "const", "logits", "dve", "hot", "count"))
        s_diff, s_exp, s_slot = (st.sem(n) for n in ("diff", "exp", "slot"))
        s_sent = st.sem_sw("sent")
        block = st.block()

        @block.sync
        def _(sp):
            sp.dma_start(gw[:, :, :], A["f0_gw"].rearrange("(k p) n -> p k n", p=P)).then_inc(s_w, 16)
            load_rows(sp, s_w, gb[:, :], A["f0_gb"])

        @block.gpsimd
        def _(pool):
            st.clear_stale(pool)
            pool.memset(ones[:, :], 1.0).then_inc(s_const, 1)
            pool.iota(code[:, :], [[1, E0]], base=E0, channel_multiplier=0, allow_small_or_imprecise_dtypes=True).then_inc(s_const, 1)
            pool.iota(node[:, :], [[P, NT]], base=0, channel_multiplier=1, allow_small_or_imprecise_dtypes=True).then_inc(s_const, 1)
            pool.wait_ge(s_const, 1)
            pool.affine_select(out=tri[:, :], in_=ones[:, :], compare_op=ALU.is_ge, fill=0.0, base=0,
                               pattern=[[1, P]], channel_multiplier=-1).then_inc(s_const, 1)
            pool.wait_ge(s_slot, 2)
            for t in range(NT):
                pool.indirect_dma_start(K.slots, bass.IndirectOffsetOnAxis(ap=K.slot_to[:, t:t + 1], axis=0), K.xn[:, t, :], None,
                                        bounds_check=E0 * CAP - 1, oob_is_err=False).then_inc(s_sent, 16)
            pool.wait_ge(s_sent, 16 * NT)

        @block.tensor
        def _(pe):
            pe.wait_ge(s_w, 32)
            for t in range(NT):
                for k in range(2):
                    ins = pe.matmul(ps_l[:, t * E0:(t + 1) * E0], lhsT=K.xn_t[:, k, t * P:(t + 1) * P], rhs=gw[:, k, :], start=(k == 0), stop=(k == 1))
            ins.then_inc(s_logits, 1)
            pe.wait_ge(s_const, 4)
            pe.wait_ge(s_hot, 1)
            flat = hot[:, :, :].rearrange("p t e -> p (t e)")
            pe.matmul(ps_c[:, 0, 0:NT * E0], lhsT=tri[:, :], rhs=flat, start=True, stop=True)
            pe.matmul(ps_c[:, 1, 0:NT * E0], lhsT=ones[:, :], rhs=flat, start=True, stop=True).then_inc(s_count, 1)

        @block.scalar
        def _(act):
            act.wait_ge(s_diff, 1)
            act.activation(tmp[:, :, :], tmp[:, :, :], ACT.Exp).then_inc(s_exp, 1)

        @block.vector
        def _(dve):
            n = [0]

            def step(ins):
                n[0] += 1
                ins.then_inc(s_dve, 1)
                dve.wait_ge(s_dve, n[0])

            dve.wait_ge(s_w, 32)
            dve.wait_ge(s_const, 4)
            dve.wait_ge(s_logits, 1)
            step(dve.tensor_copy(logits[:, :, :].rearrange("p t e -> p (t e)"), ps_l[:, 0:NT * E0]))
            first_best(dve, step, logits[:, :, :], gb[:, :], code[:, :], E0, tmp[:, :, :], best[:, :], hot[:, :, :], pick[:, :])
            dve.sem_inc(s_hot, 1)
            dve.tensor_tensor(tmp[:, :, :], logits[:, :, :], best[:, :].unsqueeze(2).broadcast_to([P, NT, E0]), ALU.subtract).then_inc(s_diff, 1)
            dve.wait_ge(s_exp, 1)
            step(dve.tensor_reduce(esum[:, :], tmp[:, :, :], AX, ALU.add))
            step(dve.reciprocal(prob[:, :], esum[:, :]))
            dve.wait_ge(s_count, 1)
            step(dve.tensor_copy(total[:, :, :].rearrange("p t e -> p (t e)"), ps_c[:, 1, 0:NT * E0]))
            for e in range(E0):
                ins = dve.tensor_tensor_scan(upto[:, :, e], total[:, :, e], total[:, :, e], 0.0, ALU.add, ALU.max)
            step(ins)
            step(dve.tensor_tensor(before[:, :, :], upto[:, :, :], total[:, :, :], ALU.subtract))
            step(dve.tensor_tensor(before[:, :, :], before[:, :, :], ps_c[:, 0, 0:NT * E0].rearrange("p (t e) -> p t e", e=E0), ALU.add))
            step(dve.tensor_tensor(placed[:, :, :], before[:, :, :], hot[:, :, :], ALU.mult))
            step(dve.tensor_reduce(place[:, :], placed[:, :, :], AX, ALU.add))
            step(dve.tensor_scalar(kept[:, :], place[:, :], float(CAP), None, ALU.is_le))
            step(dve.tensor_scalar(place[:, :], place[:, :], float(CAP), -1.0 - E0 * CAP, ALU.min, ALU.add))
            step(dve.scalar_tensor_tensor(slot[:, :], pick[:, :], float(CAP), place[:, :], ALU.mult, ALU.add))
            step(dve.tensor_scalar(far[:, :], node[:, :], float(N), FAR, ALU.is_ge, ALU.mult))
            step(dve.scalar_tensor_tensor(away[:, :], kept[:, :], -FAR, far[:, :], ALU.mult, ALU.add))
            step(dve.scalar_tensor_tensor(far[:, :], slot[:, :], FAR, away[:, :], ALU.add, ALU.add))
            dve.tensor_copy(K.slot_to[:, :], far[:, :]).then_inc(s_slot, 1)
            dve.tensor_copy(K.slot_from[:, :], slot[:, :]).then_inc(s_slot, 1)
            dve.tensor_tensor(K.gate[:, :], prob[:, :], kept[:, :], ALU.mult).then_inc(s_slot, 1)
            dve.wait_ge(s_slot, 3)


def experts_l0(prog, K, A):
    FC = F0 // P
    M = -(-CAP // P)
    size = [min(P, CAP - m * P) for m in range(M)]
    with Stage(prog, "moe0") as st:
        a = K.arena_a
        w1 = [a[:, e * 2 * F0:(e + 1) * 2 * F0].rearrange("p (k f) -> p k f", k=2) for e in range(2)]
        at = 4 * F0
        w2 = [a[:, at + e * FC * D:at + (e + 1) * FC * D].rearrange("p (c d) -> p c d", c=FC) for e in range(2)]
        at += 2 * FC * D
        rows = [a[:, at + e * M * D:at + (e + 1) * M * D].rearrange("p (m d) -> p m d", m=M) for e in range(2)]
        xs_t = K.arena_b[:, 0:2 * 512].rearrange("p (k s) -> p k s", k=2)
        h_t = K.arena_b[:, 2 * 512:2 * 512 + FC * 512].rearrange("p (c s) -> p c s", c=FC)
        y = K.al[:, 0:M * D].rearrange("p (m d) -> p m d", m=M)
        b1 = st.sbuf("b1", [P, E0 * FC])
        b2 = st.sbuf("b2", [P, E0, D])
        ps_t = st.psum("ps_t", [P, 2, 512])
        ps_h = st.psum("ps_h", [P, 2, 512])
        ps_y = st.psum("ps_y", [P, 2, 512])
        s_b = st.sem("b")
        s_in = [st.sem(f"in{e}") for e in range(2)]
        s_t, s_xt, s_h, s_ht, s_y, s_yb, s_used = (st.sem(n) for n in ("t", "xt", "h", "ht", "y", "yb", "used"))
        s_out = [st.sem_sw(f"out{m}") for m in range(M)]
        block = st.block()

        @block.sync
        def _(sp):
            sp.dma_start(b1[:, :], A["f0_b1"]).then_inc(s_b, 16)
            load_rows(sp, s_b, b2[:, :, :].rearrange("p e d -> p (e d)"), A["f0_b2"])
            with sp.Fori(0, E0 // 2) as i:
                for j in range(2):
                    e = i * 2 + j
                    sp.wait_ge(s_used, e + 1)
                    sp.dma_start(rows[j][:, 0:M - 1, :], K.slots[bass.ds(e * CAP, (M - 1) * P), :].rearrange("(m p) d -> p m d", p=P)).then_inc(s_in[j], 16)
                    sp.dma_start(rows[j][0:size[-1], M - 1, :], K.slots[bass.ds(e * CAP + (M - 1) * P, size[-1]), :]).then_inc(s_in[j], 16)
                    sp.dma_start(w1[j], A["f0_w1"][e].rearrange("(k p) f -> p k f", p=P)).then_inc(s_in[j], 16)
                    sp.dma_start(w2[j], A["f0_w2"][e].rearrange("(c p) d -> p c d", p=P)).then_inc(s_in[j], 16)

        @block.tensor
        def _(pe):
            pe.sem_inc(s_used, 2)
            with pe.Fori(0, E0 // 2) as i:
                for j in range(2):
                    e = i * 2 + j
                    pe.wait_ge(s_in[j], 64 * (i + 1))
                    pe.wait_ge(s_xt, e + 1)
                    for k in range(2):
                        for m in range(M):
                            ins = pe.transpose(ps_t[:, k, m * P:m * P + size[m]], rows[j][0:size[m], m, k * P:(k + 1) * P], K.ident[0:size[m], 0:size[m]])
                    ins.then_inc(s_t, 1)
                    pe.wait_ge(s_xt, e + 2)
                    for c in range(FC):
                        pe.wait_ge(s_ht, e * FC + c + 1)
                        for k in range(2):
                            ins = pe.matmul(ps_h[:, c % 2, 0:CAP], lhsT=w1[j][:, k, c * P:(c + 1) * P], rhs=xs_t[:, k, 0:CAP], start=(k == 0), stop=(k == 1))
                        ins.then_inc(s_h, 1)
                    pe.wait_ge(s_ht, e * FC + FC + 2)
                    for m in range(M):
                        pe.wait_ge(s_yb, e * M + m + 1)
                        for c in range(FC):
                            ins = pe.matmul(ps_y[0:size[m], m % 2, 0:D], lhsT=h_t[:, c, m * P:m * P + size[m]], rhs=w2[j][:, c, :], start=(c == 0), stop=(c == FC - 1))
                        ins.then_inc(s_y, 1)
                    pe.drain().then_inc(s_used, 1)

        @block.scalar
        def _(act):
            act.sem_inc(s_xt, 1)
            act.sem_inc(s_ht, 2)
            act.wait_ge(s_b, 32)
            with act.Fori(0, E0) as e:
                act.wait_ge(s_t, e + 1)
                act.activation(xs_t[:, :, 0:CAP], ps_t[:, :, 0:CAP], ACT.Copy).then_inc(s_xt, 1)
                for c in range(FC):
                    act.wait_ge(s_h, e * FC + c + 1)
                    act.activation(h_t[:, c, 0:CAP], ps_h[:, c % 2, 0:CAP], ACT.Relu, bias=b1[:, bass.ds(e * FC + c, 1)]).then_inc(s_ht, 1)

        @block.vector
        def _(dve):
            dve.sem_inc(s_yb, 2)
            dve.wait_ge(s_b, 32)

            def add_bias(e, m):
                dve.wait_ge(s_y, e * M + m + 1)
                dve.tensor_tensor(y[0:size[m], m, :], ps_y[0:size[m], m % 2, 0:D], b2[0:size[m], e, :], ALU.add).then_inc(s_yb, 1)

            for m in range(M):
                add_bias(0, m)
            with dve.Fori(1, E0) as e:
                for m in range(M):
                    dve.wait_ge(s_out[m], 16 * e)
                    add_bias(e, m)

        @block.gpsimd
        def _(pool):
            st.clear_stale(pool)
            with pool.Fori(0, E0) as e:
                for m in range(M):
                    pool.wait_ge(s_yb, e * M + m + 3)
                    pool.dma_start(K.y_slots[bass.ds(e * CAP + m * P, size[m]), :], y[0:size[m], m, :]).then_inc(s_out[m], 16)
            for m in range(M):
                pool.wait_ge(s_out[m], 16 * E0)


def combine_l0(prog, K):
    TOP, LIMIT = 3.4028234663852886e38, 1.0e4
    with Stage(prog, "join0") as st:
        y = K.arena_b[:, 0:NT * D].rearrange("p (t d) -> p t d", t=NT)
        z = K.arena_a[:, 0:3 * U * D].rearrange("p (a t d) -> p a t d", a=3, t=U)
        mask = st.sbuf("mask", [P, U, D], I32)
        s_y = [st.sem_sw(f"y{c}") for c in range(NT // U)]
        s_dve = st.sem("dve")
        block = st.block()

        @block.gpsimd
        def _(pool):
            st.clear_stale(pool)
            for t in range(NT):
                pool.indirect_dma_start(y[:, t, :], None, K.y_slots, bass.IndirectOffsetOnAxis(ap=K.slot_from[:, t:t + 1], axis=0)).then_inc(s_y[t // U], 16)

        @block.vector
        def _(dve):
            n = [0]

            def step(ins):
                n[0] += 1
                ins.then_inc(s_dve, 1)
                dve.wait_ge(s_dve, n[0])

            for c in range(NT // U):
                dve.wait_ge(s_y[c], 16 * U)
                part = y[:, c * U:(c + 1) * U, :]
                xc = K.x[:, c * U:(c + 1) * U, :]
                step(dve.tensor_tensor(part, part, K.gate[:, c * U:(c + 1) * U].unsqueeze(2).broadcast_to([P, U, D]), ALU.mult))
                dve.tensor_scalar(z[:, 0], part, TOP, LIMIT, ALU.is_gt, ALU.mult)
                dve.tensor_scalar(z[:, 1], part, -TOP, -LIMIT, ALU.is_lt, ALU.mult)
                step(dve.tensor_scalar(mask[:, :, :], part, 0.0, 0.0, ALU.mult, ALU.is_equal))
                step(dve.tensor_tensor(z[:, 2], z[:, 0], z[:, 1], ALU.add))
                step(dve.copy_predicated(z[:, 2], mask[:, :, :], part))
                step(dve.tensor_tensor(xc, xc, z[:, 2], ALU.add))


def project_l1(prog, K, A):
    R = DH1 + 1
    with Stage(prog, "proj1") as st:
        w = st.sbuf("w", [P, 2, H1 * DH1])
        w_att = st.sbuf("w_att", [P, 2, 2 * H1])
        att = K.arena_a[:, 0:2 * H1 * DH1].rearrange("p (a n) -> p a n", a=2)
        tmp = K.arena_a[:, 1024:3072].rearrange("p (k n) -> p k n", k=4)
        row = K.arena_b[:, 0:U * H1 * R].rearrange("p (u n) -> p u n", u=U)
        ps_h = st.psum("ps_h", [P, 4, 512])
        ps_a = st.psum("ps_a", [P, 2, 512])
        s_w, s_wa, s_dve, s_one, s_h, s_a, s_row, s_att = (st.sem(n) for n in ("w", "wa", "dve", "one", "h", "a", "row", "att"))
        s_out = [st.sem(f"out{u}") for u in range(U)]
        s_tab = st.sem("tab")
        block = st.block()

        @block.sync
        def _(sp):
            sp.dma_start(w[:, :, :], A["g1_w1"].rearrange("(k p) n -> p k n", p=P)).then_inc(s_w, 16)
            load_rows(sp, s_w, att[:, 0, :], A["g1_as1"])
            load_rows(sp, s_w, att[:, 1, :], A["g1_ad1"])
            with sp.Fori(0, NT // U) as i:
                for u in range(U):
                    t = i * U + u
                    sp.wait_ge(s_row, t + 1)
                    sp.dma_start(K.table1[bass.ds(t * P, P), :], row[:, u, :]).then_inc(s_out[u], 16)
            sp.wait_ge(s_att, NT)
            sp.dma_start(K.att_table[H1].rearrange("(t p) h -> p t h", p=P), K.att_n[:, :, 0:H1]).then_inc(s_tab, 16)
            sp.wait_ge(s_tab, 16)
            for u in range(U):
                sp.wait_ge(s_out[u], 16 * (NT // U))

        @block.gpsimd
        def _(pool):
            st.clear_stale(pool)
            pool.memset(row.rearrange("p u (h r) -> p (u h) r", r=R)[:, :, DH1:R], 1.0).then_inc(s_one, 1)

        @block.tensor
        def _(pe):
            pe.wait_ge(s_w, 48)
            pe.wait_ge(s_wa, 2)
            for t in range(NT):
                if t >= 4:
                    pe.wait_ge(s_row, t - 3)
                for k in range(2):
                    ins = pe.matmul(ps_h[:, t % 4, :], lhsT=K.xn_t[:, k, t * P:(t + 1) * P], rhs=w[:, k, :], start=(k == 0), stop=(k == 1))
                ins.then_inc(s_h, 1)
                if t >= 2:
                    pe.wait_ge(s_att, t - 1)
                for k in range(2):
                    ins = pe.matmul(ps_a[:, t % 2, 0:2 * H1], lhsT=K.xn_t[:, k, t * P:(t + 1) * P], rhs=w_att[:, k, :], start=(k == 0), stop=(k == 1))
                ins.then_inc(s_a, 1)

        @block.scalar
        def _(act):
            act.wait_ge(s_one, 1)
            for t in range(NT):
                act.wait_ge(s_h, t + 1)
                if t >= U:
                    act.wait_ge(s_out[t % U], 16 * (t // U))
                act.activation(row[:, t % U, :].rearrange("p (h r) -> p h r", r=R)[:, :, 0:DH1],
                               ps_h[:, t % 4, :].rearrange("p (h d) -> p h d", d=DH1), ACT.Copy).then_inc(s_row, 1)

        @block.vector
        def _(dve):
            dve.wait_ge(s_w, 48)
            for a in range(2):
                dve.tensor_tensor(tmp[:, 2 * a:2 * a + 2, :], w[:, :, :], att[:, a, :].unsqueeze(1).broadcast_to([P, 2, H1 * DH1]), ALU.mult).then_inc(s_dve, 1)
            dve.wait_ge(s_dve, 2)
            for a in range(2):
                dve.tensor_reduce(w_att[:, :, a * H1:(a + 1) * H1], tmp[:, 2 * a:2 * a + 2, :].rearrange("p k (h d) -> p k h d", h=H1), AX, ALU.add).then_inc(s_wa, 1)
            for t in range(NT):
                dve.wait_ge(s_a, t + 1)
                dve.tensor_copy(K.att_n[:, t, 0:2 * H1], ps_a[:, t % 2, 0:2 * H1]).then_inc(s_att, 1)


def linear_attention_l1(prog, K, A):
    KD = LH * LD
    with Stage(prog, "mix1") as st:
        a = K.arena_a
        k_t = a[:, 0:N]
        v = a[:, N:N + NT * KD].rearrange("p (t d) -> p t d", t=NT)
        ek = a[:, N + NT * KD:N + 2 * NT * KD].rearrange("p (t d) -> p t d", t=NT)
        w = st.sbuf("w", [P, 2, 2 * KD])
        wqt = st.sbuf("wqt", [P, D])
        wo = st.sbuf("wo", [P, D])
        G = -(-N // 512)
        tops = st.sbuf("tops", [P, G])
        top = st.sbuf("top", [P, 1])
        low = st.sbuf("low", [P, 1])
        ksum = st.sbuf("ksum", [P, 1])
        rsum = st.sbuf("rsum", [P, 1])
        ctx = st.sbuf("ctx", [P, P])
        co = st.sbuf("co", [P, D])
        ps_k = st.psum("ps_k", [P, 2, 512])
        ps_v = st.psum("ps_v", [P, 2, 512])
        ps_e = st.psum("ps_e", [P, 2, 512])
        ps_c = st.psum("ps_c", [P, 2, 512])
        s_w, s_k, s_kt, s_v, s_vs, s_dve, s_low, s_exp, s_e, s_ek, s_c, s_cs, s_o, s_os, s_m, s_ms = (
            st.sem(n) for n in ("w", "k", "kt", "v", "vs", "dve", "low", "exp", "e", "ek", "c", "cs", "o", "os", "m", "ms"))
        block = st.block()

        @block.sync
        def _(sp):
            sp.dma_start(w[:, :, :], A["m1_wkv"].rearrange("(k p) n -> p k n", p=P)).then_inc(s_w, 16)
            sp.dma_start(wqt[:, :], A["m1_wqt"]).then_inc(s_w, 16)
            sp.dma_start(wo[:, :], A["m1_wo"]).then_inc(s_w, 16)

        @block.gpsimd
        def _(pool):
            st.clear_stale(pool)

        def context(pe, t):
            n = P if t < NT - 1 else NLAST
            pe.wait_ge(s_ek, t + 1)
            ins = pe.matmul(ps_c[:, 0, 0:KD], lhsT=v[0:n, t, :], rhs=ek[0:n, t, :], start=(t == 0), stop=(t == NT - 1))
            if t == NT - 1:
                ins.then_inc(s_c, 1)

        @block.tensor
        def _(pe):
            pe.wait_ge(s_w, 48)
            for g in range(G):
                n = min(512, N - g * 512)
                if g >= 2:
                    pe.wait_ge(s_kt, g - 1)
                for k in range(2):
                    ins = pe.matmul(ps_k[:, g % 2, 0:n], lhsT=w[:, k, 0:KD], rhs=K.xn_t[:, k, g * 512:g * 512 + n], start=(k == 0), stop=(k == 1))
                ins.then_inc(s_k, 1)
            for t in range(NT):
                if t >= 2:
                    pe.wait_ge(s_vs, t - 1)
                for k in range(2):
                    ins = pe.matmul(ps_v[:, t % 2, 0:KD], lhsT=K.xn_t[:, k, t * P:(t + 1) * P], rhs=w[:, k, KD:2 * KD], start=(k == 0), stop=(k == 1))
                ins.then_inc(s_v, 1)
            pe.wait_ge(s_exp, 1)
            for t in range(NT):
                n = P if t < NT - 1 else NLAST
                if t >= 2:
                    pe.wait_ge(s_ek, t - 1)
                pe.transpose(ps_e[0:n, t % 2, 0:KD], k_t[:, t * P:t * P + n], K.ident[:, :]).then_inc(s_e, 1)
                if t >= 1:
                    context(pe, t - 1)
            context(pe, NT - 1)
            pe.wait_ge(s_cs, 1)
            pe.matmul(ps_k[:, 0, 0:D], lhsT=ctx[:, :], rhs=wo[:, :], start=True, stop=True).then_inc(s_o, 1)
            pe.wait_ge(s_os, 1)
            for c in range(2):
                ins = pe.matmul(ps_v[:, c, 0:D], lhsT=wqt[:, c * P:(c + 1) * P], rhs=co[:, :], start=True, stop=True)
            ins.then_inc(s_m, 1)

        @block.scalar
        def _(act):
            for t in range(NT):
                act.wait_ge(s_v, t + 1)
                act.activation(v[:, t, :], ps_v[:, t % 2, 0:KD], ACT.Copy).then_inc(s_vs, 1)
            act.wait_ge(s_low, 1)
            act.activation(k_t, k_t, ACT.Exp, bias=low[:, 0:1], accum_out=ksum[:, 0:1]).then_inc(s_exp, 1)
            for t in range(NT):
                n = P if t < NT - 1 else NLAST
                act.wait_ge(s_e, t + 1)
                act.activation(ek[0:n, t, :], ps_e[0:n, t % 2, 0:KD], ACT.Copy).then_inc(s_ek, 1)

        @block.vector
        def _(dve):
            for g in range(G):
                n = min(512, N - g * 512)
                dve.wait_ge(s_k, g + 1)
                dve.tensor_reduce(tops[:, g:g + 1], ps_k[:, g % 2, 0:n], AX, ALU.max)
                dve.tensor_copy(k_t[:, g * 512:g * 512 + n], ps_k[:, g % 2, 0:n]).then_inc(s_kt, 1)
            dve.wait_ge(s_kt, G)
            dve.tensor_reduce(top[:, :], tops[:, :], AX, ALU.max).then_inc(s_dve, 1)
            dve.wait_ge(s_dve, 1)
            dve.tensor_scalar(low[:, :], top[:, :], -1.0, None, ALU.mult).then_inc(s_low, 1)
            dve.memset(ctx[:, :], 0.0).then_inc(s_dve, 1)
            dve.wait_ge(s_exp, 1)
            dve.reciprocal(rsum[:, :], ksum[:, :]).then_inc(s_dve, 1)
            dve.wait_ge(s_dve, 3)
            dve.wait_ge(s_c, 1)
            for h in range(LH):
                b = slice(h * LD, (h + 1) * LD)
                ins = dve.tensor_copy(ctx[b, b], ps_c[b, 0, b])
            ins.then_inc(s_cs, 1)
            dve.wait_ge(s_o, 1)
            dve.tensor_scalar(co[:, :], ps_k[:, 0, 0:D], rsum[:, 0:1], float(LD) ** -0.5, ALU.mult, ALU.mult).then_inc(s_os, 1)
            dve.wait_ge(s_m, 1)
            dve.tensor_copy(K.mix[:, :, :], ps_v[:, :, 0:D]).then_inc(s_ms, 1)
            dve.wait_ge(s_ms, 1)


def self_weights(dve, act_exp, step, K, acc_den, kept, has, H, t):
    own, m, top, f1, f2, u, den = (t[n] for n in ("own", "m", "top", "f1", "f2", "u", "den"))
    shape = [P, NT, H]
    step(dve.tensor_tensor(own, K.att_n[:, :, 0:H], K.att_n[:, :, H:2 * H], ALU.add))
    step(dve.scalar_tensor_tensor(own, own, NEG_SLOPE, own, ALU.mult, ALU.max))
    step(dve.tensor_scalar(u, has, BIG, -BIG, ALU.mult, ALU.add))
    step(dve.tensor_tensor(m, kept, u.unsqueeze(2).broadcast_to(shape), ALU.add))
    step(dve.tensor_tensor(top, m, own, ALU.max))
    dve.tensor_tensor(f1, m, top, ALU.subtract)
    step(dve.tensor_tensor(f2, own, top, ALU.subtract))
    act_exp()
    step(dve.tensor_tensor(den, acc_den, f1, ALU.mult))
    step(dve.tensor_tensor(den, den, f2, ALU.add))
    step(dve.reciprocal(den, den))
    step(dve.tensor_tensor(f1, f1, den, ALU.mult))
    step(dve.tensor_tensor(f2, f2, den, ALU.mult))


def weight_tiles(st, H):
    t = {n: st.sbuf(n, [P, NT, H])[:, :, :] for n in ("own", "m", "top", "f1", "f2", "den")}
    t["u"] = st.sbuf("u", [P, NT])[:, :]
    return t


def middle_l1(prog, K, A):
    R = DH1 + 1
    HW = H1 * DH1
    with Stage(prog, "mid1") as st:
        acc = K.acc1
        w = st.sbuf("w", [P, 4, D + 2])
        att = K.xn[:, 0:2, :]
        tmp = K.xn[:, 2:10, :]
        u1 = K.xn[:, 10:14, :].rearrange("p (u a) d -> p u (a d)", a=2)
        u2 = K.xn[:, 14:18, :].rearrange("p (u a) d -> p u (a d)", a=2)
        g = K.xn[:, 18:22, :].rearrange("p (u a) d -> p u (a d)", a=2)
        b1 = K.xn[:, 22:24, :].rearrange("p a d -> p (a d)")
        g_t = K.al[:, 0:2 * HW].rearrange("p (u k n) -> p u k n", u=2, k=4)
        own = K.al[:, 2 * HW:2 * HW + 2 * H1 * R].rearrange("p (u n) -> p u n", u=2)
        tiles = weight_tiles(st, H1)
        f1, f2 = tiles["f1"], tiles["f2"]
        ps_g = st.psum("ps_g", [P, 2, 512])
        ps_h = st.psum("ps_h", [P, 2, 512])
        s_w, s_dve, s_wa, s_f, s_exp, s_u2, s_u, s_g, s_gt, s_gts, s_h, s_tab, s_att, s_out = (
            st.sem(n) for n in ("w", "dve", "wa", "f", "exp", "u2", "u", "g", "gt", "gts", "h", "tab", "att", "out"))
        s_own = [st.sem(f"own{u}") for u in range(2)]
        s_one, s_weights = st.sem("one"), st.sem("weights")
        h2 = K.tab2
        block = st.block()

        @block.sync
        def _(sp):
            sp.dma_start(w[:, :, 0:D], A["g1_w2"].rearrange("(k p) n -> p k n", p=P)).then_inc(s_w, 16)
            load_rows(sp, s_w, att[:, 0, :], A["g1_as2"])
            load_rows(sp, s_w, att[:, 1, :], A["g1_ad2"])
            load_rows(sp, s_w, b1, A["g1_b1"])
            for t in range(NT):
                if t >= 2:
                    sp.wait_ge(s_u2, t - 1)
                sp.dma_start(own[:, t % 2, :], K.table1[t * P:(t + 1) * P, :]).then_inc(s_own[t % 2], 16)
                if t >= 3:
                    sp.wait_ge(s_tab, t - 2)
                    sp.dma_start(K.table2[(t - 3) * P:(t - 2) * P, :], h2[:, t - 3, :]).then_inc(s_out, 16)
            for t in range(NT - 3, NT):
                sp.wait_ge(s_tab, t + 1)
                sp.dma_start(K.table2[t * P:(t + 1) * P, :], h2[:, t, :]).then_inc(s_out, 16)
            sp.wait_ge(s_att, NT)
            sp.dma_start(K.att_table[1].rearrange("(t p) h -> p t h", p=P), K.att_n[:, :, 0:2]).then_inc(s_out, 16)
            sp.wait_ge(s_out, 16 * (NT + 1))

        @block.gpsimd
        def _(pool):
            st.clear_stale(pool)
            pool.memset(h2[:, :, D:D + 1], 1.0).then_inc(s_one, 1)
            pool.wait_ge(s_weights, 1)
            for t in range(NT):
                pool.wait_ge(s_own[t % 2], 16 * (t // 2 + 1))
                if t >= 2:
                    pool.wait_ge(s_u, t - 1)
                pool.tensor_tensor(u2[:, t % 2, :].rearrange("p (h d) -> p h d", h=H1),
                                   own[:, t % 2, :].rearrange("p (h r) -> p h r", r=R)[:, :, 0:DH1],
                                   f2[:, t, :].unsqueeze(2).broadcast_to([P, H1, DH1]), ALU.mult).then_inc(s_u2, 1)

        @block.tensor
        def _(pe):
            pe.wait_ge(s_wa, 2)

            def down(t):
                pe.wait_ge(s_gts, t + 1)
                if t >= 2:
                    pe.wait_ge(s_att, t - 1)
                for k in range(4):
                    ins = pe.matmul(ps_h[:, t % 2, 0:D + 2], lhsT=g_t[:, t % 2, k, :], rhs=w[:, k, :], start=(k == 0), stop=(k == 3))
                ins.then_inc(s_h, 1)

            for t in range(NT):
                pe.wait_ge(s_g, t + 1)
                if t >= 2:
                    pe.wait_ge(s_gts, t - 1)
                for k in range(4):
                    ins = pe.transpose(ps_g[:, t % 2, k * P:(k + 1) * P], g[:, t % 2, k * P:(k + 1) * P], K.ident[:, :])
                ins.then_inc(s_gt, 1)
                if t >= 1:
                    down(t - 1)
            down(NT - 1)

        @block.scalar
        def _(act):
            act.wait_ge(s_f, 1)
            act.activation(f1, f1, ACT.Exp).then_inc(s_exp, 1)
            act.activation(f2, f2, ACT.Exp).then_inc(s_exp, 1)
            act.wait_ge(s_one, 1)

            def out(t):
                act.wait_ge(s_h, t + 1)
                act.activation(h2[:, t, 0:D], ps_h[:, t % 2, 0:D], ACT.Copy).then_inc(s_tab, 1)
                act.activation(K.att_n[:, t, 0:2], ps_h[:, t % 2, D:D + 2], ACT.Copy).then_inc(s_att, 1)

            for t in range(NT):
                act.wait_ge(s_u, t + 1)
                if t >= 2:
                    act.wait_ge(s_gt, t - 1)
                act.activation(g[:, t % 2, :], u1[:, t % 2, :], ACT.Gelu).then_inc(s_g, 1)
                act.wait_ge(s_gt, t + 1)
                if t >= 2:
                    act.wait_ge(s_h, t - 1)
                act.activation(g_t[:, t % 2, :, :].rearrange("p k n -> p (k n)"), ps_g[:, t % 2, :], ACT.Copy).then_inc(s_gts, 1)
                if t >= 1:
                    out(t - 1)
            out(NT - 1)

        @block.vector
        def _(dve):
            n = [0]

            def step(ins):
                n[0] += 1
                ins.then_inc(s_dve, 1)
                dve.wait_ge(s_dve, n[0])

            def act_exp():
                dve.sem_inc(s_f, 1)
                dve.wait_ge(s_exp, 2)

            ext = acc[:, :, 0, 2 * R:2 * R + H1 + 1]
            for b in range(2):
                step(dve.tensor_copy(tiles["den"][:, :, 2 * b:2 * b + 2], acc[:, :, b, DH1:2 * R:R]))
            self_weights(dve, act_exp, step, K, tiles["den"], ext[:, :, 0:H1], ext[:, :, H1], H1, tiles)
            dve.sem_inc(s_weights, 1)
            dve.wait_ge(s_w, 64)
            for a in range(2):
                step(dve.tensor_tensor(tmp[:, 4 * a:4 * a + 4, :], w[:, :, 0:D], att[:, a, :].unsqueeze(1).broadcast_to([P, 4, D]), ALU.mult))
            for a in range(2):
                dve.tensor_reduce(w[:, :, D + a], tmp[:, 4 * a:4 * a + 4, :], AX, ALU.add).then_inc(s_wa, 1)
            for t in range(NT):
                if t >= 2:
                    dve.wait_ge(s_g, t - 1)
                step(dve.tensor_tensor(u1[:, t % 2, :].rearrange("p (b h d) -> p b h d", b=2, h=2),
                                       acc[:, t, :, 0:2 * R].rearrange("p b (h r) -> p b h r", r=R)[:, :, :, 0:DH1],
                                       f1[:, t, :].rearrange("p (b h) -> p b h", b=2).unsqueeze(3).broadcast_to([P, 2, 2, DH1]), ALU.mult))
                step(dve.tensor_tensor(u1[:, t % 2, :], u1[:, t % 2, :], b1, ALU.add))
                dve.wait_ge(s_u2, t + 1)
                dve.tensor_tensor(u1[:, t % 2, :], u1[:, t % 2, :], u2[:, t % 2, :], ALU.add).then_inc(s_u, 1)


def finish_l1(prog, K, A):
    with Stage(prog, "fin1") as st:
        acc = K.acc2
        tiles = weight_tiles(st, 1)
        f1, f2 = tiles["f1"], tiles["f2"]
        bias = K.xn[:, 0:3, :]
        ps = st.psum("ps", [P, 4, 512])
        s_b, s_dve, s_f, s_exp, s_mm, s_add = (st.sem(n) for n in ("b", "dve", "f", "exp", "mm", "add"))
        block = st.block()

        @block.sync
        def _(sp):
            load_rows(sp, s_b, bias[:, 0, :], A["g1_b2"])
            load_rows(sp, s_b, bias[:, 1, :], A["m1_bo"])

        @block.gpsimd
        def _(pool):
            st.clear_stale(pool)

        @block.tensor
        def _(pe):
            for t in range(NT):
                if t >= 4:
                    pe.wait_ge(s_add, t - 3)
                for k in range(2):
                    ins = pe.matmul(ps[:, t % 4, 0:D], lhsT=K.xn_t[:, k, t * P:(t + 1) * P], rhs=K.mix[:, k, :], start=(k == 0), stop=(k == 1))
                ins.then_inc(s_mm, 1)

        @block.scalar
        def _(act):
            act.wait_ge(s_f, 1)
            act.activation(f1, f1, ACT.Exp).then_inc(s_exp, 1)
            act.activation(f2, f2, ACT.Exp).then_inc(s_exp, 1)

        @block.vector
        def _(dve):
            n = [0]

            def step(ins):
                n[0] += 1
                ins.then_inc(s_dve, 1)
                dve.wait_ge(s_dve, n[0])

            def act_exp():
                dve.sem_inc(s_f, 1)
                dve.wait_ge(s_exp, 2)

            self_weights(dve, act_exp, step, K, acc[:, :, D:D + 1], acc[:, :, D + 1:D + 2], acc[:, :, D + 2], 1, tiles)
            dve.wait_ge(s_b, 32)
            step(dve.tensor_tensor(bias[:, 2, :], bias[:, 0, :], bias[:, 1, :], ALU.add))
            rows, own = acc[:, :, 0:D], K.tab2[:, :, 0:D]
            dve.tensor_tensor(own, own, f2.broadcast_to([P, NT, D]), ALU.mult)
            step(dve.tensor_tensor(rows, rows, f1.broadcast_to([P, NT, D]), ALU.mult))
            step(dve.tensor_tensor(K.x[:, :, :], K.x[:, :, :], bias[:, 2, :].unsqueeze(1).broadcast_to([P, NT, D]), ALU.add))
            step(dve.tensor_tensor(K.x[:, :, :], K.x[:, :, :], rows, ALU.add))
            step(dve.tensor_tensor(K.x[:, :, :], K.x[:, :, :], own, ALU.add))
            for t in range(NT):
                dve.wait_ge(s_mm, t + 1)
                dve.tensor_tensor(K.x[:, t, :], K.x[:, t, :], ps[:, t % 4, 0:D], ALU.add).then_inc(s_add, 1)
            dve.wait_ge(s_add, NT)


def experts_l1(prog, K, A, out):
    C = E1 * F1 // P
    G = -(-NT // 4)
    with Stage(prog, "moe1") as st:
        a, b = K.arena_a, K.arena_b
        w1 = a[:, 0:2 * E1 * F1].rearrange("p (k n) -> p k n", k=2)
        w2 = a[:, 2 * E1 * F1:2 * E1 * F1 + C * D].rearrange("p (c d) -> p c d", c=C)
        hot_t = a[0:E1, 2 * E1 * F1 + C * D:2 * E1 * F1 + C * D + NPAD]
        b1 = st.sbuf("b1", [P, C])
        b2 = st.sbuf("b2", [E1, D])
        rw = st.sbuf("rw", [P, 2, E1])
        rb = st.sbuf("rb", [P, E1])
        code = st.sbuf("code", [P, E1])
        best, pick = st.sbuf("best", [P, NT]), st.sbuf("pick", [P, NT])
        logits = K.al[:, 0:NT * E1].rearrange("p (t e) -> p t e", e=E1)
        tmp = K.al[:, NT * E1:2 * NT * E1].rearrange("p (t e) -> p t e", e=E1)
        hot = K.al[:, 2 * NT * E1:3 * NT * E1].rearrange("p (t e) -> p t e", e=E1)
        shut = a[0:E1, 2 * E1 * F1 + C * D + NPAD:2 * E1 * F1 + C * D + NPAD + NPAD // 2].bitcast(BF16)
        h_t = st.sbuf("h_t", [P, C // 2, 512])
        h_t2 = b[:, 0:C // 2 * 512].rearrange("p (c n) -> p c n", c=C // 2)
        sel = st.sbuf("sel", [E1, C, P], BF16)
        y = K.xn
        ps_l = st.psum("ps_l", [P, 2, 512])
        ps_h = st.psum("ps_h", [P, 3, 512])
        ps_y = st.psum("ps_y", [P, 2, 512])
        s_w, s_r, s_const, s_logits, s_dve, s_hot, s_turn, s_turned, s_h, s_ht, s_y, s_ys, s_out, s_b = (
            st.sem(n) for n in ("w", "r", "const", "logits", "dve", "hot", "turn", "turned", "h", "ht", "y", "ys", "out", "b"))
        block = st.block()

        def hidden(c):
            return h_t[:, c, :] if c < C // 2 else h_t2[:, c - C // 2, :]

        @block.sync
        def _(sp):
            sp.dma_start(rw[:, :, :], A["f1_rwt"].rearrange("(k p) n -> p k n", p=P)).then_inc(s_r, 16)
            load_rows(sp, s_r, rb[:, :], A["f1_rb"])
            sp.dma_start(w1, A["f1_w1"].rearrange("(k p) n -> p k n", p=P)).then_inc(s_w, 16)
            sp.dma_start(w2, A["f1_w2"].rearrange("(c p) d -> p c d", p=P)).then_inc(s_w, 16)
            sp.dma_start(b1[:, :], A["f1_b1"]).then_inc(s_w, 16)
            sp.dma_start(b2[:, :], A["f1_b2"]).then_inc(s_w, 16)
            for t in range(NT):
                n = P if t < NT - 1 else NLAST
                sp.wait_ge(s_ys, t + 1)
                sp.dma_start(out[t * P:t * P + n, :], y[0:n, t, :]).then_inc(s_out, 16)
            sp.wait_ge(s_out, 16 * NT)

        @block.gpsimd
        def _(pool):
            st.clear_stale(pool)
            pool.iota(code[:, :], [[1, E1]], base=E1, channel_multiplier=0, allow_small_or_imprecise_dtypes=True).then_inc(s_const, 1)
            pool.memset(sel[:, :, :], 0.0).then_inc(s_const, 1)
            pool.wait_ge(s_const, 2)
            view = sel[:, :, :].rearrange("k c (m u) -> k c m u", u=F1)
            pool.affine_select(out=view, in_=view, compare_op=ALU.not_equal, fill=1.0, base=0,
                               pattern=[[-(P // F1), C], [-1, P // F1], [0, F1]], channel_multiplier=1).then_inc(s_const, 1)

        @block.tensor
        def _(pe):
            pe.wait_ge(s_r, 32)
            for t in range(NT):
                for k in range(2):
                    ins = pe.matmul(ps_l[:, t // 16, (t % 16) * E1:(t % 16 + 1) * E1], lhsT=K.xn_t[:, k, t * P:(t + 1) * P], rhs=rw[:, k, :], start=(k == 0), stop=(k == 1))
            ins.then_inc(s_logits, 1)
            pe.wait_ge(s_hot, 1)
            for g in range(G):
                if g >= 2:
                    pe.wait_ge(s_turned, g - 1)
                for t in range(4 * g, min(NT, 4 * g + 4)):
                    ins = pe.transpose(ps_l[0:E1, g % 2, (t % 4) * P:(t % 4 + 1) * P], hot[:, t, :], K.ident[:, :])
                ins.then_inc(s_turn, 1)
            pe.wait_ge(s_turned, G)
            pe.wait_ge(s_w, 64)
            pe.wait_ge(s_const, 3)
            for g in range(G):
                t0, t1 = 4 * g, min(NT, 4 * g + 4)
                cols = slice(t0 * P, t1 * P)
                n = (t1 - t0) * P
                for c in range(C):
                    q = g * C + c
                    if q >= 3:
                        pe.wait_ge(s_ht, q - 2)
                    pe.matmul(ps_h[:, q % 3, 0:n], lhsT=sel[:, c, :], rhs=shut[:, cols], start=True, stop=False)
                    for k in range(2):
                        ins = pe.matmul(ps_h[:, q % 3, 0:n], lhsT=w1[:, k, c * P:(c + 1) * P], rhs=K.xn_t[:, k, cols], start=False, stop=(k == 1))
                    ins.then_inc(s_h, 1)
                pe.wait_ge(s_ht, (g + 1) * C)
                for t in range(t0, t1):
                    if t >= 2:
                        pe.wait_ge(s_ys, t - 1)
                    at = slice((t - t0) * P, (t - t0 + 1) * P)
                    pe.matmul(ps_y[:, t % 2, 0:D], lhsT=hot_t[:, t * P:(t + 1) * P], rhs=b2[:, :], start=True, stop=False)
                    for c in range(C):
                        ins = pe.matmul(ps_y[:, t % 2, 0:D], lhsT=hidden(c)[:, at], rhs=w2[:, c, :], start=False, stop=(c == C - 1))
                    ins.then_inc(s_y, 1)

        @block.scalar
        def _(act):
            act.wait_ge(s_w, 64)
            for g in range(G):
                t0, t1 = 4 * g, min(NT, 4 * g + 4)
                n = (t1 - t0) * P
                if g:
                    act.wait_ge(s_y, t0)
                for c in range(C):
                    q = g * C + c
                    act.wait_ge(s_h, q + 1)
                    act.activation(hidden(c)[:, 0:n], ps_h[:, q % 3, 0:n], ACT.Relu, bias=b1[:, c:c + 1]).then_inc(s_ht, 1)

        @block.vector
        def _(dve):
            n = [0]

            def step(ins):
                n[0] += 1
                ins.then_inc(s_dve, 1)
                dve.wait_ge(s_dve, n[0])

            dve.wait_ge(s_r, 32)
            dve.wait_ge(s_const, 3)
            dve.wait_ge(s_logits, 1)
            flat = logits.rearrange("p t e -> p (t e)")
            dve.tensor_copy(flat[:, 0:512], ps_l[:, 0, :])
            step(dve.tensor_copy(flat[:, 512:NT * E1], ps_l[:, 1, 0:NT * E1 - 512]))
            first_best(dve, step, logits, rb[:, :], code[:, :], E1, tmp, best[:, :], hot, pick[:, :])
            dve.sem_inc(s_hot, 1)
            for g in range(G):
                t0, t1 = 4 * g, min(NT, 4 * g + 4)
                dve.wait_ge(s_turn, g + 1)
                dve.tensor_copy(hot_t[:, t0 * P:t1 * P], ps_l[0:E1, g % 2, 0:(t1 - t0) * P])
                dve.tensor_scalar(shut[:, t0 * P:t1 * P], ps_l[0:E1, g % 2, 0:(t1 - t0) * P], -1.0, BIG, ALU.add, ALU.mult).then_inc(s_turned, 1)
            for t in range(NT):
                dve.wait_ge(s_y, t + 1)
                dve.scalar_tensor_tensor(y[:, t, :], ps_y[:, t % 2, 0:D], 0.0, K.x[:, t, :], ALU.max, ALU.add).then_inc(s_ys, 1)


def dump(prog, K, out):
        with Stage(prog, "out") as st:
            s_out = st.sem("out")
            block = st.block()

            @block.sync
            def _(sp):
                sp.dma_start(out[0:(NT - 1) * P, :].rearrange("(t p) d -> p t d", p=P), K.x[:, 0:NT - 1, :]).then_inc(s_out, 16)
                sp.dma_start(out[(NT - 1) * P:N, :], K.x[0:NLAST, NT - 1, :]).then_inc(s_out, 16)
                sp.wait_ge(s_out, 32)


def stages(prog, K, A, out):
    edge_items(prog, K, A["x"], A["src"], A["dst"], A["attr"])
    layer_norm(prog, K, "ln0")
    project_l0(prog, K, A)
    edge_scores(prog, K, "score0", H0, 11, A)
    segment_softmax(prog, K, "soft0", H0, 11)
    aggregate(prog, K, "sum0", H0, H0 * (DH0 + 1), K.table0, K.acc0, H0 * (DH0 + 1))
    finish_l0(prog, K, A)
    layer_norm(prog, K, "ln1")
    route_l0(prog, K, A)
    experts_l0(prog, K, A)
    combine_l0(prog, K)
    layer_norm(prog, K, "ln2")
    linear_attention_l1(prog, K, A)
    project_l1(prog, K, A)
    for H, C, RW, table, acc, width in ((H1, 22, H1 * (DH1 + 1), K.table1, K.acc1.rearrange("p t b c -> p t (b c)"), K.width1),
                                        (1, 110, D + 1, K.table2, K.acc2, D + 3)):
        keep = K.al[:, WS * H:WS * (2 * H + 1)].rearrange("p (s h) -> p s h", h=H + 1)
        edge_scores(prog, K, f"score_h{H}", H, C)
        segment_softmax(prog, K, f"soft_h{H}", H, C, keep)
        aggregate(prog, K, f"sum_h{H}", H, RW, table, acc, width, keep)
        if H == H1:
            middle_l1(prog, K, A)
    finish_l1(prog, K, A)
    layer_norm(prog, K, "ln3")
    experts_l1(prog, K, A, out)


class Keep:
    pass


def build(nc, A, out):
    with ExitStack() as stack:
        prog = Program(nc, stack)
        K = Keep()
        K.x = prog.sbuf("x", [P, NT, D])
        K.xn = prog.sbuf("xn", [P, NT, D])
        K.xn_t = prog.sbuf("xn_t", [P, 2, NPAD])
        K.ident = prog.sbuf("ident", [P, P])
        K.iota_row = prog.sbuf("iota_row", [P, P])
        K.iota_part = prog.sbuf("iota_part", [P, 1])
        K.eps = prog.sbuf("eps", [P, 1])
        K.one = prog.sbuf("one", [P, 1])
        K.src_col = prog.sbuf("src_col", [P, WS], I32)
        K.rel_col = prog.sbuf("rel_col", [P, WS])
        K.last_col = prog.sbuf("last_col", [P, WS])
        K.window = prog.sbuf("window", [P, W], I32)
        K.slots = prog.dram("slots", [E0 * CAP, D])
        K.key_flat = prog.dram("key_flat", [WS * P + 2])
        K.attr_rows = prog.dram("attr_rows", [3, W, EB])
        K.rel_rows = prog.dram("rel_rows", [W, EB], BF16)
        K.pen_prev = prog.dram("pen_prev", [WS * P])
        K.pen_next = prog.dram("pen_next", [WS * P])
        K.att_table = {h: prog.dram(f"att_table_{h}", [NPAD, max(h, 2)]) for h in (H0, H1, 1)}
        K.table0 = prog.dram("table0", [NPAD, H0 * (DH0 + 1)])
        K.arena_a = prog.sbuf("arena_a", [P, NT * 526])
        K.arena_b = prog.sbuf("arena_b", [P, NT * H0 * (DH0 + 1)])
        K.tab0 = K.arena_b[:, :].rearrange("p (t r) -> p t r", t=NT)
        K.acc0 = K.arena_a[:, 0:NT * H0 * (DH0 + 1)].rearrange("p (t r) -> p t r", t=NT)
        K.al = prog.sbuf("al", [P, WS * (2 * H1 + 1)])
        K.slot_to = prog.sbuf("slot_to", [P, NT], I32)
        K.slot_from = prog.sbuf("slot_from", [P, NT], I32)
        K.gate = prog.sbuf("gate", [P, NT])
        K.y_slots = prog.dram("y_slots", [E0 * CAP, D])
        K.table1 = prog.dram("table1", [NPAD, H1 * (DH1 + 1)])
        K.table2 = prog.dram("table2", [NPAD, D + 1])
        K.width1 = 2 * (DH1 + 1) + H1 + 1
        K.acc1 = K.arena_a[:, 0:NT * 2 * K.width1].rearrange("p (t b c) -> p t b c", t=NT, b=2)
        K.acc2 = K.arena_a[:, 0:NT * (D + 3)].rearrange("p (t c) -> p t c", t=NT)
        K.tab2 = K.arena_b[:, 0:NT * (D + 1)].rearrange("p (t c) -> p t c", t=NT)
        K.att_n = prog.sbuf("att_n", [P, NT, 2 * H0])
        K.mix = prog.sbuf("mix", [P, 2, D])
        K.gath = [nc.alloc_semaphore(f"gath{q}") for q in range(4)]
        K.gathered = 0
        stages(prog, K, A, out)


def kernel(**inputs):
    import numpy as _np
    import concourse.bacc as _bacc
    from concourse import mybir as _mybir
    from concourse.bass_utils import run_bass_kernel_spmd as _run

    a = {k: _np.asarray(v) for k, v in inputs.items()}
    slots = NB * EB

    def padded(v, fill):
        return _np.concatenate([v, _np.full((slots - E,) + v.shape[1:], fill, v.dtype)])

    g0, m0, f0, g1, m1, f1 = "L0_gnn_", "L0_mix_", "L0_ffn_", "L1_gnn_", "L1_mix_", "L1_ffn_"
    A = {
        "x": a["x"],
        "src": padded(a["src"], 0).reshape(NB, EB),
        "dst": padded(a["dst"], NPAD + P).reshape(NB, EB),
        "attr": padded(a["edge_attr_3"], 0).reshape(NB, EB, 3).transpose(0, 2, 1).reshape(NB, 3 * EB),
        "g0_wt": a[g0 + "W"].T, "g0_as": a[g0 + "a_src"].reshape(1, -1), "g0_ad": a[g0 + "a_dst"].reshape(1, -1),
        "g0_ewt": a[g0 + "edge_W"].T, "g0_eb": a[g0 + "edge_b"].reshape(1, -1), "g0_b": a[g0 + "bias"].reshape(1, -1),
        "m0_wq": a[m0 + "wq"], "m0_wkt": a[m0 + "wk"].T, "m0_wvt": a[m0 + "wv"].T, "m0_wot": a[m0 + "wo"].T,
        "m0_bo": a[m0 + "bo"].reshape(1, -1),
        "m0_kg": a[m0 + "ln_k_g"].reshape(1, -1), "m0_kb": a[m0 + "ln_k_b"].reshape(1, -1),
        "m0_vg": a[m0 + "ln_v_g"].reshape(1, -1), "m0_vb": a[m0 + "ln_v_b"].reshape(1, -1),
        "f0_gw": a[f0 + "gate_w"], "f0_gb": a[f0 + "gate_b"].reshape(1, -1),
        "f0_w1": a[f0 + "w1"], "f0_b1": a[f0 + "b1"].reshape(E0, F0 // P, P).transpose(2, 0, 1).reshape(P, -1),
        "f0_w2": a[f0 + "w2"], "f0_b2": a[f0 + "b2"].reshape(1, -1),
        "g1_w1": a[g1 + "W1"], "g1_as1": a[g1 + "att_src1"].reshape(1, -1), "g1_ad1": a[g1 + "att_dst1"].reshape(1, -1),
        "g1_b1": a[g1 + "b1"].reshape(1, -1), "g1_w2": a[g1 + "W2"], "g1_as2": a[g1 + "att_src2"].reshape(1, -1),
        "g1_ad2": a[g1 + "att_dst2"].reshape(1, -1), "g1_b2": a[g1 + "b2"].reshape(1, -1),
        "m1_wqt": a[m1 + "W_qkv"][:, 0:LH * LD].T, "m1_wkv": a[m1 + "W_qkv"][:, LH * LD:], "m1_wo": a[m1 + "W_out"],
        "m1_bo": a[m1 + "b_out"].reshape(1, -1),
        "f1_rwt": a[f1 + "router_w"].T, "f1_rb": a[f1 + "router_b"].reshape(1, -1),
        "f1_w1": a[f1 + "W1"].transpose(1, 0, 2).reshape(D, E1 * F1), "f1_b1": a[f1 + "b1"].reshape(E1 * F1 // P, P).T,
        "f1_w2": a[f1 + "W2"].reshape(E1 * F1, D), "f1_b2": a[f1 + "b2"],
    }
    A = {k: _np.ascontiguousarray(v) for k, v in A.items()}
    nc = _bacc.Bacc("TRN2", target_bir_lowering=False, num_devices=1)
    arrays, aps = {}, {}
    for name, v in A.items():
        arrays[f"in_{name}"] = v
        aps[name] = nc.dram_tensor(f"in_{name}", v.shape, _mybir.dt.from_np(v.dtype), kind="ExternalInput").ap()
    out = nc.dram_tensor("out_0", (N, D), _mybir.dt.float32, kind="ExternalOutput").ap()
    build(nc, aps, out)
    r = _run(nc, [arrays], core_ids=[0])
    return r.results[0]["out_0"]
```

```python
from contextlib import ExitStack

import concourse.bass as bass
from concourse import mybir

F32 = mybir.dt.float32
BF16 = mybir.dt.bfloat16
I32 = mybir.dt.int32
ALU = mybir.AluOpType
ACT = mybir.ActivationFunctionType
AX = mybir.AxisListType.X

P = 128
N = 3125
D = 256
E = 50000
NT = -(-N // P)
NLAST = N - (NT - 1) * P
NPAD = NT * P
U = 5
EB = 256
NB = -(-E // EB)
W = NB + NT - 1
SUB = EB // P
WS = W * SUB
WC = 2
WP = W // WC
BIG = 1.0e30
NEG_SLOPE = 0.2
LN_EPS = 1e-5

H0, DH0 = 8, 32
MH, MD = 4, 64
E0, F0 = 8, 1024
CAP = -(-5 * N // (4 * E0))
H1, DH1 = 4, 128
E1, F1 = 32, 64
LH, LD = 4, 32
T1 = (NPAD - E1) // P + E1
ENC_ROWS = 3 * (3 * 3 + 1)
SPLITS0 = 2 * 5 + 7
C0, C1, C2 = 11, 22, 110


class Program:

    def __init__(self, nc, stack):
        self.nc, self.stack, self.used = nc, stack, []

    def sbuf(self, name, shape, dt=F32):
        return self.stack.enter_context(self.nc.sbuf_tensor(name, shape, dt))

    def dram(self, name, shape, dt=F32):
        return self.nc.dram_tensor(name, shape, dt, kind="Internal").ap()


class Stage:
    def __init__(self, prog, name):
        self.prog, self.nc, self.name = prog, prog.nc, name
        self.stack = ExitStack()
        self.sems = []
        self.stale = prog.used

    def sem(self, name):
        s = self.nc.alloc_semaphore(f"{self.name}_{name}")
        self.sems.append(s)
        return s

    def sem_sw(self, name):
        return self.nc.alloc_semaphore(f"{self.name}_{name}")

    def sbuf(self, name, shape, dt=F32):
        return self.stack.enter_context(self.nc.sbuf_tensor(f"{self.name}_{name}", shape, dt))

    def psum(self, name, shape, dt=F32):
        return self.stack.enter_context(self.nc.psum_tensor(f"{self.name}_{name}", shape, dt))

    def block(self):
        return self.stack.enter_context(self.nc.Block())

    def clear_stale(self, pool):
        for s in self.stale:
            pool.sem_clear(s)

    def __enter__(self):
        return self

    def __exit__(self, *exc):
        self.stack.__exit__(*exc)
        for s in self.stale:
            self.nc.release_semaphore(s)
        self.prog.used = self.sems
        return False


def split3(step, out, value, rest):
    dve = step.engine
    step(dve.tensor_copy(out[0], value))
    step(dve.tensor_tensor(rest[0], value, out[0], ALU.subtract))
    step(dve.tensor_copy(out[1], rest[0]))
    step(dve.tensor_tensor(rest[1], rest[0], out[1], ALU.subtract))
    step(dve.tensor_copy(out[2], rest[1]))


class Steps:

    def __init__(self, engine, sem):
        self.engine, self.sem, self.n = engine, sem, 0

    def __call__(self, ins):
        self.n += 1
        ins.then_inc(self.sem, 1)
        self.engine.wait_ge(self.sem, self.n)


def edge_items(prog, K, x, dst):
    with Stage(prog, "items") as st:
        def carve(i):
            rows = K.xn[0:WP, :, :].rearrange("p t d -> p (t d)")[:, i * WC * EB:(i + 1) * WC * EB]
            return rows.rearrange("p (c e) -> p c e", c=WC)

        edges = st.sbuf("edges", [P, NB * EB // P], I32)
        edges_f = st.sbuf("edges_f", [P, NB * EB // P])
        below = st.sbuf("below", [P, NB * EB // P])
        count = st.sbuf("count", [P, NT - 1])
        ones = st.sbuf("ones", [P, P])
        t_step = st.sbuf("t_step", [P, NT - 1])
        key_t = st.sbuf("key_t", [P, NT - 1])
        w_row = st.sbuf("w_row", [P, W])
        w_col = st.sbuf("w_col", [WP, WC])
        w_id = st.sbuf("w_id", [WP, WC])
        passed = K.arena_a[:, 0:W * (NT - 1)].rearrange("p (w t) -> p w t", w=W)
        passed_c = st.sbuf("passed_c", [WP, WC, NT - 1])
        t_f = st.sbuf("t_f", [P, W])
        t_c = st.sbuf("t_c", [WP, WC])
        t_first = st.sbuf("t_first", [WP, WC])
        b_col = st.sbuf("b_col", [WP, WC, 3], I32)
        b_f = st.sbuf("b_f", [WP, WC])
        gsrc = st.sbuf("gsrc", [WP, WC, EB], I32)
        gdst = st.sbuf("gdst", [WP, WC, EB], I32)
        gattr = K.arena_b[0:WP, 0:WC * 3 * EB].rearrange("p (c a e) -> p c a e", c=WC, a=3)
        attr_rest = K.arena_b[0:WP, 1536:3072].rearrange("p (c a e) -> p c a e", c=WC, a=3)
        attr_parts = K.arena_b[0:WP, 3072:3072 + WC * 10 * EB // 2].bitcast(BF16).rearrange("p (c k e) -> p c k e", c=WC, k=10)
        src_f = carve(0)
        dst_f = carve(1)
        rel = carve(2)
        inside = carve(3)
        inside2 = carve(4)
        key = carve(5)
        clip = st.sbuf("clip", [WP, WC, EB], BF16)
        place = st.sbuf("place", [WP, WC, EB], BF16)
        tile = st.sbuf("tile", [P, WS], I32)
        key_prev = carve(6)
        key_next = carve(7)
        first = carve(8)
        last = carve(9)
        pen_p = carve(10)
        pen_n = carve(11)
        guard = st.sbuf("guard", [1, 1])
        zeros = K.arena_a[:, W * (NT - 1):W * (NT - 1) + E0 * CAP * D // P // 4]
        ps_total = st.psum("ps_total", [P, NT - 1])
        ps_turn = st.psum("ps_turn", [P, 4, WP])

        s_const = st.sem("const")
        s_ident = st.sem("ident")
        s_edges = st.sem("edges")
        s_dve = st.sem("dve")
        s_xpad = st.sem("xpad")
        s_x = st.sem("x")
        s_count = st.sem("count")
        s_total = st.sem("total")
        s_gather = st.sem_sw("gather")
        s_rows = st.sem("rows")
        s_key = st.sem("key")
        s_store = st.sem("store")
        s_shift = st.sem("shift")
        s_pen = st.sem("pen")
        s_turn = st.sem("turn")
        s_turned = st.sem("turned")
        s_srcf = st.sem("srcf")
        s_zero = st.sem("zero")
        s_parts = st.sem("parts")
        s_stored = st.sem("stored")
        key_flat = K.key_flat
        block = st.block()

        @block.sync
        def _(sp):
            sp.dma_start(edges[:, :], dst.rearrange("b e -> (b e)").rearrange("(p j) -> p j", p=P)).then_inc(s_edges, 16)
            sp.dma_start(K.x[:, 0:NT - 1, :], x[0:(NT - 1) * P, :].rearrange("(t p) d -> p t d", p=P)).then_inc(s_x, 16)
            sp.wait_ge(s_xpad, 2)
            sp.dma_start(K.x[0:NLAST, NT - 1, :], x[(NT - 1) * P:N, :]).then_inc(s_x, 16)
            sp.wait_ge(s_zero, 1)
            zrows = K.slots.rearrange("s d -> (s d)").rearrange("(q p j) -> q p j", q=4, p=P)
            for q in range(4):
                sp.dma_start(zrows[q], zeros[:, :]).then_inc(s_store, 16)
            sp.dma_start(key_flat[0:1].unsqueeze(0), guard[:, :]).then_inc(s_shift, 16)
            sp.dma_start(key_flat[1 + WS * P:2 + WS * P].unsqueeze(0), guard[:, :]).then_inc(s_shift, 16)
            sp.wait_ge(s_gather, 16 * 5 * WC)
            sp.wait_ge(s_key, 1)
            sp.dma_start(key_flat[1:1 + WS * P].rearrange("(c p e) -> p c e", c=WC, p=WP), key[:, :, :]).then_inc(s_shift, 16)
            sp.wait_ge(s_shift, 48)
            sp.dma_start(key_prev[:, :, :], key_flat[0:WS * P].rearrange("(c p e) -> p c e", c=WC, p=WP)).then_inc(s_rows, 16)
            sp.dma_start(key_next[:, :, :], key_flat[2:2 + WS * P].rearrange("(c p e) -> p c e", c=WC, p=WP)).then_inc(s_rows, 16)
            sp.wait_ge(s_key, 2)
            planes = K.edge_rows.rearrange("g (m a e) -> (g m) a e", m=2, a=2)
            sp.dma_start(planes[:, 0, :].rearrange("(c p) e -> p c e", c=WC), clip[:, :, :]).then_inc(s_store, 16)
            sp.wait_ge(s_key, 3)
            sp.dma_start(planes[:, 1, :].rearrange("(c p) e -> p c e", c=WC), place[:, :, :]).then_inc(s_store, 16)
            sp.wait_ge(s_pen, 2)
            sp.dma_start(K.pen_prev.rearrange("(c p e) -> p c e", c=WC, p=WP), pen_p[:, :, :]).then_inc(s_store, 16)
            sp.dma_start(K.pen_next.rearrange("(c p e) -> p c e", c=WC, p=WP), pen_n[:, :, :]).then_inc(s_store, 16)
            sp.wait_ge(s_store, 16 * 8)
            sp.wait_ge(s_x, 32)

        @block.scalar
        def _(act):
            act.wait_ge(s_parts, 6)
            for k in range(ENC_ROWS // 3):
                act.dma_start(K.attr_parts[k].rearrange("(c p e) -> p c e", c=WC, p=WP), attr_parts[:, :, k, :]).then_inc(s_stored, 16)
            act.wait_ge(s_stored, 16 * (ENC_ROWS // 3))

        @block.gpsimd
        def _(pool):
            st.clear_stale(pool)
            pool.memset(zeros[:, :], 0.0).then_inc(s_zero, 1)
            pool.iota(w_row[:, :], [[EB, W]], base=EB, channel_multiplier=0, allow_small_or_imprecise_dtypes=True).then_inc(s_const, 1)
            pool.iota(w_col[:, :], [[EB * WP, WC]], base=EB, channel_multiplier=EB, allow_small_or_imprecise_dtypes=True).then_inc(s_const, 1)
            pool.iota(w_id[:, :], [[WP, WC]], base=0, channel_multiplier=1, allow_small_or_imprecise_dtypes=True).then_inc(s_const, 1)
            pool.iota(t_step[:, :], [[EB, NT - 1]], base=EB, channel_multiplier=0, allow_small_or_imprecise_dtypes=True).then_inc(s_const, 1)
            pool.iota(K.iota_row[:, :], [[1, P]], base=0, channel_multiplier=0, allow_small_or_imprecise_dtypes=True).then_inc(s_const, 1)
            pool.iota(K.iota_part[:, :], [[0, 1]], base=0, channel_multiplier=1, allow_small_or_imprecise_dtypes=True).then_inc(s_const, 1)
            pool.memset(K.ident[:, :], 0.0).then_inc(s_ident, 1)
            pool.wait_ge(s_ident, 1)
            pool.affine_select(out=K.ident[:, :], in_=K.ident[:, :], compare_op=ALU.not_equal, fill=1.0, base=0,
                               pattern=[[-1, P]], channel_multiplier=1).then_inc(s_ident, 1)
            pool.wait_ge(s_count, 2)
            for c in range(WC):
                at = [bass.IndirectOffsetOnAxis(ap=b_col[:, c, a:a + 1], axis=0) for a in range(3)]
                pool.indirect_dma_start(gdst[:, c, :], None, K.dst_s, at[0]).then_inc(s_gather, 16)
                pool.indirect_dma_start(gsrc[:, c, :], None, K.src_s, at[0]).then_inc(s_gather, 16)
                for a in range(3):
                    pool.indirect_dma_start(gattr[:, c, a, :], None, K.attr_s, at[a]).then_inc(s_gather, 16)
            pool.wait_ge(s_gather, 16 * 5 * WC)

        @block.vector
        def _(dve):
            n = [0]

            def step(ins):
                n[0] += 1
                ins.then_inc(s_dve, 1)
                dve.wait_ge(s_dve, n[0])

            dve.memset(K.x[:, NT - 1, :], 0.0).then_inc(s_xpad, 1)
            dve.memset(guard[:, :], -7.0).then_inc(s_xpad, 1)
            dve.memset(K.eps[:, :], LN_EPS)
            step(dve.memset(ones[:, :], 1.0))
            dve.wait_ge(s_edges, 16)
            step(dve.tensor_copy(edges_f[:, :], edges[:, :]))
            for t in range(NT - 1):
                step(dve.tensor_scalar(below[:, :], edges_f[:, :], float(P * (t + 1)), 0.0, ALU.is_lt, ALU.add,
                                       accum_out=count[:, t:t + 1]))
            dve.sem_inc(s_count, 1)
            dve.wait_ge(s_const, 6)
            dve.wait_ge(s_total, 1)
            step(dve.tensor_tensor(key_t[:, :], ps_total[:, :], t_step[:, :], ALU.add))
            dve.tensor_tensor(passed_c[:, :, :], w_col[:, :].unsqueeze(2).broadcast_to([WP, WC, NT - 1]),
                              key_t[0:WP, :].unsqueeze(1).broadcast_to([WP, WC, NT - 1]), ALU.is_gt)
            step(dve.tensor_tensor(passed[:, :, :], w_row[:, :].unsqueeze(2).broadcast_to([P, W, NT - 1]),
                                   key_t[:, :].unsqueeze(1).broadcast_to([P, W, NT - 1]), ALU.is_gt))
            step(dve.tensor_reduce(t_c[:, :], passed_c[:, :, :], AX, ALU.add))
            step(dve.tensor_tensor(b_f[:, :], w_id[:, :], t_c[:, :], ALU.subtract))
            for a in range(3):
                ins = dve.tensor_scalar(b_col[:, :, a], b_f[:, :], float(a * NB), None, ALU.add)
            ins.then_inc(s_count, 1)
            step(dve.tensor_scalar(t_first[:, :], t_c[:, :], float(P), None, ALU.mult))
            step(dve.tensor_reduce(t_f[:, :], passed[:, :, :], AX, ALU.add))
            step(dve.tensor_copy(K.window[:, :], t_f[:, :]))
            dve.wait_ge(s_gather, 16 * 5 * WC)
            dve.tensor_copy(src_f[:, :, :], gsrc[:, :, :]).then_inc(s_srcf, 1)
            step(dve.tensor_copy(dst_f[:, :, :], gdst[:, :, :]))
            for c in range(WC):
                ins = dve.tensor_scalar(rel[:, c, :], dst_f[:, c, :], t_first[:, c:c + 1], None, ALU.subtract)
            ins.then_inc(s_srcf, 1)
            dve.wait_ge(s_srcf, 2)
            step(dve.tensor_scalar(inside[:, :, :], rel[:, :, :], 0.0, None, ALU.is_ge))
            step(dve.scalar_tensor_tensor(inside2[:, :, :], rel[:, :, :], float(P - 1), inside[:, :, :], ALU.is_le, ALU.mult))
            dve.scalar_tensor_tensor(key[:, :, :], dst_f[:, :, :], 1.0, inside2[:, :, :], ALU.add, ALU.mult).then_inc(s_key, 1)
            dve.tensor_scalar(clip[:, :, :], rel[:, :, :], -1.0, float(P), ALU.max, ALU.min).then_inc(s_key, 1)
            dve.wait_ge(s_key, 1)
            dve.wait_ge(s_rows, 32)
            dve.tensor_tensor(last[:, :, :], key[:, :, :], key_next[:, :, :], ALU.not_equal).then_inc(s_srcf, 1)
            step(dve.tensor_tensor(first[:, :, :], key[:, :, :], key_prev[:, :, :], ALU.not_equal))
            dve.wait_ge(s_srcf, 3)
            dve.tensor_scalar(pen_p[:, :, :], first[:, :, :], -BIG, None, ALU.mult).then_inc(s_pen, 1)
            dve.tensor_scalar(pen_n[:, :, :], last[:, :, :], -BIG, None, ALU.mult).then_inc(s_pen, 1)
            part_step = Steps(dve, s_parts)
            part_step(dve.memset(attr_parts[:, :, 9, :], 1.0))
            split3(part_step, [attr_parts[:, :, 3 * k:3 * k + 3, :] for k in range(3)], gattr, [attr_rest, attr_rest])
            step(dve.tensor_scalar(gdst[:, :, :], gsrc[:, :, :], P - 1, None, ALU.bitwise_and))
            dve.tensor_copy(place[:, :, :], gdst[:, :, :]).then_inc(s_key, 1)
            for r, out in enumerate((K.src_col, K.rel_col, K.last_col)):
                dve.wait_ge(s_turn, r + 1)
                ins = dve.tensor_copy(out[:, :].rearrange("e (c p s) -> e c p s", c=WC, s=SUB),
                                      ps_turn[:, :, :].rearrange("e (c s) p -> e c p s", c=WC)).then_inc(s_turned, 1)
            dve.wait_ge(s_pen, 2)
            dve.wait_ge(s_turned, 1)
            step(dve.tensor_scalar(tile[:, :], K.src_col[:, :], P.bit_length() - 1, None, ALU.logical_shift_right))
            step(dve.tensor_copy(K.hi_col[:, :], tile[:, :]))

        @block.tensor
        def _(pe):
            pe.wait_ge(s_count, 1)
            pe.wait_ge(s_dve, 1)
            pe.matmul(ps_total[:, :], lhsT=ones[:, :], rhs=count[:, :], start=True, stop=True).then_inc(s_total, 1)
            pe.wait_ge(s_ident, 2)
            for r, rows in enumerate((src_f, rel, last)):
                pe.wait_ge(s_srcf, r + 1)
                if r:
                    pe.wait_ge(s_turned, r)
                for c in range(WC):
                    for s in range(SUB):
                        ins = pe.transpose(ps_turn[:, c * SUB + s, :], rows[:, c, s * P:(s + 1) * P], K.ident[0:WP, 0:WP])
                ins.then_inc(s_turn, 1)


def layer_norm(prog, K, name):
    with Stage(prog, name) as st:
        stats = st.sbuf("stats", [P, NT, 6])
        total, gap, within = (st.sbuf(n, [P, NT]) for n in ("total", "gap", "within"))
        mean, gap2, within2, var = (st.sbuf(n, [P, NT]) for n in ("mean", "gap2", "within2", "var"))
        std = st.sbuf("std", [P, NT])
        rstd = st.sbuf("rstd", [P, NT])
        ps = st.psum("ps", [P, U, 4, P])
        s_stats, s_mom, s_std, s_rstd = st.sem("stats"), st.sem("mom"), st.sem("std"), st.sem("rstd")
        s_xn, s_turn, s_free = st.sem("xn"), st.sem("turn"), st.sem("free")
        block = st.block()

        @block.gpsimd
        def _(pool):
            st.clear_stale(pool)

        @block.vector
        def _(dve):
            with dve.Fori(0, NT // U) as i:
                for j in range(U):
                    t = i * U + j
                    dve.bn_stats(stats[:, t, :], K.x[:, t, :]).then_inc(s_stats, 1)
            dve.wait_ge(s_stats, NT)
            dve.tensor_tensor(total[:, :], stats[:, :, 1], stats[:, :, 4], ALU.add).then_inc(s_mom, 1)
            dve.tensor_tensor(gap[:, :], stats[:, :, 1], stats[:, :, 4], ALU.subtract).then_inc(s_mom, 1)
            dve.tensor_tensor(within[:, :], stats[:, :, 2], stats[:, :, 5], ALU.add).then_inc(s_mom, 1)
            dve.wait_ge(s_mom, 3)
            dve.tensor_scalar(mean[:, :], total[:, :], 0.5, None, ALU.mult).then_inc(s_mom, 1)
            dve.tensor_tensor(gap2[:, :], gap[:, :], gap[:, :], ALU.mult).then_inc(s_mom, 1)
            dve.tensor_scalar(within2[:, :], within[:, :], 1.0 / D, None, ALU.mult).then_inc(s_mom, 1)
            dve.wait_ge(s_mom, 6)
            dve.scalar_tensor_tensor(var[:, :], gap2[:, :], 0.25, within2[:, :], ALU.mult, ALU.add).then_inc(s_mom, 1)
            dve.wait_ge(s_std, 1)
            dve.reciprocal(rstd[:, :], std[:, :]).then_inc(s_rstd, 1)
            dve.wait_ge(s_rstd, 1)
            with dve.Fori(0, NT // U) as i:
                for j in range(U):
                    t = i * U + j
                    dve.tensor_scalar(K.xn[:, t, :], K.x[:, t, :], mean[:, bass.ds(t, 1)], rstd[:, bass.ds(t, 1)],
                                      ALU.subtract, ALU.mult).then_inc(s_xn, 1)

        @block.scalar
        def _(act):
            act.wait_ge(s_mom, 7)
            act.activation(std[:, :], var[:, :], ACT.Sqrt, bias=K.eps[:, 0:1]).then_inc(s_std, 1)
            with act.Fori(0, NT // U) as i:
                for j in range(U):
                    t = i * U + j
                    act.wait_ge(s_turn, t + 1)
                    act.activation(K.xn_t[:, :, bass.ds(t * P, P)], ps[:, j, 0:2, :], ACT.Copy).then_inc(s_free, 1)

        @block.tensor
        def _(pe):
            for t in range(NT):
                pe.wait_ge(s_xn, t + 1)
                if t >= U:
                    pe.wait_ge(s_free, t - U + 1)
                pe.transpose(ps[:, t % U, 0, :], K.xn[:, t, 0:P], K.ident[:, :])
                pe.transpose(ps[:, t % U, 1, :], K.xn[:, t, P:D], K.ident[:, :]).then_inc(s_turn, 1)


def order_edges(prog, K, A):
    SLOTS = NB * EB
    L = SLOTS // P
    dst = A["dst"].rearrange("b e -> (b e)")
    with Stage(prog, "order") as st:
        here = K.xn[:, 0:2, :].rearrange("p t d -> p (t d)")[:, 0:L].bitcast(I32)
        after = K.xn[:, 2:4, :].rearrange("p t d -> p (t d)")[:, 0:L].bitcast(I32)
        falls = K.xn[:, 4:6, :].rearrange("p t d -> p (t d)")[:, 0:L]
        fall = st.sbuf("fall", [P, 1])
        flag = st.sbuf("flag", [P, 1], I32)
        ones = st.sbuf("ones", [P, P])
        tri = st.sbuf("tri", [P, P])
        digit_id = st.sbuf("digit_id", [P, P])
        pair = st.sbuf("pair", [P, 2], I32)
        attr = st.sbuf("attr", [P, 3])
        bits = st.sbuf("bits", [P, 1], I32)
        digit = st.sbuf("digit", [P, 1])
        hot = st.sbuf("hot", [P, P])
        count = st.sbuf("count", [P, P])
        upto = st.sbuf("upto", [P, P])
        spread = st.sbuf("spread", [P, P])
        rank_f = st.sbuf("rank_f", [P, 1])
        rank = st.sbuf("rank", [P, 1], I32)
        pairs = K.arena_a[:, 0:2 * L].bitcast(I32).rearrange("p (j a) -> p j a", a=2)
        attrs = K.arena_a[:, 2 * L:5 * L].rearrange("p (j a) -> p j a", a=3)
        planes = K.arena_a[:, 5 * L:10 * L].rearrange("p (a j) -> p a j", a=5)
        ps_f = st.psum("ps_f", [P, 1])
        ps_b = st.psum("ps_b", [P, P])
        ps_n = st.psum("ps_n", [P, P])
        s_in, s_copy, s_dve, s_fall, s_sum, s_flag, s_tri = (st.sem(n) for n in ("in", "copy", "dve", "fall", "sum", "flag", "tri"))
        s_read, s_sent, s_load, s_store = (st.sem_sw(n) for n in ("read", "sent", "load", "store"))
        s_hot, s_mm, s_used, s_rank, s_step, s_split = (st.sem(n) for n in ("hot", "mm", "used", "rank", "step", "split"))
        block = st.block()

        @block.sync
        def _(sp):
            sp.dma_start(here, dst.rearrange("(p j) -> p j", p=P)).then_inc(s_in, 16)
            sp.dma_start(after[0:P - 1, :], dst[1:1 + (P - 1) * L].rearrange("(p j) -> p j", p=P - 1)).then_inc(s_in, 16)
            sp.dma_start(after[P - 1:P, 0:L - 1], dst[1 + (P - 1) * L:SLOTS].rearrange("(p j) -> p j", p=1)).then_inc(s_in, 16)
            sp.dma_start(after[P - 1:P, L - 1:L], dst[SLOTS - 1:SLOTS].rearrange("(p j) -> p j", p=1)).then_inc(s_in, 16)
            sp.dma_start(K.src_s, A["src"]).then_inc(s_copy, 16)
            sp.dma_start(K.dst_s, A["dst"]).then_inc(s_copy, 16)
            sp.dma_start(K.attr_s, A["attr"]).then_inc(s_copy, 16)
            sp.wait_ge(s_copy, 48)

        @block.gpsimd
        def _(pool):
            pool.memset(ones[:, :], 1.0).then_inc(s_tri, 1)
            pool.wait_ge(s_tri, 1)
            pool.affine_select(out=tri[:, :], in_=ones[:, :], compare_op=ALU.is_gt, fill=0.0, base=0,
                               pattern=[[1, P]], channel_multiplier=-1).then_inc(s_tri, 1)
            pool.iota(digit_id[:, :], [[1, P]], base=0, channel_multiplier=0, allow_small_or_imprecise_dtypes=True).then_inc(s_tri, 1)
            pool.wait_ge(s_flag, 1)
            unsorted = pool.value_load(flag[0:1, 0:1], min_val=0, max_val=SLOTS)
            with pool.If(unsorted > 0):
                pool.wait_ge(s_copy, 48)
                for turn, (pi, ai, po, ao) in enumerate(((A["pair"], A["attr_rows"], K.pair_a, K.attr_a),
                                                         (K.pair_a, K.attr_a, K.pair_b, K.attr_b))):
                    with pool.Fori(0, L) as b:
                        pool.wait_ge(s_used, 2 * L * turn + b + 1)
                        pool.nop(nofuse=True)
                        pool.dma_start(pair[:, :], pi[bass.ds(b * P, P), :]).then_inc(s_read, 16)
                    with pool.Fori(0, L) as b:
                        pool.wait_ge(s_used, 2 * L * turn + L + b + 1)
                        pool.nop(nofuse=True)
                        pool.dma_start(pair[:, :], pi[bass.ds(b * P, P), :]).then_inc(s_read, 16)
                        pool.dma_start(attr[:, :], ai[bass.ds(b * P, P), :]).then_inc(s_load, 16)
                        pool.wait_ge(s_rank, L * turn + b + 1)
                        pool.wait_ge(s_load, 16 * (L * turn + b + 1))
                        pool.nop(nofuse=True)
                        at = bass.IndirectOffsetOnAxis(ap=rank[:, 0:1], axis=0)
                        pool.indirect_dma_start(po, at, pair[:, :], None).then_inc(s_sent, 16)
                        pool.indirect_dma_start(ao, at, attr[:, :], None).then_inc(s_sent, 16)
                        pool.wait_ge(s_sent, 32 * (L * turn + b + 1))
                        pool.nop(nofuse=True).then_inc(s_step, 1)
                pool.dma_start(pairs, K.pair_b.rearrange("(p j) a -> p j a", p=P)).then_inc(s_load, 16)
                pool.dma_start(attrs, K.attr_b.rearrange("(p j) a -> p j a", p=P)).then_inc(s_load, 16)
                pool.wait_ge(s_split, 5)
                for a, out in enumerate((K.src_s, K.dst_s)):
                    pool.dma_start(out.rearrange("b e -> (b e)").rearrange("(p j) -> p j", p=P), planes[:, a, :].bitcast(I32)).then_inc(s_store, 16)
                for a in range(3):
                    pool.dma_start(K.attr_s[a * NB:(a + 1) * NB, :].rearrange("b e -> (b e)").rearrange("(p j) -> p j", p=P),
                                   planes[:, 2 + a, :]).then_inc(s_store, 16)
                pool.wait_ge(s_store, 16 * 5)
            pool.nop(nofuse=True)

        @block.tensor
        def _(pe):
            pe.wait_ge(s_tri, 3)
            pe.wait_ge(s_fall, 1)
            pe.matmul(ps_f[:, :], lhsT=ones[:, :], rhs=fall[:, :], start=True, stop=True).then_inc(s_sum, 1)
            pe.wait_ge(s_flag, 1)
            unsorted = pe.value_load(flag[0:1, 0:1], min_val=0, max_val=SLOTS)
            with pe.If(unsorted > 0):
                with pe.Fori(0, 4 * L) as b:
                    pe.wait_ge(s_hot, b + 1)
                    pe.matmul(ps_b[:, :], lhsT=tri[:, :], rhs=hot[:, :], start=True, stop=True)
                    pe.matmul(ps_n[:, :], lhsT=ones[:, :], rhs=hot[:, :], start=True, stop=True).then_inc(s_mm, 1)
            pe.nop(nofuse=True)

        @block.vector
        def _(dve):
            dve.wait_ge(s_in, 64)
            dve.tensor_tensor(falls, here, after, ALU.is_gt).then_inc(s_dve, 1)
            dve.wait_ge(s_dve, 1)
            dve.tensor_reduce(fall[:, :], falls, AX, ALU.add).then_inc(s_fall, 1)
            dve.wait_ge(s_sum, 1)
            dve.tensor_copy(flag[:, :], ps_f[:, :]).then_inc(s_flag, 1)
            dve.wait_ge(s_flag, 1)
            unsorted = dve.value_load(flag[0:1, 0:1], min_val=0, max_val=SLOTS)
            with dve.If(unsorted > 0):
                def one_hot(turn, b, n):
                    dve.wait_ge(s_read, 16 * (n + 1))
                    if turn == 0:
                        dve.tensor_scalar(bits[:, :], pair[:, 1:2], P - 1, None, ALU.bitwise_and).then_inc(s_dve, 1)
                    else:
                        dve.tensor_scalar(bits[:, :], pair[:, 1:2], 7, None, ALU.logical_shift_right).then_inc(s_dve, 1)
                    dve.drain()
                    dve.tensor_copy(digit[:, :], bits[:, :])
                    dve.drain()
                    dve.tensor_scalar(hot[:, :], digit_id[:, :], digit[:, 0:1], None, ALU.is_equal).then_inc(s_hot, 1)
                    dve.wait_ge(s_mm, n + 1)

                dve.sem_inc(s_used, 1)
                for turn in range(2):
                    dve.memset(count[:, :], 0.0)
                    dve.drain()
                    with dve.Fori(0, L) as b:
                        n = 2 * L * turn + b
                        one_hot(turn, b, n)
                        dve.tensor_tensor(count[:, :], count[:, :], ps_n[:, :], ALU.add)
                        dve.drain()
                        dve.nop(nofuse=True).then_inc(s_used, 1)
                    dve.tensor_tensor_scan(upto[:, :], count[:, :], count[:, :], 0.0, ALU.add, ALU.max)
                    dve.drain()
                    dve.tensor_tensor(count[:, :], upto[:, :], count[:, :], ALU.subtract)
                    dve.drain()
                    with dve.Fori(0, L) as b:
                        n = 2 * L * turn + L + b
                        one_hot(turn, b, n)
                        dve.tensor_tensor(spread[:, :], count[:, :], ps_b[:, :], ALU.add)
                        dve.drain()
                        dve.tensor_tensor(spread[:, :], spread[:, :], hot[:, :], ALU.mult)
                        dve.drain()
                        dve.tensor_reduce(rank_f[:, :], spread[:, :], AX, ALU.add)
                        dve.tensor_tensor(count[:, :], count[:, :], ps_n[:, :], ALU.add)
                        dve.drain()
                        dve.tensor_copy(rank[:, :], rank_f[:, :]).then_inc(s_rank, 1)
                        dve.wait_ge(s_step, L * turn + b + 1)
                        dve.nop(nofuse=True).then_inc(s_used, 1)
                dve.wait_ge(s_load, 16 * (2 * L + 2))
                for a in range(2):
                    dve.tensor_copy(planes[:, a, :].bitcast(I32), pairs[:, :, a]).then_inc(s_split, 1)
                for a in range(3):
                    dve.tensor_copy(planes[:, 2 + a, :], attrs[:, :, a]).then_inc(s_split, 1)
                dve.wait_ge(s_split, 5)
            dve.nop(nofuse=True)


def load_rows(sp, sem, dst, rows):
    return sp.dma_start(dst, rows.partition_broadcast(P).rearrange("p a d -> p (a d)")).then_inc(sem, 16)


def project_l0(prog, K, A):
    R = DH0 + 1
    with Stage(prog, "proj0") as st:
        kv = K.arena_a[:, 0:NT * 2 * D].rearrange("p (t d) -> p t d", t=NT)
        w = st.sbuf("w", [P, 2, D + 2 * H0])
        wkv = st.sbuf("wkv", [P, 2, 2 * D])
        wot = st.sbuf("wot", [P, 2, D])
        wq = st.sbuf("wq", [P, 2, D])
        att = st.sbuf("att", [P, 2, D])
        att_w = K.xn[:, 10:12, :]
        att_w2 = K.xn[:, 12:14, :]
        gain = st.sbuf("gain", [P, 2, 64])
        shift = st.sbuf("shift", [P, 2, 64])
        groups = U * 2 * MH
        gsum = st.sbuf("gsum", [P, groups])
        gmean = st.sbuf("gmean", [P, groups])
        gsq = st.sbuf("gsq", [P, groups])
        gstd = st.sbuf("gstd", [P, groups])
        grstd = st.sbuf("grstd", [P, groups])
        square = K.xn[:, 0:2 * U, :].rearrange("p (t a) d -> p t (a d)", a=2)
        kv_t = st.sbuf("kv_t", [P, 2, P])
        kvo = st.sbuf("kvo", [P, 2, D])
        ps_h = st.psum("ps_h", [P, 2, 512])
        ps_kv = st.psum("ps_kv", [P, 2, 512])
        ps_c = st.psum("ps_c", [P, 2, 512])
        ps_m = st.psum("ps_m", [P, 2, 512])
        s_w, s_wa, s_h, s_kv = st.sem("w"), st.sem("wa"), st.sem("h"), st.sem("kv")
        s_hout, s_adout, s_kvout, s_table = st.sem("hout"), st.sem("adout"), st.sem("kvout"), st.sem("table")
        s_dve, s_cen, s_sq, s_var, s_std, s_norm, s_gain, s_shift = (
            st.sem(n) for n in ("dve", "cen", "sq", "var", "std", "norm", "gain", "shift"))
        s_c, s_bd, s_kvo, s_kvos, s_m, s_ones = (st.sem(n) for n in ("c", "bd", "kvo", "kvos", "m", "ones"))
        block = st.block()

        @block.sync
        def _(sp):
            sp.dma_start(w[:, :, 0:D], A["g0_wt"].rearrange("(k p) n -> p k n", p=P)).then_inc(s_w, 16)
            load_rows(sp, s_w, att[:, 0, :], A["g0_as"])
            load_rows(sp, s_w, att[:, 1, :], A["g0_ad"])
            sp.dma_start(wkv[:, :, 0:D], A["m0_wkt"].rearrange("(k p) n -> p k n", p=P)).then_inc(s_w, 16)
            sp.dma_start(wkv[:, :, D:2 * D], A["m0_wvt"].rearrange("(k p) n -> p k n", p=P)).then_inc(s_w, 16)
            sp.dma_start(wot[:, :, :], A["m0_wot"].rearrange("(k p) n -> p k n", p=P)).then_inc(s_w, 16)
            sp.dma_start(wq[:, :, :], A["m0_wq"].rearrange("(k p) n -> p k n", p=P)).then_inc(s_w, 16)
            load_rows(sp, s_w, gain[:, 0, :], A["m0_kg"])
            load_rows(sp, s_w, gain[:, 1, :], A["m0_vg"])
            load_rows(sp, s_w, shift[:, 0, :], A["m0_kb"])
            load_rows(sp, s_w, shift[:, 1, :], A["m0_vb"])
            sp.wait_ge(s_ones, 1)
            with sp.Fori(0, NT) as t:
                sp.wait_ge(s_hout, t + 1)
                sp.dma_start(K.table0[bass.ds(t * P, P), :], K.tab0[:, t, :]).then_inc(s_table, 16)
            sp.wait_ge(s_adout, NT)
            sp.dma_start(K.att_table.rearrange("(t p) h -> p t h", p=P), K.att_n[:, :, 0:H0]).then_inc(s_table, 16)
            sp.wait_ge(s_table, 16 * (NT + 1))

        @block.gpsimd
        def _(pool):
            st.clear_stale(pool)
            pool.memset(K.tab0[:, :, :].rearrange("p t (h r) -> p (t h) r", r=R)[:, :, DH0:R], 1.0).then_inc(s_ones, 1)
            pool.wait_ge(s_w, 16 * 11)
            for c in range(NT // U):
                view = kv[:, c * U:(c + 1) * U, :].rearrange("p t (a h d) -> p t a h d", a=2, h=MH)
                pool.wait_ge(s_norm, c + 1)
                for t in range(U):
                    ins = pool.tensor_tensor(view[:, t], view[:, t], gain[:, :, :].unsqueeze(2).broadcast_to([P, 2, MH, MD]), ALU.mult)
                ins.then_inc(s_gain, 1)
                pool.wait_ge(s_gain, c + 1)
                for t in range(U):
                    ins = pool.tensor_tensor(view[:, t], view[:, t], shift[:, :, :].unsqueeze(2).broadcast_to([P, 2, MH, MD]), ALU.add)
                ins.then_inc(s_shift, 1)

        @block.tensor
        def _(pe):
            pe.wait_ge(s_w, 16 * 11)
            pe.wait_ge(s_wa, 2)
            for t in range(NT):
                if t >= 2:
                    pe.wait_ge(s_adout, t - 1)
                    pe.wait_ge(s_kvout, t - 1)
                for k in range(2):
                    ins = pe.matmul(ps_h[:, t % 2, 0:D + 2 * H0], lhsT=K.xn_t[:, k, t * P:(t + 1) * P], rhs=w[:, k, :],
                                    start=(k == 0), stop=(k == 1))
                ins.then_inc(s_h, 1)
                for k in range(2):
                    ins = pe.matmul(ps_kv[:, t % 2, :], lhsT=K.xn_t[:, k, t * P:(t + 1) * P], rhs=wkv[:, k, :],
                                    start=(k == 0), stop=(k == 1))
                ins.then_inc(s_kv, 1)
            for t in range(NT):
                if t % U == 0:
                    pe.wait_ge(s_shift, t // U + 1)
                rows = P if t < NT - 1 else NLAST
                for c in range(2):
                    ins = pe.matmul(ps_c[:, c, 0:P], lhsT=kv[0:rows, t, D + c * P:D + (c + 1) * P],
                                    rhs=kv[0:rows, t, c * P:(c + 1) * P], start=(t == 0), stop=(t == NT - 1))
            ins.then_inc(s_c, 1)
            pe.wait_ge(s_bd, 1)
            for c in range(2):
                ins = pe.matmul(ps_m[:, c, 0:D], lhsT=kv_t[:, c, :], rhs=wot[:, c, :], start=True, stop=True)
            ins.then_inc(s_kvo, 1)
            pe.wait_ge(s_kvos, 1)
            for c in range(2):
                for k in range(2):
                    ins = pe.matmul(ps_c[:, c, 0:D], lhsT=wq[:, k, c * P:(c + 1) * P], rhs=kvo[:, k, :],
                                    start=(k == 0), stop=(k == 1))
            ins.then_inc(s_m, 1)

        @block.scalar
        def _(act):
            def tile_out(t):
                act.wait_ge(s_h, t + 1)
                act.activation(K.tab0[:, t, :].rearrange("p (h r) -> p h r", r=R)[:, :, 0:DH0],
                               ps_h[:, t % 2, 0:D].rearrange("p (h d) -> p h d", d=DH0), ACT.Copy).then_inc(s_hout, 1)
                act.activation(K.att_n[:, t, :], ps_h[:, t % 2, D:D + 2 * H0], ACT.Copy).then_inc(s_adout, 1)
                act.wait_ge(s_kv, t + 1)
                act.activation(kv[:, t, :], ps_kv[:, t % 2, :], ACT.Copy).then_inc(s_kvout, 1)

            for t in range(U):
                tile_out(t)
            for c in range(NT // U):
                for t in range((c + 1) * U, min(NT, (c + 2) * U)):
                    tile_out(t)
                act.wait_ge(s_cen, c + 1)
                act.activation(square[:, :, :], kv[:, c * U:(c + 1) * U, :], ACT.Square).then_inc(s_sq, 1)
                act.wait_ge(s_var, c + 1)
                act.activation(gstd[:, :], gsq[:, :], ACT.Sqrt, scale=1.0 / MD, bias=K.eps[:, 0:1]).then_inc(s_std, 1)

        @block.vector
        def _(dve):
            n = [0]

            def step(ins):
                n[0] += 1
                ins.then_inc(s_dve, 1)
                dve.wait_ge(s_dve, n[0])

            dve.wait_ge(s_w, 16 * 11)
            for a, tmp in ((0, att_w), (1, att_w2)):
                step(dve.tensor_tensor(tmp[:, :, :], w[:, :, 0:D], att[:, a, :].unsqueeze(1).broadcast_to([P, 2, D]), ALU.mult))
                dve.tensor_reduce(w[:, :, D + a * H0:D + (a + 1) * H0], tmp[:, :, :].rearrange("p k (h d) -> p k h d", h=H0),
                                  AX, ALU.add).then_inc(s_wa, 1)
            for c in range(NT // U):
                part = kv[:, c * U:(c + 1) * U, :].rearrange("p t (g d) -> p (t g) d", d=MD)
                dve.wait_ge(s_kvout, (c + 1) * U)
                step(dve.tensor_reduce(gsum[:, :], part, AX, ALU.add))
                step(dve.tensor_scalar(gmean[:, :], gsum[:, :], 1.0 / MD, None, ALU.mult))
                dve.tensor_tensor(part, part, gmean[:, :].unsqueeze(2).broadcast_to([P, groups, MD]), ALU.subtract).then_inc(s_cen, 1)
                dve.wait_ge(s_sq, c + 1)
                dve.tensor_reduce(gsq[:, :], square[:, :, :].rearrange("p t (g d) -> p (t g) d", d=MD), AX, ALU.add).then_inc(s_var, 1)
                dve.wait_ge(s_std, c + 1)
                step(dve.reciprocal(grstd[:, :], gstd[:, :]))
                dve.tensor_tensor(part, part, grstd[:, :].unsqueeze(2).broadcast_to([P, groups, MD]), ALU.mult).then_inc(s_norm, 1)
            step(dve.memset(kv_t[:, :, :], 0.0))
            dve.wait_ge(s_c, 1)
            for h in range(2):
                ins = dve.tensor_scalar(kv_t[h * MD:(h + 1) * MD, :, h * MD:(h + 1) * MD],
                                        ps_c[h * MD:(h + 1) * MD, :, h * MD:(h + 1) * MD], 1.0 / N, None, ALU.mult)
            ins.then_inc(s_bd, 1)
            dve.wait_ge(s_kvo, 1)
            dve.tensor_copy(kvo[:, :, :], ps_m[:, :, 0:D]).then_inc(s_kvos, 1)
            dve.wait_ge(s_m, 1)
            dve.tensor_copy(K.mix[:, :, :], ps_c[:, :, 0:D]).then_inc(s_kvos, 1)
            dve.wait_ge(s_kvos, 2)


def edge_scores_l0(prog, K, A):
    H, C = H0, C0
    with Stage(prog, "score0") as st:
        G, Q, U2 = 2, 5, 2
        GS = G * SUB
        R = ENC_ROWS
        al = K.al[:, 0:WS * H].rearrange("p (s h) -> p s h", h=H)
        near = K.arena_a[:, 0:NT * 3 * (D + H) // 2].bitcast(BF16).rearrange("p (t c d) -> p t c d", t=NT, c=3)
        flat = K.xn[:, :, :].rearrange("p t d -> p (t d)")
        al2 = flat[:, 0:WS * H].rearrange("p (s h) -> p s h", h=H)
        enc = flat[:, WS * H:WS * H + U2 * SUB * D].rearrange("p (u n) -> p u n", u=U2)
        prod = flat[:, WS * H + U2 * SUB * D:WS * H + 2 * U2 * SUB * D].rearrange("p (u n) -> p u n", u=U2)
        rel = st.sbuf("rel", [P, Q, G * EB], BF16)
        hot = st.sbuf("hot", [P, Q, G * EB], BF16)
        attr = st.sbuf("attr", [R, Q, G * EB], BF16)
        enc_w = st.sbuf("enc_w", [R, D])
        enc_rest = st.sbuf("enc_rest", [R, 2, D])
        enc_parts = st.sbuf("enc_parts", [R, 3, D], BF16)
        enc_rows = st.sbuf("enc_rows", [R, D], BF16)
        part_is = st.sbuf("part_is", [R, 3])
        asg = st.sbuf("asg", [P, Q, GS, H])
        idx = st.sbuf("idx", [P, Q, GS], I32)
        rest = st.sbuf("rest", [P, 2, NT, H])
        ps_en = st.psum("ps_en", [P, U2, 512])
        ps_hd = st.psum("ps_hd", [P, U2, SUB, 512])
        s_load = [st.sem(f"load{q}") for q in range(Q)]
        s_gath, gathered = K.gath, list(K.gathered)
        s_hot, s_al, s_fin, s_idx, s_terms, s_encw, s_en, s_hd, s_enc, s_prod, s_red = (
            st.sem(n) for n in ("hot", "al", "fin", "idx", "terms", "encw", "en", "hd", "enc", "prod", "red"))
        s_round, s_rest = st.sem("round"), st.sem("rest")
        h = K.tab0[:, :, :].rearrange("p t (h r) -> p t h r", h=H)[:, :, :, 0:DH0]
        by_head = [near[:, :, c, 0:D].rearrange("p t (h d) -> p t h d", h=H) for c in range(3)]
        h_rest = flat[:, 0:NT * D].rearrange("p (t h d) -> p t h d", t=NT, h=H)
        turns = W // (G * Q)
        block = st.block()

        @block.sync
        def _(sp):
            sp.dma_start(enc_w[:, :], A["g0_enc"]).then_inc(s_encw, 16)
            with sp.Fori(0, turns) as i:
                for q in range(Q):
                    g = i * Q + q
                    sp.wait_ge(s_hot, g + 1)
                    planes = K.edge_rows[bass.ds(g, 1), :].rearrange("g (m a e) -> g m a e", m=G, a=2)[:, :, 0, :]
                    sp.dma_start(rel[:, q, :].rearrange("p (m e) -> p m e", m=G),
                                 planes.partition_broadcast(P).rearrange("p g m e -> p (g m) e")).then_inc(s_load[q], 16)

        @block.gpsimd
        def _(pool):
            st.clear_stale(pool)
            with pool.Fori(0, turns) as i:
                for q in range(Q):
                    pool.wait_ge(s_idx, i * Q + q + 1)
                    pool.nop(nofuse=True)
                    for k in range(GS):
                        pool.indirect_dma_start(asg[:, q, k, :], None, K.att_table[:, :],
                                                bass.IndirectOffsetOnAxis(ap=idx[:, q, k:k + 1], axis=0)).then_inc(s_gath[q], 16)

        @block.tensor
        def _(pe):
            pe.sem_inc(s_hd, G * Q)
            pe.wait_ge(s_terms, SPLITS0)
            pe.wait_ge(s_round, 3 * (NT // U))
            with pe.Fori(0, turns) as i:
                for q in range(Q):
                    g = i * Q + q
                    pe.wait_ge(s_load[q], 32 * (i + 1))
                    pe.wait_ge(s_hot, g + 1 + Q)
                    for m in range(G):
                        w = g * G + m
                        window = pe.value_load(K.window[0:1, bass.ds(w, 1)], min_val=0, max_val=NT - 1)
                        edges = [slice(m * EB + s * P, m * EB + (s + 1) * P) for s in range(SUB)]
                        pe.wait_ge(s_enc, w + 1)
                        for s in range(SUB):
                            ins = pe.matmul(ps_en[:, m, s * D:(s + 1) * D], lhsT=attr[:, q, edges[s]], rhs=enc_rows[:, :], start=True, stop=True)
                        ins.then_inc(s_en, 1)
                        pe.wait_ge(s_prod, w + 1)
                        pe.wait_ge(s_al, w + G * Q - 1)
                        for s in range(SUB):
                            for c in range(3):
                                ins = pe.matmul(ps_hd[:, m, s, 0:D + H], lhsT=hot[:, q, edges[s]],
                                                rhs=near[:, window, c, :], start=(c == 0), stop=(c == 2))
                        ins.then_inc(s_hd, 1)

        @block.scalar
        def _(act):
            def sources(i, q):
                g = i * Q + q
                act.wait_ge(s_al, G * g + G)
                act.activation(idx[:, q, :], K.src_col[:, bass.ds(g * GS, GS)], ACT.Copy).then_inc(s_idx, 1)

            def load_attributes(i, q):
                g = i * Q + q
                act.wait_ge(s_hd, G * g + G)
                act.dma_start(attr[:, q, :], bass.AP(tensor=K.attr_parts.tensor, offset=g * (G * EB), ap=[[0, 3], [W * EB, R // 3], [1, G * EB]])).then_inc(s_load[q], 16)

            def encode(i, q):
                for m in range(G):
                    w = (i * Q + q) * G + m
                    act.wait_ge(s_en, w + 1)
                    act.wait_ge(s_prod, w + 1)
                    act.activation(enc[:, m, :], ps_en[:, m, :], ACT.Relu).then_inc(s_enc, 1)

            act.sem_inc(s_enc, U2)
            for q in range(3):
                sources(0, q)
                load_attributes(0, q)
            for c in range(3):
                for u in range(NT // U):
                    if c:
                        act.wait_ge(s_rest, (c - 1) * (NT // U) + u + 1)
                    t = slice(u * U, (u + 1) * U)
                    act.activation(by_head[c][:, t], (h_rest if c else h)[:, t], ACT.Copy).then_inc(s_round, 1)

            def turn(i, tail=False):
                for q in range(Q):
                    if q + 3 < Q:
                        sources(i, q + 3)
                        load_attributes(i, q + 3)
                    elif not tail:
                        sources(i + 1, q + 3 - Q)
                        load_attributes(i + 1, q + 3 - Q)
                    encode(i, q)

            with act.Fori(0, turns - 1) as i:
                turn(i)
            turn(turns - 1, tail=True)

        @block.vector
        def _(dve):
            def one_hot(i, q):
                g = i * Q + q
                dve.wait_ge(s_load[q], 32 * (i + 1))
                dve.wait_ge(s_hd, G * g + G)
                dve.tensor_scalar(hot[:, q, :], rel[:, q, :], K.iota_part[:, 0:1], None, ALU.is_equal).then_inc(s_hot, 1)

            def scores(i, q, m):
                w = (i * Q + q) * G + m
                dve.wait_ge(s_hd, w + 1 + G * Q)
                dve.wait_ge(s_enc, w + 1 + U2)
                dve.wait_ge(s_red, w + 1)
                dve.tensor_tensor(prod[:, m, :].rearrange("p (s d) -> p s d", s=SUB), enc[:, m, :].rearrange("p (s d) -> p s d", s=SUB),
                                  ps_hd[:, m, :, 0:D], ALU.mult).then_inc(s_prod, 1)
                dve.wait_ge(s_gath[q], gathered[q] + 16 * GS * (i + 1))
                dve.tensor_tensor(al2[:, bass.ds(w * SUB, SUB), :], ps_hd[:, m, :, D:D + H],
                                  asg[:, q, m * SUB:(m + 1) * SUB, :], ALU.add).then_inc(s_al, 1)
                dve.wait_ge(s_prod, w + 1 + U2)
                dve.tensor_reduce(al[:, bass.ds(w * SUB, SUB), :], prod[:, m, :].rearrange("p (s h d) -> p s h d", s=SUB, d=DH0),
                                  AX, ALU.add).then_inc(s_red, 1)

            def turn(i, tail=False):
                for q in range(Q):
                    if q + 2 < Q:
                        one_hot(i, q + 2)
                    elif not tail:
                        one_hot(i + 1, q + 2 - Q)
                    for m in range(G):
                        scores(i, q, m)

            dve.sem_inc(s_hot, Q)
            dve.sem_inc(s_al, G * Q)
            dve.sem_inc(s_prod, U2)
            dve.sem_inc(s_red, U2)
            step = Steps(dve, s_terms)
            for c in range(2):
                for u in range(NT // U):
                    dve.wait_ge(s_round, c * (NT // U) + u + 1)
                    t = slice(u * U, (u + 1) * U)
                    dve.tensor_tensor(h_rest[:, t], (h_rest if c else h)[:, t], by_head[c][:, t], ALU.subtract).then_inc(s_rest, 1)
            split3(step, [near[:, :, c, D:D + H] for c in range(3)], K.att_n[:, :, H:2 * H], [rest[:, r, :, :] for r in range(2)])
            dve.wait_ge(s_encw, 16)
            split3(step, [enc_parts[:, c, :] for c in range(3)], enc_w[:, :], [enc_rest[:, r, :] for r in range(2)])
            step(dve.tensor_scalar(part_is[:, 0:1], K.iota_part[0:R, :], float(R // 3), None, ALU.is_lt))
            step(dve.tensor_scalar(part_is[:, 2:3], K.iota_part[0:R, :], float(2 * R // 3), None, ALU.is_ge))
            step(dve.tensor_tensor(part_is[:, 1:2], part_is[:, 0:1], part_is[:, 2:3], ALU.add))
            step(dve.tensor_scalar(part_is[:, 1:2], part_is[:, 1:2], -1.0, 1.0, ALU.mult, ALU.add))
            step(dve.tensor_scalar(enc_rows[:, :], enc_parts[:, 0, :], part_is[:, 0:1], None, ALU.mult))
            for c in (1, 2):
                step(dve.scalar_tensor_tensor(enc_rows[:, :], enc_parts[:, c, :], part_is[:, c:c + 1], enc_rows[:, :], ALU.mult, ALU.add))
            assert step.n == SPLITS0
            one_hot(0, 0)
            one_hot(0, 1)
            with dve.Fori(0, turns - 1) as i:
                turn(i)
            turn(turns - 1, tail=True)
            dve.wait_ge(s_al, W + G * Q)
            dve.wait_ge(s_red, W + U2)
            dve.tensor_tensor(al[:, :, :], al[:, :, :], al2[:, :, :], ALU.add).then_inc(s_fin, 1)
            dve.wait_ge(s_fin, 1)
            turned = flat[:, 0:WS * H].rearrange("p (j c h) -> p j c h", c=C, h=H)
            view = al.rearrange("p (c j) h -> p j c h", c=C)
            for c in range(C):
                ins = dve.scalar_tensor_tensor(turned[:, :, c, :], view[:, :, c, :], NEG_SLOPE, view[:, :, c, :], ALU.mult, ALU.max)
            ins.then_inc(s_fin, 1)
            dve.wait_ge(s_fin, 2)

        K.gathered = [n + 16 * GS * turns for n in K.gathered]




def edge_scores_l1(prog, K, name, H, C):
    with Stage(prog, name) as st:
        G, Q = 2, 5
        GS = G * SUB
        al = K.al[:, 0:WS * H].rearrange("p (s h) -> p s h", h=H)
        rows = st.sbuf("rows", [P, Q, G * 2 * EB], BF16)
        hot = st.sbuf("hot", [P, Q, G, 2, EB], BF16)
        pick = st.sbuf("pick", [P, Q, GS, NT], BF16)
        free = K.xn[:, :, :].rearrange("p t d -> p (t d)")[:, WS * H1:]
        prod = free[:, 0:Q * GS * H * NT].rearrange("p (q k n) -> p q k n", q=Q, k=GS)
        red = st.sbuf("red", [P, Q, GS * H])
        src_terms = st.sbuf("src_terms", [P, 3, H, NT], BF16)
        dst_terms = st.sbuf("dst_terms", [P, NT, 3, H], BF16)
        near = st.sbuf("near", [P, Q, G, 3, H], BF16)
        rest = st.sbuf("rest", [P, 2, H, NT])
        ps = st.psum("ps", [P, Q, 512])
        first = GS * H * NT
        s_load = [st.sem(f"load{q}") for q in range(Q)]
        s_near0, s_near1 = st.sem("near0"), st.sem("near1")
        s_terms, s_hot, s_pick, s_mm, s_prod, s_red, s_al, s_fin = (
            st.sem(n) for n in ("terms", "hot", "pick", "mm", "prod", "red", "al", "fin"))
        turns = W // (G * Q)
        block = st.block()

        @block.sync
        def _(sp):
            with sp.Fori(0, turns) as i:
                for q in range(Q):
                    g = i * Q + q
                    sp.wait_ge(s_hot, g + 1)
                    sp.dma_start(rows[:, q, :], K.edge_rows[bass.ds(g, 1), :].partition_broadcast(P).rearrange("p a e -> p (a e)")).then_inc(s_load[q], 16)

        @block.scalar
        def _(act):
            act.wait_ge(s_terms, 10)
            with act.Fori(0, turns) as i:
                for q in range(Q):
                    g = i * Q + q
                    window = act.value_load(K.window[0:1, bass.ds(g * G, 1)], min_val=0, max_val=NT - 1)
                    act.wait_ge(s_mm, g + 1)
                    act.activation(near[:, q, 0, :, :], dst_terms[:, window, :, :], ACT.Copy).then_inc(s_near0, 1)

        @block.gpsimd
        def _(pool):
            st.clear_stale(pool)
            pool.wait_ge(s_terms, 10)
            with pool.Fori(0, turns) as i:
                for q in range(Q):
                    g = i * Q + q
                    window = pool.value_load(K.window[0:1, bass.ds(g * G + 1, 1)], min_val=0, max_val=NT - 1)
                    pool.wait_ge(s_mm, g + 1)
                    pool.nop(nofuse=True)
                    pool.tensor_copy(near[:, q, 1, :, :], dst_terms[:, window, :, :]).then_inc(s_near1, 1)

        @block.tensor
        def _(pe):
            pe.sem_inc(s_mm, Q)
            pe.wait_ge(s_terms, 10)
            with pe.Fori(0, turns) as i:
                for q in range(Q):
                    g = i * Q + q
                    pe.wait_ge(s_hot, g + 1 + Q)
                    pe.wait_ge(s_al, g + 1)
                    pe.wait_ge(s_near0, g + 1)
                    pe.wait_ge(s_near1, g + 1)
                    for m in range(G):
                        for s in range(SUB):
                            k = m * SUB + s
                            for c in range(3):
                                pe.matmul(ps[:, q, k * H * NT:(k + 1) * H * NT], lhsT=hot[:, q, m, 1, s * P:(s + 1) * P],
                                          rhs=src_terms[:, c, :, :].rearrange("p h t -> p (h t)"), start=(c == 0), stop=(c == 2))
                            for c in range(3):
                                ins = pe.matmul(ps[:, q, first + k * H:first + (k + 1) * H], lhsT=hot[:, q, m, 0, s * P:(s + 1) * P],
                                                rhs=near[:, q, m, c, :], start=(c == 0), stop=(c == 2))
                    ins.then_inc(s_mm, 1)

        @block.vector
        def _(dve):
            def one_hot(i, q):
                g = i * Q + q
                dve.wait_ge(s_load[q], 16 * (i + 1))
                dve.wait_ge(s_mm, g + 1)
                dve.tensor_scalar(hot[:, q, :, :, :].rearrange("p m a e -> p (m a e)"), rows[:, q, :], K.iota_part[:, 0:1], None, ALU.is_equal).then_inc(s_hot, 1)
                dve.wait_ge(s_prod, g + 1)
                dve.tensor_tensor(pick[:, q, :, :], K.iota_row[:, 0:NT].unsqueeze(1).broadcast_to([P, GS, NT]),
                                  K.hi_col[:, bass.ds(g * GS, GS)].unsqueeze(2).broadcast_to([P, GS, NT]), ALU.is_equal).then_inc(s_pick, 1)

            def mask(i, q):
                g = i * Q + q
                dve.wait_ge(s_pick, g + 1)
                dve.wait_ge(s_mm, g + 1 + Q)
                dve.wait_ge(s_red, g + 1)
                dve.tensor_tensor(prod[:, q, :, :].rearrange("p k (h t) -> p k h t", t=NT), ps[:, q, 0:first].rearrange("p (k h t) -> p k h t", k=GS, t=NT),
                                  pick[:, q, :, :].unsqueeze(2).broadcast_to([P, GS, H, NT]), ALU.mult).then_inc(s_prod, 1)

            def pick_source(i, q):
                g = i * Q + q
                dve.wait_ge(s_prod, g + 1 + Q)
                dve.wait_ge(s_al, g + 1)
                dve.tensor_reduce(red[:, q, :], prod[:, q, :, :].rearrange("p k (h t) -> p (k h) t", t=NT), AX, ALU.add).then_inc(s_red, 1)

            def add_target(i, q):
                g = i * Q + q
                dve.wait_ge(s_red, g + 1 + Q)
                dve.tensor_tensor(al[:, bass.ds(g * GS, GS), :].rearrange("p k h -> p (k h)") if H == 1 else al[:, bass.ds(g * GS, GS), :],
                                  red[:, q, :] if H == 1 else red[:, q, :].rearrange("p (k h) -> p k h", h=H),
                                  ps[:, q, first:first + GS * H] if H == 1 else ps[:, q, first:first + GS * H].rearrange("p (k h) -> p k h", h=H), ALU.add).then_inc(s_al, 1)

            def turn(i, head=False, tail=False):
                for q in range(Q):
                    mask(i, q)
                    if q:
                        add_target(i, q - 1)
                    elif not head:
                        add_target(i - 1, Q - 1)
                    pick_source(i, q)
                    if q + 2 < Q:
                        one_hot(i, q + 2)
                    elif not tail:
                        one_hot(i + 1, q + 2 - Q)

            step = Steps(dve, s_terms)
            split3(step, [src_terms[:, c, :, :] for c in range(3)], K.att_n[:, :, 0:H].rearrange("p t h -> p h t"), [rest[:, r, :, :] for r in range(2)])
            by_tile = [rest[:, r, :, :].rearrange("p h t -> p (h t)").rearrange("p (t h) -> p t h", h=H) for r in range(2)]
            split3(step, [dst_terms[:, :, c, :] for c in range(3)], K.att_n[:, :, H:2 * H], by_tile)
            for s in (s_hot, s_prod, s_red, s_al):
                dve.sem_inc(s, Q)
            one_hot(0, 0)
            one_hot(0, 1)
            turn(0, head=True)
            with dve.Fori(0, turns - 2) as i:
                turn(i + 1)
            turn(turns - 1, tail=True)
            add_target(turns - 1, Q - 1)
            dve.wait_ge(s_al, W // G + Q)
            turned = K.xn[:, :, :].rearrange("p t d -> p (t d)")[:, 0:WS * H].rearrange("p (j c h) -> p j c h", c=C, h=H)
            view = al.rearrange("p (c j) h -> p j c h", c=C)
            for c in range(C):
                ins = dve.scalar_tensor_tensor(turned[:, :, c, :], view[:, :, c, :], NEG_SLOPE, view[:, :, c, :], ALU.mult, ALU.max)
            ins.then_inc(s_fin, 1)
            dve.wait_ge(s_fin, 1)


def segment_softmax(prog, K, name, H, C, keep_max=None):
    J = WS // C
    R, L = C * H, J * P
    G = min(4, 512 // P)
    with Stage(prog, name) as st:
        al = K.al[:, 0:WS * H].rearrange("p (s h) -> p s h", h=H)
        turn = K.xn[:, :, :].rearrange("p t d -> p (t d)")[:, 0:WS * H]
        pen_p = K.arena_a[0:R, 0:L]
        pen_n = K.arena_a[0:R, L:2 * L]
        score = st.sbuf("score", [R, L])
        run = st.sbuf("run", [R, L]) if H == 1 else K.arena_b[0:R, 0:L]
        back = pen_p
        ends = st.sbuf("ends", [R, 2, 2])
        ends_row = st.sbuf("ends_row", [1, 2, 2, C, H])
        carry_row = st.sbuf("carry_row", [1, 2, C + 2, H])
        carry = st.sbuf("carry", [R, 2])
        ps_in = st.psum("ps_in", [P, 2, 512])
        ps_row = st.psum("ps_row", [P, 2, 512])
        s_pen, s_turn, s_score, s_step, s_end, s_endrow = (st.sem(n) for n in ("pen", "turn", "score", "step", "end", "endrow"))
        s_carry, s_carried, s_diff, s_exp, s_back, s_out = (st.sem(n) for n in ("carry", "carried", "diff", "exp", "back", "out"))
        turns = J // G
        block = st.block()

        @block.sync
        def _(sp):
            for pen, rows in ((pen_p, K.pen_prev), (pen_n, K.pen_next)):
                sp.dma_start(pen,
                             bass.AP(tensor=rows.tensor, offset=0, ap=[[L, C], [0, H], [1, L]])).then_inc(s_pen, 16)

        @block.gpsimd
        def _(pool):
            st.clear_stale(pool)

        @block.tensor
        def _(pe):
            for g in range(turns):
                if g >= 2:
                    pe.wait_ge(s_score, g - 1)
                for j in range(G):
                    ins = pe.transpose(ps_in[0:R, g % 2, j * P:(j + 1) * P],
                                       turn[:, (g * G + j) * R:(g * G + j + 1) * R], K.ident[:, :])
                ins.then_inc(s_turn, 1)
            for d in range(2):
                pe.wait_ge(s_end, d + 1)
                pe.transpose(ps_row[0:1, 0, 0:R], ends[:, d, 0:1], K.ident[0:R, 0:R])
                pe.transpose(ps_row[0:1, 0, R:2 * R], ends[:, d, 1:2], K.ident[0:R, 0:R]).then_inc(s_endrow, 1)
                pe.wait_ge(s_carry, d + 1)
                first = 0 if d == 0 else 2
                pe.transpose(ps_row[0:R, 1, 0:1], carry_row[:, d, first:first + C, :].rearrange("p c h -> p (c h)"),
                             K.ident[0:1, 0:1]).then_inc(s_carried, 1)
            for g in range(turns):
                pe.wait_ge(s_exp, 1)
                if g >= 2:
                    pe.wait_ge(s_out, g - 1)
                for j in range(G):
                    ins = pe.transpose(ps_in[:, g % 2, j * R:(j + 1) * R], score[:, (g * G + j) * P:(g * G + j + 1) * P],
                                       K.ident[0:R, 0:R])
                ins.then_inc(s_back, 1)
            if keep_max is not None:
                for g in range(turns):
                    pe.wait_ge(s_diff, 3)
                    b = turns + g
                    if b >= 2:
                        pe.wait_ge(s_out, b - 1)
                    for j in range(G):
                        ins = pe.transpose(ps_in[:, b % 2, j * R:(j + 1) * R], run[:, (g * G + j) * P:(g * G + j + 1) * P],
                                           K.ident[0:R, 0:R])
                    ins.then_inc(s_back, 1)

        @block.scalar
        def _(act):
            for g in range(turns):
                act.wait_ge(s_turn, g + 1)
                act.activation(score[:, g * G * P:(g + 1) * G * P], ps_in[0:R, g % 2, 0:G * P], ACT.Copy).then_inc(s_score, 1)
            act.wait_ge(s_diff, 1)
            act.activation(score[:, :], score[:, :], ACT.Exp).then_inc(s_exp, 1)

            def put(out, b):
                act.activation(out, ps_in[:, b % 2, 0:G * R].rearrange("p (j c h) -> p c j h", j=G, h=H), ACT.Copy).then_inc(s_out, 1)

            for g in range(turns):
                act.wait_ge(s_back, g + 1)
                put(al.rearrange("p (c j) h -> p c j h", j=J)[:, :, g * G:(g + 1) * G, :], g)
            if keep_max is not None:
                kept = keep_max.rearrange("p (c j) h -> p c j h", j=J)
                for g in range(turns):
                    act.wait_ge(s_back, turns + g + 1)
                    put(kept[:, :, g * G:(g + 1) * G, 0:H], turns + g)
                act.activation(keep_max[:, :, H], K.last_col[:, :], ACT.Copy).then_inc(s_out, 1)
                act.wait_ge(s_out, 2 * turns + 1)

        @block.vector
        def _(dve):
            n = [0]

            def step(ins):
                n[0] += 1
                ins.then_inc(s_step, 1)
                dve.wait_ge(s_step, n[0])

            dve.memset(carry_row[:, :, :, :], -BIG)
            dve.wait_ge(s_pen, 32)
            dve.tensor_reduce(ends[:, 0, 1:2], pen_p, AX, ALU.min)
            step(dve.tensor_reduce(ends[:, 1, 1:2], pen_n, AX, ALU.min))
            dve.wait_ge(s_score, turns)
            for d, (out, pen, data, last) in enumerate(((run[:, :], pen_p, score[:, :], L - 1),
                                                        (back[:, ::-1], pen_n[:, ::-1], run[:, ::-1], 0))):
                step(dve.tensor_tensor_scan(out, pen, data, -BIG, ALU.add, ALU.max))
                whole = (run if d == 0 else back)
                dve.tensor_copy(ends[:, d, 0:1], whole[:, last:last + 1]).then_inc(s_end, 1)
                dve.wait_ge(s_endrow, d + 1)
                step(dve.tensor_copy(ends_row[:, d, :, :, :].rearrange("p a c h -> p (a c h)"), ps_row[0:1, 0, 0:2 * R]))
                order = slice(None) if d == 0 else slice(None, None, -1)
                for h in range(H):
                    ins = dve.tensor_tensor_scan(carry_row[:, d, 1:C + 1, h][:, order], ends_row[:, d, 1, :, h][:, order],
                                                 ends_row[:, d, 0, :, h][:, order], -BIG, ALU.add, ALU.max)
                ins.then_inc(s_carry, 1)
                dve.wait_ge(s_carried, d + 1)
                step(dve.tensor_copy(carry[:, d:d + 1], ps_row[0:R, 1, 0:1]))
                step(dve.tensor_tensor_scan(out, pen, data, carry[:, d:d + 1], ALU.add, ALU.max))
            dve.tensor_tensor(score[:, :], score[:, :], back, ALU.subtract).then_inc(s_diff, 1)
            if keep_max is not None:
                dve.wait_ge(s_diff, 1)
                dve.tensor_scalar(pen_n, pen_n, -1.0 / BIG, None, ALU.mult).then_inc(s_diff, 1)
                dve.wait_ge(s_diff, 2)
                dve.tensor_tensor(run[:, :], back, pen_n, ALU.mult).then_inc(s_diff, 1)
                dve.wait_ge(s_diff, 3)


def aggregate(prog, K, name, H, RW, table, acc, extra=None, blank=None):
    X = 0 if extra is None else extra.shape[2]
    B = 1 if RW <= 512 else 2
    part = -(-(RW + X) // B)
    with Stage(prog, name) as st:
        Q, U2 = 5, 4
        J = Q * U2
        al = K.al[:, 0:WS * H].rearrange("p (s h) -> p s h", h=H)
        rows = st.sbuf("rows", [P, Q, SUB, B * part])
        hot = st.sbuf("hot", [P, Q, SUB, P])
        idx = st.sbuf("idx", [P, Q, SUB], I32)
        s_idx = st.sem("idx")
        HALF = 1 if B > 1 else SUB
        weight = st.sbuf("weight", [P, Q, H])
        s_extra, s_pad = st.sem("extra"), st.sem("pad")
        s_weight, s_msg2 = st.sem("weight"), st.sem("msg2")
        ps = st.psum("ps", [P, U2, B, 512])
        zeros = st.sbuf("zeros", [P, 4 * D]) if blank is not None else None
        s_zeros, s_blank = st.sem("zeros"), st.sem("blank")
        s_gath, gathered = K.gath, list(K.gathered)
        s_hot, s_msg, s_sum, s_acc, s_zero = (st.sem(n) for n in ("hot", "msg", "sum", "acc", "zero"))
        block = st.block()

        if blank is not None:
            @block.sync
            def _(sp):
                sp.wait_ge(s_zeros, 1)
                for r in range(blank.shape[0] // (4 * P)):
                    sp.dma_start(blank[r * 4 * P:(r + 1) * 4 * P, :].rearrange("(p j) d -> p (j d)", j=4), zeros[:, :]).then_inc(s_blank, 16)
                sp.wait_ge(s_blank, 16 * (blank.shape[0] // (4 * P)))

        @block.gpsimd
        def _(pool):
            st.clear_stale(pool)
            if B * part > RW + X:
                pool.memset(rows[:, :, :, RW + X:], 0.0).then_inc(s_pad, 1)
            with pool.Fori(0, W // J) as i:
                for j in range(J):
                    w, q = i * J + j, j % Q
                    pool.wait_ge(s_idx, w + 1)
                    pool.nop(nofuse=True)
                    for s in range(SUB):
                        pool.indirect_dma_start(rows[:, q, s, 0:RW], None, table,
                                                bass.IndirectOffsetOnAxis(ap=idx[:, q, s:s + 1], axis=0)).then_inc(s_gath[q], 16)

        @block.scalar
        def _(act):
            def sources(i, j):
                w, q = i * J + j, j % Q
                act.wait_ge(s_sum, w + 1)
                act.activation(idx[:, q, :], K.src_col[:, bass.ds(w * SUB, SUB)], ACT.Copy).then_inc(s_idx, 1)
                if X:
                    act.activation(rows[:, q, :, RW:RW + X], extra[:, bass.ds(w * SUB, SUB), :], ACT.Copy).then_inc(s_extra, 1)
                if HALF < SUB:
                    act.activation(weight[:, q, :], al[:, bass.ds(w * SUB + 1, 1), :].rearrange("p s h -> p (s h)"), ACT.Copy).then_inc(s_weight, 1)

            def message(i, j):
                if HALF < SUB:
                    w, q = i * J + j, j % Q
                    act.wait_ge(s_gath[q], gathered[q] + 32 * (i * (J // Q) + j // Q + 1))
                    act.wait_ge(s_weight, w + 1)
                    for h in range(H):
                        part = rows[:, q, 1, h * (RW // H):(h + 1) * (RW // H)]
                        ins = act.activation(part, part, ACT.Copy, scale=weight[:, q, h:h + 1])
                    ins.then_inc(s_msg2, 1)

            ahead = Q - 2
            for j in range(ahead):
                sources(0, j)
            with act.Fori(0, W // J - 1) as i:
                for j in range(J):
                    sources(i + (j + ahead) // J, (j + ahead) % J)
                    message(i, j)
            for j in range(J):
                if j + ahead < J:
                    sources(W // J - 1, j + ahead)
                message(W // J - 1, j)

        @block.tensor
        def _(pe):
            pe.sem_inc(s_sum, Q)
            if B * part > RW + X:
                pe.wait_ge(s_pad, 1)
            with pe.Fori(0, W // J) as i:
                for j in range(J):
                    w, q, u = i * J + j, j % Q, j % U2
                    pe.wait_ge(s_hot, w + 1)
                    pe.wait_ge(s_msg, w + 1)
                    if HALF < SUB:
                        pe.wait_ge(s_msg2, w + 1)
                    if X:
                        pe.wait_ge(s_extra, w + 1)
                    pe.wait_ge(s_acc, w + 1)
                    for s in range(SUB):
                        for b in range(B):
                            ins = pe.matmul(ps[:, u, b, 0:part], lhsT=hot[:, q, s, :], rhs=rows[:, q, s, b * part:(b + 1) * part],
                                            start=(s == 0), stop=(s == SUB - 1))
                    ins.then_inc(s_sum, 1)

        @block.vector
        def _(dve):
            def message(i, j):
                w, q = i * J + j, j % Q
                dve.wait_ge(s_sum, w + 1)
                for s in range(SUB):
                    ins = dve.tensor_scalar(hot[:, q, s, :], K.iota_row[:, :], K.rel_col[:, bass.ds(w * SUB + s, 1)], None, ALU.is_equal)
                ins.then_inc(s_hot, 1)
                dve.wait_ge(s_gath[q], gathered[q] + 32 * (i * (J // Q) + j // Q + 1))
                view = rows[:, q, 0:HALF, 0:RW].rearrange("p s (h r) -> p (s h) r", h=H)
                dve.tensor_tensor(view, view, al[:, bass.ds(w * SUB, HALF), :].rearrange("p s h -> p (s h)").unsqueeze(2).broadcast_to([P, HALF * H, RW // H]),
                                  ALU.mult).then_inc(s_msg, 1)

            def add(i, j):
                w, u = i * J + j, j % U2
                window = dve.value_load(K.window[0:1, bass.ds(w, 1)], min_val=0, max_val=NT - 1)
                dve.wait_ge(s_sum, w + 1 + Q)
                dve.wait_ge(s_acc, w + U2)
                out = acc[:, window, :].rearrange("p (b c) -> p b c", b=B)
                dve.tensor_tensor(out, out, ps[:, u, :, 0:part], ALU.add).then_inc(s_acc, 1)

            dve.sem_inc(s_acc, U2)
            if blank is not None:
                dve.memset(zeros[:, :], 0.0).then_inc(s_zeros, 1)
            dve.memset(acc, 0.0).then_inc(s_zero, 1)
            dve.wait_ge(s_zero, 1)
            message(0, 0)
            message(0, 1)
            with dve.Fori(0, W // J - 1) as i:
                for j in range(J):
                    message(i + (j + 2) // J, (j + 2) % J)
                    add(i, j)
            for j in range(J):
                if j + 2 < J:
                    message(W // J - 1, j + 2)
                add(W // J - 1, j)
            dve.wait_ge(s_acc, W + U2)

        K.gathered = [n + 32 * (W // Q) for n in K.gathered]


def finish_l0(prog, K, A):
    R = DH0 + 1
    with Stage(prog, "fin0") as st:
        den = st.sbuf("den", [P, NT, H0])
        rden = st.sbuf("rden", [P, NT, H0])
        bias = st.sbuf("bias", [P, 3, D])
        ps = st.psum("ps", [P, 4, 512])
        s_b, s_dve, s_mm, s_add = (st.sem(n) for n in ("b", "dve", "mm", "add"))
        acc = K.acc0[:, :, :].rearrange("p t (h r) -> p t h r", r=R)
        block = st.block()

        @block.sync
        def _(sp):
            load_rows(sp, s_b, bias[:, 0, :], A["g0_b"])
            load_rows(sp, s_b, bias[:, 1, :], A["m0_bo"])

        @block.gpsimd
        def _(pool):
            st.clear_stale(pool)

        @block.tensor
        def _(pe):
            for t in range(NT):
                if t >= 4:
                    pe.wait_ge(s_add, t - 3)
                for k in range(2):
                    ins = pe.matmul(ps[:, t % 4, 0:D], lhsT=K.xn_t[:, k, t * P:(t + 1) * P], rhs=K.mix[:, k, :], start=(k == 0), stop=(k == 1))
                ins.then_inc(s_mm, 1)

        @block.vector
        def _(dve):
            n = [0]

            def step(ins):
                n[0] += 1
                ins.then_inc(s_dve, 1)
                dve.wait_ge(s_dve, n[0])

            step(dve.tensor_scalar(den[:, :, :], acc[:, :, :, DH0], 1e-10, None, ALU.max))
            step(dve.reciprocal(rden[:, :, :], den[:, :, :]))
            dve.wait_ge(s_b, 32)
            step(dve.tensor_tensor(bias[:, 2, :], bias[:, 0, :], bias[:, 1, :], ALU.add))
            step(dve.tensor_tensor(acc[:, :, :, 0:DH0], acc[:, :, :, 0:DH0], rden[:, :, :].unsqueeze(3).broadcast_to([P, NT, H0, DH0]), ALU.mult))
            step(dve.tensor_tensor(K.x[:, :, :], K.x[:, :, :], bias[:, 2, :].unsqueeze(1).broadcast_to([P, NT, D]), ALU.add))
            step(dve.tensor_tensor(K.x[:, :, :].rearrange("p t (h d) -> p t h d", h=H0), K.x[:, :, :].rearrange("p t (h d) -> p t h d", h=H0),
                                   acc[:, :, :, 0:DH0], ALU.add))
            for t in range(NT):
                dve.wait_ge(s_mm, t + 1)
                dve.tensor_tensor(K.x[:, t, :], K.x[:, t, :], ps[:, t % 4, 0:D], ALU.add).then_inc(s_add, 1)
            dve.wait_ge(s_add, NT)


def first_best(dve, step, logits, bias, code, EX, tmp, best, hot, pick):
    shape = [P, NT, EX]
    step(dve.tensor_tensor(logits, logits, bias.unsqueeze(1).broadcast_to(shape), ALU.add))
    step(dve.tensor_reduce(best, logits, AX, ALU.max))
    step(dve.tensor_tensor(tmp, logits, best.unsqueeze(2).broadcast_to(shape), ALU.is_lt))
    step(dve.scalar_tensor_tensor(tmp, tmp, float(EX), code.unsqueeze(1).broadcast_to(shape), ALU.mult, ALU.add))
    step(dve.tensor_reduce(pick, tmp, AX, ALU.min))
    step(dve.tensor_tensor(hot, code.unsqueeze(1).broadcast_to(shape), pick.unsqueeze(2).broadcast_to(shape), ALU.is_equal))


def expert_weights_l0(K):
    a, n = K.arena_a, 2 * F0
    w1 = [a[:, e * n:(e + 1) * n].rearrange("p (k f) -> p k f", k=2) for e in range(2)]
    w2 = [a[:, (2 + e) * n:(3 + e) * n].rearrange("p (c d) -> p c d", d=D) for e in range(2)]
    return w1, w2


def load_expert_l0(sp, A, w1, w2, e, j, sem):
    sp.dma_start(w1[j], A["f0_w1"][e].rearrange("(k p) f -> p k f", p=P)).then_inc(sem, 16)
    sp.dma_start(w2[j], A["f0_w2"][e].rearrange("(c p) d -> p c d", p=P)).then_inc(sem, 16)


def route_l0(prog, K, A):
    FAR = 1.0e6
    with Stage(prog, "route0") as st:
        gw = st.sbuf("gw", [P, 2, E0])
        gb = st.sbuf("gb", [P, E0])
        code = st.sbuf("code", [P, E0])
        node = st.sbuf("node", [P, NT])
        tri = st.sbuf("tri", [P, P])
        ones = st.sbuf("ones", [P, P])
        logits, tmp, hot, before, placed = (st.sbuf(n, [P, NT, E0]) for n in ("logits", "tmp", "hot", "before", "placed"))
        total, upto = st.sbuf("total", [P, NT, E0]), st.sbuf("upto", [P, NT, E0])
        best, pick, esum, prob, place, kept, slot, far, away = (
            st.sbuf(n, [P, NT]) for n in ("best", "pick", "esum", "prob", "place", "kept", "slot", "far", "away"))
        ps_l = st.psum("ps_l", [P, 512])
        ps_c = st.psum("ps_c", [P, 2, 512])
        s_w, s_const, s_logits, s_dve, s_hot, s_count = (st.sem(n) for n in ("w", "const", "logits", "dve", "hot", "count"))
        s_diff, s_exp, s_slot = (st.sem(n) for n in ("diff", "exp", "slot"))
        s_sent = st.sem_sw("sent")
        s_first = st.sem("first")
        block = st.block()

        @block.sync
        def _(sp):
            sp.dma_start(gw[:, :, :], A["f0_gw"].rearrange("(k p) n -> p k n", p=P)).then_inc(s_w, 16)
            load_rows(sp, s_w, gb[:, :], A["f0_gb"])
            for e in range(2):
                load_expert_l0(sp, A, *expert_weights_l0(K), e, e, s_first)
            sp.wait_ge(s_first, 64)

        @block.gpsimd
        def _(pool):
            st.clear_stale(pool)
            pool.memset(ones[:, :], 1.0).then_inc(s_const, 1)
            pool.iota(code[:, :], [[1, E0]], base=E0, channel_multiplier=0, allow_small_or_imprecise_dtypes=True).then_inc(s_const, 1)
            pool.iota(node[:, :], [[P, NT]], base=0, channel_multiplier=1, allow_small_or_imprecise_dtypes=True).then_inc(s_const, 1)
            pool.wait_ge(s_const, 1)
            pool.affine_select(out=tri[:, :], in_=ones[:, :], compare_op=ALU.is_ge, fill=0.0, base=0,
                               pattern=[[1, P]], channel_multiplier=-1).then_inc(s_const, 1)
            pool.wait_ge(s_slot, 2)
            for t in range(NT):
                pool.indirect_dma_start(K.slots, bass.IndirectOffsetOnAxis(ap=K.slot_to[:, t:t + 1], axis=0), K.xn[:, t, :], None,
                                        bounds_check=E0 * CAP - 1, oob_is_err=False).then_inc(s_sent, 16)
            pool.wait_ge(s_sent, 16 * NT)

        @block.tensor
        def _(pe):
            pe.wait_ge(s_w, 32)
            for t in range(NT):
                for k in range(2):
                    ins = pe.matmul(ps_l[:, t * E0:(t + 1) * E0], lhsT=K.xn_t[:, k, t * P:(t + 1) * P], rhs=gw[:, k, :], start=(k == 0), stop=(k == 1))
            ins.then_inc(s_logits, 1)
            pe.wait_ge(s_const, 4)
            pe.wait_ge(s_hot, 1)
            flat = hot[:, :, :].rearrange("p t e -> p (t e)")
            pe.matmul(ps_c[:, 0, 0:NT * E0], lhsT=tri[:, :], rhs=flat, start=True, stop=True)
            pe.matmul(ps_c[:, 1, 0:NT * E0], lhsT=ones[:, :], rhs=flat, start=True, stop=True).then_inc(s_count, 1)

        @block.scalar
        def _(act):
            act.wait_ge(s_diff, 1)
            act.activation(tmp[:, :, :], tmp[:, :, :], ACT.Exp).then_inc(s_exp, 1)

        @block.vector
        def _(dve):
            n = [0]

            def step(ins):
                n[0] += 1
                ins.then_inc(s_dve, 1)
                dve.wait_ge(s_dve, n[0])

            dve.wait_ge(s_w, 32)
            dve.wait_ge(s_const, 4)
            dve.wait_ge(s_logits, 1)
            step(dve.tensor_copy(logits[:, :, :].rearrange("p t e -> p (t e)"), ps_l[:, 0:NT * E0]))
            first_best(dve, step, logits[:, :, :], gb[:, :], code[:, :], E0, tmp[:, :, :], best[:, :], hot[:, :, :], pick[:, :])
            dve.sem_inc(s_hot, 1)
            dve.tensor_tensor(tmp[:, :, :], logits[:, :, :], best[:, :].unsqueeze(2).broadcast_to([P, NT, E0]), ALU.subtract).then_inc(s_diff, 1)
            dve.wait_ge(s_exp, 1)
            step(dve.tensor_reduce(esum[:, :], tmp[:, :, :], AX, ALU.add))
            step(dve.reciprocal(prob[:, :], esum[:, :]))
            dve.wait_ge(s_count, 1)
            step(dve.tensor_copy(total[:, :, :].rearrange("p t e -> p (t e)"), ps_c[:, 1, 0:NT * E0]))
            for e in range(E0):
                ins = dve.tensor_tensor_scan(upto[:, :, e], total[:, :, e], total[:, :, e], 0.0, ALU.add, ALU.max)
            step(ins)
            step(dve.tensor_tensor(before[:, :, :], upto[:, :, :], total[:, :, :], ALU.subtract))
            step(dve.tensor_tensor(before[:, :, :], before[:, :, :], ps_c[:, 0, 0:NT * E0].rearrange("p (t e) -> p t e", e=E0), ALU.add))
            step(dve.tensor_tensor(placed[:, :, :], before[:, :, :], hot[:, :, :], ALU.mult))
            step(dve.tensor_reduce(place[:, :], placed[:, :, :], AX, ALU.add))
            step(dve.tensor_scalar(kept[:, :], place[:, :], float(CAP), None, ALU.is_le))
            step(dve.tensor_scalar(place[:, :], place[:, :], float(CAP), -1.0 - E0 * CAP, ALU.min, ALU.add))
            step(dve.scalar_tensor_tensor(slot[:, :], pick[:, :], float(CAP), place[:, :], ALU.mult, ALU.add))
            step(dve.tensor_scalar(far[:, :], node[:, :], float(N), FAR, ALU.is_ge, ALU.mult))
            step(dve.scalar_tensor_tensor(away[:, :], kept[:, :], -FAR, far[:, :], ALU.mult, ALU.add))
            step(dve.scalar_tensor_tensor(far[:, :], slot[:, :], FAR, away[:, :], ALU.add, ALU.add))
            dve.tensor_copy(K.slot_to[:, :], far[:, :]).then_inc(s_slot, 1)
            dve.tensor_copy(K.slot_from[:, :], slot[:, :]).then_inc(s_slot, 1)
            dve.tensor_tensor(K.gate[:, :], prob[:, :], kept[:, :], ALU.mult).then_inc(s_slot, 1)
            dve.wait_ge(s_slot, 3)


def experts_l0(prog, K, A):
    FC = F0 // P
    M = -(-CAP // P)
    size = [min(P, CAP - m * P) for m in range(M)]
    with Stage(prog, "moe0") as st:
        a = K.arena_a
        w1, w2 = expert_weights_l0(K)
        at = 4 * F0 + 2 * FC * D
        rows = [a[:, at + e * M * D:at + (e + 1) * M * D].rearrange("p (m d) -> p m d", m=M) for e in range(2)]
        xs_t = K.arena_b[:, 0:2 * 512].rearrange("p (k s) -> p k s", k=2)
        h_t = K.arena_b[:, 2 * 512:2 * 512 + FC * 512].rearrange("p (c s) -> p c s", c=FC)
        y = K.al[:, 0:M * D].rearrange("p (m d) -> p m d", m=M)
        b1 = st.sbuf("b1", [P, E0 * FC])
        b2 = st.sbuf("b2", [P, E0, D])
        ps_t = st.psum("ps_t", [P, 2, 512])
        ps_h = st.psum("ps_h", [P, 2, 512])
        ps_y = st.psum("ps_y", [P, 2, 512])
        s_b = st.sem("b")
        s_in = [st.sem(f"in{e}") for e in range(2)]
        s_t, s_xt, s_h, s_ht, s_y, s_yb, s_used = (st.sem(n) for n in ("t", "xt", "h", "ht", "y", "yb", "used"))
        s_out = [st.sem_sw(f"out{m}") for m in range(M)]
        block = st.block()

        @block.sync
        def _(sp):
            sp.dma_start(b1[:, :], A["f0_b1"]).then_inc(s_b, 16)
            load_rows(sp, s_b, b2[:, :, :].rearrange("p e d -> p (e d)"), A["f0_b2"])
            def load(e, j):
                sp.dma_start(rows[j][:, 0:M - 1, :], K.slots[bass.ds(e * CAP, (M - 1) * P), :].rearrange("(m p) d -> p m d", p=P)).then_inc(s_in[j], 16)
                sp.dma_start(rows[j][0:size[-1], M - 1, :], K.slots[bass.ds(e * CAP + (M - 1) * P, size[-1]), :]).then_inc(s_in[j], 16)

            load(0, 0)
            load(1, 1)
            with sp.Fori(1, E0 // 2) as i:
                for j in range(2):
                    e = i * 2 + j
                    sp.wait_ge(s_used, e + 1)
                    load(e, j)
                    load_expert_l0(sp, A, w1, w2, e, j, s_in[j])

        @block.tensor
        def _(pe):
            pe.sem_inc(s_used, 2)
            with pe.Fori(0, E0 // 2) as i:
                for j in range(2):
                    e = i * 2 + j
                    pe.wait_ge(s_in[j], 64 * i + 32)
                    pe.wait_ge(s_xt, e + 1)
                    for k in range(2):
                        for m in range(M):
                            ins = pe.transpose(ps_t[:, k, m * P:m * P + size[m]], rows[j][0:size[m], m, k * P:(k + 1) * P], K.ident[0:size[m], 0:size[m]])
                    ins.then_inc(s_t, 1)
                    pe.wait_ge(s_xt, e + 2)
                    for c in range(FC):
                        pe.wait_ge(s_ht, e * FC + c + 1)
                        for k in range(2):
                            ins = pe.matmul(ps_h[:, c % 2, 0:CAP], lhsT=w1[j][:, k, c * P:(c + 1) * P], rhs=xs_t[:, k, 0:CAP], start=(k == 0), stop=(k == 1))
                        ins.then_inc(s_h, 1)
                    pe.wait_ge(s_ht, e * FC + FC + 2)
                    for m in range(M):
                        pe.wait_ge(s_yb, e * M + m + 1)
                        for c in range(FC):
                            ins = pe.matmul(ps_y[0:size[m], m % 2, 0:D], lhsT=h_t[:, c, m * P:m * P + size[m]], rhs=w2[j][:, c, :], start=(c == 0), stop=(c == FC - 1))
                        ins.then_inc(s_y, 1)
                    pe.drain().then_inc(s_used, 1)

        @block.scalar
        def _(act):
            act.sem_inc(s_xt, 1)
            act.sem_inc(s_ht, 2)
            act.wait_ge(s_b, 32)
            with act.Fori(0, E0) as e:
                act.wait_ge(s_t, e + 1)
                act.activation(xs_t[:, :, 0:CAP], ps_t[:, :, 0:CAP], ACT.Copy).then_inc(s_xt, 1)
                for c in range(FC):
                    act.wait_ge(s_h, e * FC + c + 1)
                    act.activation(h_t[:, c, 0:CAP], ps_h[:, c % 2, 0:CAP], ACT.Relu, bias=b1[:, bass.ds(e * FC + c, 1)]).then_inc(s_ht, 1)

        @block.vector
        def _(dve):
            dve.sem_inc(s_yb, 2)
            dve.wait_ge(s_b, 32)

            def add_bias(e, m):
                dve.wait_ge(s_y, e * M + m + 1)
                dve.tensor_tensor(y[0:size[m], m, :], ps_y[0:size[m], m % 2, 0:D], b2[0:size[m], e, :], ALU.add).then_inc(s_yb, 1)

            for m in range(M):
                add_bias(0, m)
            with dve.Fori(1, E0) as e:
                for m in range(M):
                    dve.wait_ge(s_out[m], 16 * e)
                    add_bias(e, m)

        @block.gpsimd
        def _(pool):
            st.clear_stale(pool)
            with pool.Fori(0, E0) as e:
                for m in range(M):
                    pool.wait_ge(s_yb, e * M + m + 3)
                    pool.dma_start(K.y_slots[bass.ds(e * CAP + m * P, size[m]), :], y[0:size[m], m, :]).then_inc(s_out[m], 16)
            for m in range(M):
                pool.wait_ge(s_out[m], 16 * E0)


def combine_l0(prog, K):
    TOP, LIMIT = 3.4028234663852886e38, 1.0e4
    with Stage(prog, "join0") as st:
        y = K.arena_b[:, 0:NT * D].rearrange("p (t d) -> p t d", t=NT)
        z = K.arena_a[:, 0:3 * U * D].rearrange("p (a t d) -> p a t d", a=3, t=U)
        mask = st.sbuf("mask", [P, U, D], I32)
        s_y = [st.sem_sw(f"y{c}") for c in range(NT // U)]
        s_dve = st.sem("dve")
        block = st.block()

        @block.gpsimd
        def _(pool):
            st.clear_stale(pool)
            for t in range(NT):
                pool.indirect_dma_start(y[:, t, :], None, K.y_slots, bass.IndirectOffsetOnAxis(ap=K.slot_from[:, t:t + 1], axis=0)).then_inc(s_y[t // U], 16)

        @block.vector
        def _(dve):
            n = [0]

            def step(ins):
                n[0] += 1
                ins.then_inc(s_dve, 1)
                dve.wait_ge(s_dve, n[0])

            for c in range(NT // U):
                dve.wait_ge(s_y[c], 16 * U)
                part = y[:, c * U:(c + 1) * U, :]
                xc = K.x[:, c * U:(c + 1) * U, :]
                step(dve.tensor_tensor(part, part, K.gate[:, c * U:(c + 1) * U].unsqueeze(2).broadcast_to([P, U, D]), ALU.mult))
                dve.tensor_scalar(z[:, 0], part, TOP, LIMIT, ALU.is_gt, ALU.mult)
                dve.tensor_scalar(z[:, 1], part, -TOP, -LIMIT, ALU.is_lt, ALU.mult)
                step(dve.tensor_scalar(mask[:, :, :], part, 0.0, 0.0, ALU.mult, ALU.is_equal))
                step(dve.tensor_tensor(z[:, 2], z[:, 0], z[:, 1], ALU.add))
                step(dve.copy_predicated(z[:, 2], mask[:, :, :], part))
                step(dve.tensor_tensor(xc, xc, z[:, 2], ALU.add))


def project_l1(prog, K, A):
    R = DH1 + 1
    with Stage(prog, "proj1") as st:
        w = st.sbuf("w", [P, 2, H1 * DH1])
        w_att = st.sbuf("w_att", [P, 2, 2 * H1])
        att = K.arena_a[:, 0:2 * H1 * DH1].rearrange("p (a n) -> p a n", a=2)
        tmp = K.arena_a[:, 1024:3072].rearrange("p (k n) -> p k n", k=4)
        row = K.arena_b[:, 0:U * H1 * R].rearrange("p (u n) -> p u n", u=U)
        ps_h = st.psum("ps_h", [P, 4, 512])
        ps_a = st.psum("ps_a", [P, 2, 512])
        s_w, s_wa, s_dve, s_one, s_h, s_a, s_row, s_att = (st.sem(n) for n in ("w", "wa", "dve", "one", "h", "a", "row", "att"))
        s_out = [st.sem(f"out{u}") for u in range(U)]
        block = st.block()

        @block.sync
        def _(sp):
            sp.dma_start(w[:, :, :], A["g1_w1"].rearrange("(k p) n -> p k n", p=P)).then_inc(s_w, 16)
            load_rows(sp, s_w, att[:, 0, :], A["g1_as1"])
            load_rows(sp, s_w, att[:, 1, :], A["g1_ad1"])
            with sp.Fori(0, NT // U) as i:
                for u in range(U):
                    t = i * U + u
                    sp.wait_ge(s_row, t + 1)
                    sp.dma_start(K.table1[bass.ds(t * P, P), :], row[:, u, :]).then_inc(s_out[u], 16)
            for u in range(U):
                sp.wait_ge(s_out[u], 16 * (NT // U))

        @block.gpsimd
        def _(pool):
            st.clear_stale(pool)
            pool.memset(row.rearrange("p u (h r) -> p (u h) r", r=R)[:, :, DH1:R], 1.0).then_inc(s_one, 1)

        @block.tensor
        def _(pe):
            pe.wait_ge(s_w, 48)
            pe.wait_ge(s_wa, 2)
            for t in range(NT):
                if t >= 4:
                    pe.wait_ge(s_row, t - 3)
                for k in range(2):
                    ins = pe.matmul(ps_h[:, t % 4, :], lhsT=K.xn_t[:, k, t * P:(t + 1) * P], rhs=w[:, k, :], start=(k == 0), stop=(k == 1))
                ins.then_inc(s_h, 1)
                if t >= 2:
                    pe.wait_ge(s_att, t - 1)
                for k in range(2):
                    ins = pe.matmul(ps_a[:, t % 2, 0:2 * H1], lhsT=K.xn_t[:, k, t * P:(t + 1) * P], rhs=w_att[:, k, :], start=(k == 0), stop=(k == 1))
                ins.then_inc(s_a, 1)

        @block.scalar
        def _(act):
            act.wait_ge(s_one, 1)
            for t in range(NT):
                act.wait_ge(s_h, t + 1)
                if t >= U:
                    act.wait_ge(s_out[t % U], 16 * (t // U))
                act.activation(row[:, t % U, :].rearrange("p (h r) -> p h r", r=R)[:, :, 0:DH1],
                               ps_h[:, t % 4, :].rearrange("p (h d) -> p h d", d=DH1), ACT.Copy).then_inc(s_row, 1)

        @block.vector
        def _(dve):
            dve.wait_ge(s_w, 48)
            for a in range(2):
                dve.tensor_tensor(tmp[:, 2 * a:2 * a + 2, :], w[:, :, :], att[:, a, :].unsqueeze(1).broadcast_to([P, 2, H1 * DH1]), ALU.mult).then_inc(s_dve, 1)
            dve.wait_ge(s_dve, 2)
            for a in range(2):
                dve.tensor_reduce(w_att[:, :, a * H1:(a + 1) * H1], tmp[:, 2 * a:2 * a + 2, :].rearrange("p k (h d) -> p k h d", h=H1), AX, ALU.add).then_inc(s_wa, 1)
            for t in range(NT):
                dve.wait_ge(s_a, t + 1)
                dve.tensor_copy(K.att_n[:, t, 0:2 * H1], ps_a[:, t % 2, 0:2 * H1]).then_inc(s_att, 1)


def linear_attention_l1(prog, K, A):
    KD = LH * LD
    with Stage(prog, "mix1") as st:
        a = K.arena_a
        k_t = a[:, 0:N]
        v = a[:, N:N + NT * KD].rearrange("p (t d) -> p t d", t=NT)
        ek = a[:, N + NT * KD:N + 2 * NT * KD].rearrange("p (t d) -> p t d", t=NT)
        w = st.sbuf("w", [P, 2, 2 * KD])
        wqt = st.sbuf("wqt", [P, D])
        wo = st.sbuf("wo", [P, D])
        G = -(-N // 512)
        tops = st.sbuf("tops", [P, G])
        top = st.sbuf("top", [P, 1])
        low = st.sbuf("low", [P, 1])
        ksum = st.sbuf("ksum", [P, 1])
        rsum = st.sbuf("rsum", [P, 1])
        ctx = st.sbuf("ctx", [P, P])
        co = st.sbuf("co", [P, D])
        ps_k = st.psum("ps_k", [P, 2, 512])
        ps_v = st.psum("ps_v", [P, 2, 512])
        ps_e = st.psum("ps_e", [P, 2, 512])
        ps_c = st.psum("ps_c", [P, 2, 512])
        s_w, s_k, s_kt, s_v, s_vs, s_dve, s_low, s_exp, s_e, s_ek, s_c, s_cs, s_o, s_os, s_m, s_ms = (
            st.sem(n) for n in ("w", "k", "kt", "v", "vs", "dve", "low", "exp", "e", "ek", "c", "cs", "o", "os", "m", "ms"))
        block = st.block()

        @block.sync
        def _(sp):
            sp.dma_start(w[:, :, :], A["m1_wkv"].rearrange("(k p) n -> p k n", p=P)).then_inc(s_w, 16)
            sp.dma_start(wqt[:, :], A["m1_wqt"]).then_inc(s_w, 16)
            sp.dma_start(wo[:, :], A["m1_wo"]).then_inc(s_w, 16)

        @block.gpsimd
        def _(pool):
            st.clear_stale(pool)

        def context(pe, t):
            n = P if t < NT - 1 else NLAST
            pe.wait_ge(s_ek, t + 1)
            ins = pe.matmul(ps_c[:, 0, 0:KD], lhsT=v[0:n, t, :], rhs=ek[0:n, t, :], start=(t == 0), stop=(t == NT - 1))
            if t == NT - 1:
                ins.then_inc(s_c, 1)

        @block.tensor
        def _(pe):
            pe.wait_ge(s_w, 48)
            for g in range(G):
                n = min(512, N - g * 512)
                if g >= 2:
                    pe.wait_ge(s_kt, g - 1)
                for k in range(2):
                    ins = pe.matmul(ps_k[:, g % 2, 0:n], lhsT=w[:, k, 0:KD], rhs=K.xn_t[:, k, g * 512:g * 512 + n], start=(k == 0), stop=(k == 1))
                ins.then_inc(s_k, 1)
            for t in range(NT):
                if t >= 2:
                    pe.wait_ge(s_vs, t - 1)
                for k in range(2):
                    ins = pe.matmul(ps_v[:, t % 2, 0:KD], lhsT=K.xn_t[:, k, t * P:(t + 1) * P], rhs=w[:, k, KD:2 * KD], start=(k == 0), stop=(k == 1))
                ins.then_inc(s_v, 1)
            pe.wait_ge(s_exp, 1)
            for t in range(NT):
                n = P if t < NT - 1 else NLAST
                if t >= 2:
                    pe.wait_ge(s_ek, t - 1)
                pe.transpose(ps_e[0:n, t % 2, 0:KD], k_t[:, t * P:t * P + n], K.ident[:, :]).then_inc(s_e, 1)
                if t >= 1:
                    context(pe, t - 1)
            context(pe, NT - 1)
            pe.wait_ge(s_cs, 1)
            pe.matmul(ps_k[:, 0, 0:D], lhsT=ctx[:, :], rhs=wo[:, :], start=True, stop=True).then_inc(s_o, 1)
            pe.wait_ge(s_os, 1)
            for c in range(2):
                ins = pe.matmul(ps_v[:, c, 0:D], lhsT=wqt[:, c * P:(c + 1) * P], rhs=co[:, :], start=True, stop=True)
            ins.then_inc(s_m, 1)

        @block.scalar
        def _(act):
            for t in range(NT):
                act.wait_ge(s_v, t + 1)
                act.activation(v[:, t, :], ps_v[:, t % 2, 0:KD], ACT.Copy).then_inc(s_vs, 1)
            act.wait_ge(s_low, 1)
            act.activation(k_t, k_t, ACT.Exp, bias=low[:, 0:1], accum_out=ksum[:, 0:1]).then_inc(s_exp, 1)
            for t in range(NT):
                n = P if t < NT - 1 else NLAST
                act.wait_ge(s_e, t + 1)
                act.activation(ek[0:n, t, :], ps_e[0:n, t % 2, 0:KD], ACT.Copy).then_inc(s_ek, 1)

        @block.vector
        def _(dve):
            for g in range(G):
                n = min(512, N - g * 512)
                dve.wait_ge(s_k, g + 1)
                dve.tensor_reduce(tops[:, g:g + 1], ps_k[:, g % 2, 0:n], AX, ALU.max)
                dve.tensor_copy(k_t[:, g * 512:g * 512 + n], ps_k[:, g % 2, 0:n]).then_inc(s_kt, 1)
            dve.wait_ge(s_kt, G)
            dve.tensor_reduce(top[:, :], tops[:, :], AX, ALU.max).then_inc(s_dve, 1)
            dve.wait_ge(s_dve, 1)
            dve.tensor_scalar(low[:, :], top[:, :], -1.0, None, ALU.mult).then_inc(s_low, 1)
            dve.memset(ctx[:, :], 0.0).then_inc(s_dve, 1)
            dve.wait_ge(s_exp, 1)
            dve.reciprocal(rsum[:, :], ksum[:, :]).then_inc(s_dve, 1)
            dve.wait_ge(s_dve, 3)
            dve.wait_ge(s_c, 1)
            for h in range(LH):
                b = slice(h * LD, (h + 1) * LD)
                ins = dve.tensor_copy(ctx[b, b], ps_c[b, 0, b])
            ins.then_inc(s_cs, 1)
            dve.wait_ge(s_o, 1)
            dve.tensor_scalar(co[:, :], ps_k[:, 0, 0:D], rsum[:, 0:1], float(LD) ** -0.5, ALU.mult, ALU.mult).then_inc(s_os, 1)
            dve.wait_ge(s_m, 1)
            dve.tensor_copy(K.mix[:, :, :], ps_v[:, :, 0:D]).then_inc(s_ms, 1)
            dve.wait_ge(s_ms, 1)


def self_weights(dve, act_exp, step, K, acc_den, kept, has, H, t):
    own, m, top, f1, f2, u, den = (t[n] for n in ("own", "m", "top", "f1", "f2", "u", "den"))
    shape = [P, NT, H]
    step(dve.tensor_tensor(own, K.att_n[:, :, 0:H], K.att_n[:, :, H:2 * H], ALU.add))
    step(dve.scalar_tensor_tensor(own, own, NEG_SLOPE, own, ALU.mult, ALU.max))
    step(dve.tensor_scalar(u, has, BIG, -BIG, ALU.mult, ALU.add))
    step(dve.tensor_tensor(m, kept, u.unsqueeze(2).broadcast_to(shape), ALU.add))
    step(dve.tensor_tensor(top, m, own, ALU.max))
    dve.tensor_tensor(f1, m, top, ALU.subtract)
    step(dve.tensor_tensor(f2, own, top, ALU.subtract))
    act_exp()
    step(dve.tensor_tensor(den, acc_den, f1, ALU.mult))
    step(dve.tensor_tensor(den, den, f2, ALU.add))
    step(dve.reciprocal(den, den))
    step(dve.tensor_tensor(f1, f1, den, ALU.mult))
    step(dve.tensor_tensor(f2, f2, den, ALU.mult))


def weight_tiles(st, H):
    t = {n: st.sbuf(n, [P, NT, H])[:, :, :] for n in ("own", "m", "top", "f1", "f2", "den")}
    t["u"] = st.sbuf("u", [P, NT])[:, :]
    return t


def middle_l1(prog, K, A):
    R = DH1 + 1
    HW = H1 * DH1
    with Stage(prog, "mid1") as st:
        acc = K.acc1
        w = st.sbuf("w", [P, 4, D + 2])
        att = K.xn[:, 0:2, :]
        tmp = K.xn[:, 2:10, :]
        u1 = K.xn[:, 10:14, :].rearrange("p (u a) d -> p u (a d)", a=2)
        u2 = K.xn[:, 14:18, :].rearrange("p (u a) d -> p u (a d)", a=2)
        g = K.xn[:, 18:22, :].rearrange("p (u a) d -> p u (a d)", a=2)
        b1 = K.xn[:, 22:24, :].rearrange("p a d -> p (a d)")
        g_t = K.al[:, 0:2 * HW].rearrange("p (u k n) -> p u k n", u=2, k=4)
        own = K.al[:, 2 * HW:2 * HW + 4 * H1 * R].rearrange("p (u n) -> p u n", u=4)
        tiles = weight_tiles(st, H1)
        f1, f2 = tiles["f1"], tiles["f2"]
        ps_g = st.psum("ps_g", [P, 2, 512])
        ps_h = st.psum("ps_h", [P, 2, 512])
        s_w, s_dve, s_wa, s_f, s_exp, s_u2, s_u, s_g, s_gt, s_gts, s_h, s_tab, s_att, s_out = (
            st.sem(n) for n in ("w", "dve", "wa", "f", "exp", "u2", "u", "g", "gt", "gts", "h", "tab", "att", "out"))
        s_own = [st.sem(f"own{u}") for u in range(4)]
        s_one, s_weights = st.sem("one"), st.sem("weights")
        h2 = K.tab2
        block = st.block()

        @block.sync
        def _(sp):
            sp.dma_start(w[:, :, 0:D], A["g1_w2"].rearrange("(k p) n -> p k n", p=P)).then_inc(s_w, 16)
            load_rows(sp, s_w, att[:, 0, :], A["g1_as2"])
            load_rows(sp, s_w, att[:, 1, :], A["g1_ad2"])
            load_rows(sp, s_w, b1, A["g1_b1"])
            for t in range(NT):
                if t >= 4:
                    sp.wait_ge(s_u2, t - 3)
                sp.dma_start(own[:, t % 4, :], K.table1[t * P:(t + 1) * P, :]).then_inc(s_own[t % 4], 16)
                if t >= 5:
                    sp.wait_ge(s_tab, t - 4)
                    sp.dma_start(K.table2[(t - 5) * P:(t - 4) * P, :], h2[:, t - 5, :]).then_inc(s_out, 16)
            for t in range(NT - 5, NT):
                sp.wait_ge(s_tab, t + 1)
                sp.dma_start(K.table2[t * P:(t + 1) * P, :], h2[:, t, :]).then_inc(s_out, 16)
            sp.wait_ge(s_out, 16 * NT)

        @block.gpsimd
        def _(pool):
            st.clear_stale(pool)
            pool.memset(h2[:, :, D:D + 1], 1.0).then_inc(s_one, 1)
            pool.wait_ge(s_weights, 1)
            for t in range(NT):
                pool.wait_ge(s_own[t % 4], 16 * (t // 4 + 1))
                if t >= 2:
                    pool.wait_ge(s_u, t - 1)
                pool.tensor_tensor(u2[:, t % 2, :].rearrange("p (h d) -> p h d", h=H1),
                                   own[:, t % 4, :].rearrange("p (h r) -> p h r", r=R)[:, :, 0:DH1],
                                   f2[:, t, :].unsqueeze(2).broadcast_to([P, H1, DH1]), ALU.mult).then_inc(s_u2, 1)

        @block.tensor
        def _(pe):
            pe.wait_ge(s_wa, 2)

            def down(t):
                pe.wait_ge(s_gts, t + 1)
                if t >= 2:
                    pe.wait_ge(s_att, t - 1)
                for k in range(4):
                    ins = pe.matmul(ps_h[:, t % 2, 0:D + 2], lhsT=g_t[:, t % 2, k, :], rhs=w[:, k, :], start=(k == 0), stop=(k == 3))
                ins.then_inc(s_h, 1)

            for t in range(NT):
                pe.wait_ge(s_g, t + 1)
                if t >= 2:
                    pe.wait_ge(s_gts, t - 1)
                for k in range(4):
                    ins = pe.transpose(ps_g[:, t % 2, k * P:(k + 1) * P], g[:, t % 2, k * P:(k + 1) * P], K.ident[:, :])
                ins.then_inc(s_gt, 1)
                if t >= 1:
                    down(t - 1)
            down(NT - 1)

        @block.scalar
        def _(act):
            act.wait_ge(s_f, 1)
            act.activation(f1, f1, ACT.Exp).then_inc(s_exp, 1)
            act.activation(f2, f2, ACT.Exp).then_inc(s_exp, 1)
            act.wait_ge(s_one, 1)

            def out(t):
                act.wait_ge(s_h, t + 1)
                act.activation(h2[:, t, 0:D], ps_h[:, t % 2, 0:D], ACT.Copy).then_inc(s_tab, 1)
                act.activation(K.att_n[:, t, 0:2], ps_h[:, t % 2, D:D + 2], ACT.Copy).then_inc(s_att, 1)

            def gelu(t):
                act.wait_ge(s_u, t + 1)
                if t >= 2:
                    act.wait_ge(s_gt, t - 1)
                act.activation(g[:, t % 2, :], u1[:, t % 2, :], ACT.Gelu).then_inc(s_g, 1)

            gelu(0)
            for t in range(NT):
                if t + 1 < NT:
                    gelu(t + 1)
                act.wait_ge(s_gt, t + 1)
                if t >= 2:
                    act.wait_ge(s_h, t - 1)
                act.activation(g_t[:, t % 2, :, :].rearrange("p k n -> p (k n)"), ps_g[:, t % 2, :], ACT.Copy).then_inc(s_gts, 1)
                if t >= 1:
                    out(t - 1)
            out(NT - 1)

        @block.vector
        def _(dve):
            n = [0]

            def step(ins):
                n[0] += 1
                ins.then_inc(s_dve, 1)
                dve.wait_ge(s_dve, n[0])

            def act_exp():
                dve.sem_inc(s_f, 1)
                dve.wait_ge(s_exp, 2)

            ext = acc[:, :, H1 * R:H1 * R + H1 + 1]
            step(dve.tensor_copy(tiles["den"][:, :, :], acc[:, :, DH1:H1 * R:R]))
            self_weights(dve, act_exp, step, K, tiles["den"], ext[:, :, 0:H1], ext[:, :, H1], H1, tiles)
            dve.sem_inc(s_weights, 1)
            dve.wait_ge(s_w, 64)
            for a in range(2):
                step(dve.tensor_tensor(tmp[:, 4 * a:4 * a + 4, :], w[:, :, 0:D], att[:, a, :].unsqueeze(1).broadcast_to([P, 4, D]), ALU.mult))
            for a in range(2):
                dve.tensor_reduce(w[:, :, D + a], tmp[:, 4 * a:4 * a + 4, :], AX, ALU.add).then_inc(s_wa, 1)
            for t in range(NT):
                if t >= 2:
                    dve.wait_ge(s_g, t - 1)
                step(dve.tensor_tensor(u1[:, t % 2, :].rearrange("p (h d) -> p h d", h=H1),
                                       acc[:, t, 0:H1 * R].rearrange("p (h r) -> p h r", r=R)[:, :, 0:DH1],
                                       f1[:, t, :].unsqueeze(2).broadcast_to([P, H1, DH1]), ALU.mult))
                step(dve.tensor_tensor(u1[:, t % 2, :], u1[:, t % 2, :], b1, ALU.add))
                dve.wait_ge(s_u2, t + 1)
                dve.tensor_tensor(u1[:, t % 2, :], u1[:, t % 2, :], u2[:, t % 2, :], ALU.add).then_inc(s_u, 1)


def finish_l1(prog, K, A):
    with Stage(prog, "fin1") as st:
        acc = K.acc2
        tiles = weight_tiles(st, 1)
        f1, f2 = tiles["f1"], tiles["f2"]
        bias = K.xn[:, 0:3, :]
        ps = st.psum("ps", [P, 4, 512])
        s_b, s_dve, s_f, s_exp, s_mm, s_add = (st.sem(n) for n in ("b", "dve", "f", "exp", "mm", "add"))
        block = st.block()

        @block.sync
        def _(sp):
            load_rows(sp, s_b, bias[:, 0, :], A["g1_b2"])
            load_rows(sp, s_b, bias[:, 1, :], A["m1_bo"])

        @block.gpsimd
        def _(pool):
            st.clear_stale(pool)

        @block.tensor
        def _(pe):
            for t in range(NT):
                if t >= 4:
                    pe.wait_ge(s_add, t - 3)
                for k in range(2):
                    ins = pe.matmul(ps[:, t % 4, 0:D], lhsT=K.xn_t[:, k, t * P:(t + 1) * P], rhs=K.mix[:, k, :], start=(k == 0), stop=(k == 1))
                ins.then_inc(s_mm, 1)

        @block.scalar
        def _(act):
            act.wait_ge(s_f, 1)
            act.activation(f1, f1, ACT.Exp).then_inc(s_exp, 1)
            act.activation(f2, f2, ACT.Exp).then_inc(s_exp, 1)

        @block.vector
        def _(dve):
            n = [0]

            def step(ins):
                n[0] += 1
                ins.then_inc(s_dve, 1)
                dve.wait_ge(s_dve, n[0])

            def act_exp():
                dve.sem_inc(s_f, 1)
                dve.wait_ge(s_exp, 2)

            self_weights(dve, act_exp, step, K, acc[:, :, D:D + 1], acc[:, :, D + 1:D + 2], acc[:, :, D + 2], 1, tiles)
            dve.wait_ge(s_b, 32)
            step(dve.tensor_tensor(bias[:, 2, :], bias[:, 0, :], bias[:, 1, :], ALU.add))
            rows, own = acc[:, :, 0:D], K.tab2[:, :, 0:D]
            dve.tensor_tensor(own, own, f2.broadcast_to([P, NT, D]), ALU.mult)
            step(dve.tensor_tensor(rows, rows, f1.broadcast_to([P, NT, D]), ALU.mult))
            step(dve.tensor_tensor(K.x[:, :, :], K.x[:, :, :], bias[:, 2, :].unsqueeze(1).broadcast_to([P, NT, D]), ALU.add))
            step(dve.tensor_tensor(K.x[:, :, :], K.x[:, :, :], rows, ALU.add))
            step(dve.tensor_tensor(K.x[:, :, :], K.x[:, :, :], own, ALU.add))
            for t in range(NT):
                dve.wait_ge(s_mm, t + 1)
                dve.tensor_tensor(K.x[:, t, :], K.x[:, t, :], ps[:, t % 4, 0:D], ALU.add).then_inc(s_add, 1)
            dve.wait_ge(s_add, NT)


def route_l1(prog, K, A):
    with Stage(prog, "route1") as st:
        shape = [P, NT, E1]
        WIDE = NT * E1
        rw = st.sbuf("rw", [P, 2, E1])
        rb = st.sbuf("rb", [P, E1])
        code = st.sbuf("code", [P, E1])
        tile_id = st.sbuf("tile_id", [P, T1])
        tri = st.sbuf("tri", [P, P])
        ones = st.sbuf("ones", [P, P])
        logits, tmp, hot, total = (K.al[:, k * WIDE:(k + 1) * WIDE].rearrange("p (t e) -> p t e", e=E1) for k in range(4))
        upto, before, placed = (K.arena_b[:, k * WIDE:(k + 1) * WIDE].rearrange("p (t e) -> p t e", e=E1) for k in range(3))
        passed = K.arena_b[:, 3 * WIDE:3 * WIDE + T1 * E1].rearrange("p (j e) -> p j e", e=E1)
        best, pick, slot = (st.sbuf(n, [P, NT]) for n in ("best", "pick", "slot"))
        tiles_i, tiles_s = st.sbuf("tiles_i", [P, E1], I32), st.sbuf("tiles_s", [P, E1], I32)
        filled, tiles, ends, first = (st.sbuf(n, [P, E1]) for n in ("filled", "tiles", "ends", "first"))
        which = st.sbuf("which", [P, T1])
        ps_l = st.psum("ps_l", [P, 2, 512])
        ps_c = st.psum("ps_c", [P, 2, 2, 512])
        s_w, s_const, s_logits, s_dve, s_hot, s_count, s_slot = (st.sem(n) for n in ("w", "const", "logits", "dve", "hot", "count", "slot"))
        s_sent = st.sem_sw("sent")
        halves = ((0, 512), (512, WIDE))
        block = st.block()

        @block.sync
        def _(sp):
            sp.dma_start(rw[:, :, :], A["f1_rwt"].rearrange("(k p) n -> p k n", p=P)).then_inc(s_w, 16)
            load_rows(sp, s_w, rb[:, :], A["f1_rb"])

        @block.gpsimd
        def _(pool):
            st.clear_stale(pool)
            pool.memset(ones[:, :], 1.0).then_inc(s_const, 1)
            pool.iota(code[:, :], [[1, E1]], base=E1, channel_multiplier=0, allow_small_or_imprecise_dtypes=True).then_inc(s_const, 1)
            pool.iota(tile_id[:, :], [[1, T1]], base=0, channel_multiplier=0, allow_small_or_imprecise_dtypes=True).then_inc(s_const, 1)
            pool.wait_ge(s_const, 1)
            pool.affine_select(out=tri[:, :], in_=ones[:, :], compare_op=ALU.is_ge, fill=0.0, base=0,
                               pattern=[[1, P]], channel_multiplier=-1).then_inc(s_const, 1)
            pool.wait_ge(s_slot, 1)
            for t in range(NT):
                pool.indirect_dma_start(K.slots1, bass.IndirectOffsetOnAxis(ap=K.slot_to[:, t:t + 1], axis=0), K.xn[:, t, :], None).then_inc(s_sent, 16)
            pool.wait_ge(s_sent, 16 * NT)

        @block.tensor
        def _(pe):
            pe.wait_ge(s_w, 32)
            for t in range(NT):
                for k in range(2):
                    ins = pe.matmul(ps_l[:, t // 16, (t % 16) * E1:(t % 16 + 1) * E1], lhsT=K.xn_t[:, k, t * P:(t + 1) * P], rhs=rw[:, k, :], start=(k == 0), stop=(k == 1))
            ins.then_inc(s_logits, 1)
            pe.wait_ge(s_const, 4)
            pe.wait_ge(s_hot, 1)
            flat = hot.rearrange("p t e -> p (t e)")
            for m, sums in enumerate((tri, ones)):
                for b, (lo, hi) in enumerate(halves):
                    ins = pe.matmul(ps_c[:, m, b, 0:hi - lo], lhsT=sums[:, :], rhs=flat[:, lo:hi], start=True, stop=True)
            ins.then_inc(s_count, 1)

        @block.vector
        def _(dve):
            step = Steps(dve, s_dve)
            dve.wait_ge(s_w, 32)
            dve.wait_ge(s_const, 4)
            dve.wait_ge(s_logits, 1)
            for b, (lo, hi) in enumerate(halves):
                step(dve.tensor_copy(logits.rearrange("p t e -> p (t e)")[:, lo:hi], ps_l[:, b, 0:hi - lo]))
            first_best(dve, step, logits, rb[:, :], code[:, :], E1, tmp, best[:, :], hot, pick[:, :])
            dve.sem_inc(s_hot, 1)
            dve.wait_ge(s_count, 1)
            for b, (lo, hi) in enumerate(halves):
                step(dve.tensor_copy(total.rearrange("p t e -> p (t e)")[:, lo:hi], ps_c[:, 1, b, 0:hi - lo]))
            for e in range(E1):
                ins = dve.tensor_tensor_scan(upto[:, :, e], total[:, :, e], total[:, :, e], 0.0, ALU.add, ALU.max)
            step(ins)
            step(dve.tensor_scalar(filled[:, :], upto[:, NT - 1, :], float(P - 1), None, ALU.add))
            step(dve.tensor_copy(tiles_i[:, :], filled[:, :]))
            step(dve.tensor_scalar(tiles_s[:, :], tiles_i[:, :], P.bit_length() - 1, None, ALU.logical_shift_right))
            step(dve.tensor_copy(tiles[:, :], tiles_s[:, :]))
            step(dve.tensor_tensor_scan(ends[:, :], tiles[:, :], tiles[:, :], 0.0, ALU.add, ALU.max))
            step(dve.tensor_tensor(first[:, :], ends[:, :], tiles[:, :], ALU.subtract))
            step(dve.tensor_scalar(first[:, :], first[:, :], float(P), -1.0, ALU.mult, ALU.add))
            step(dve.tensor_tensor(before, upto, total, ALU.subtract))
            for b, (lo, hi) in enumerate(halves):
                part = before.rearrange("p t e -> p (t e)")[:, lo:hi]
                step(dve.tensor_tensor(part, part, ps_c[:, 0, b, 0:hi - lo], ALU.add))
            step(dve.tensor_tensor(before, before, first[:, :].unsqueeze(1).broadcast_to(shape), ALU.add))
            step(dve.tensor_tensor(placed, before, hot, ALU.mult))
            step(dve.tensor_reduce(slot[:, :], placed, AX, ALU.add))
            dve.tensor_copy(K.slot_to[:, :], slot[:, :]).then_inc(s_slot, 1)
            step(dve.tensor_tensor(passed, ends[:, :].unsqueeze(1).broadcast_to([P, T1, E1]), tile_id[:, :].unsqueeze(2).broadcast_to([P, T1, E1]), ALU.is_le))
            step(dve.tensor_reduce(which[:, :], passed, AX, ALU.add))
            step(dve.tensor_scalar(which[:, :], which[:, :], float(E1 - 1), None, ALU.min))
            step(dve.tensor_copy(K.expert_at[:, :], which[:, :]))


def experts_l1(prog, K, A):
    with Stage(prog, "moe1") as st:
        Q, U2 = 4, 2
        sizes = {"rows": D, "w": 2 * F1 + D, "xs_t": 2 * P, "h_t": P, "y": D}
        at, tile = 0, {}
        for name, n in sizes.items():
            tile[name] = K.arena_a[:, at:at + Q * n].rearrange("p (q n) -> p q n", q=Q)
            at += Q * n
        rows, w, xs_t, h_t, y = tile.values()
        w1, w2 = w[:, :, 0:2 * F1], w[:, :, 2 * F1:]
        b1 = st.sbuf("b1", [F1, E1])
        ps_t, ps_h, ps_y = (st.psum(n, [P, U2, 512]) for n in ("ps_t", "ps_h", "ps_y"))
        s_in = [st.sem(f"in{q}") for q in range(Q)]
        s_out = [st.sem_sw(f"out{q}") for q in range(Q)]
        s_b, s_one, s_t, s_xt, s_h, s_ht, s_y, s_yb = (st.sem(n) for n in ("b", "one", "t", "xt", "h", "ht", "y", "yb"))
        turns = T1 // Q
        block = st.block()

        @block.sync
        def _(sp):
            sp.dma_start(b1[:, :], A["f1_b1"]).then_inc(s_b, 16)
            with sp.Fori(0, turns) as i:
                for q in range(Q):
                    j = i * Q + q
                    expert = sp.value_load(K.expert_at[0:1, bass.ds(j, 1)], min_val=0, max_val=E1 - 1)
                    sp.wait_ge(s_y, j + 1)
                    sp.dma_start(w[:, q, :], A["f1_w"][expert]).then_inc(s_in[q], 16)

        @block.tensor
        def _(pe):
            def turn_rows(i, q):
                j = i * Q + q
                pe.wait_ge(s_in[q], 32 * (i + 1))
                pe.wait_ge(s_xt, j + 1)
                for k in range(2):
                    ins = pe.transpose(ps_t[:, q % U2, k * P:(k + 1) * P], rows[:, q, k * P:(k + 1) * P], K.ident[:, :])
                ins.then_inc(s_t, 1)

            def up(i, q):
                j = i * Q + q
                pe.wait_ge(s_xt, j + 1 + U2)
                pe.wait_ge(s_ht, j + 1)
                for k in range(2):
                    ins = pe.matmul(ps_h[0:F1, q % U2, 0:P], lhsT=w1[:, q, k * F1:(k + 1) * F1], rhs=xs_t[:, q, k * P:(k + 1) * P], start=(k == 0), stop=(k == 1))
                ins.then_inc(s_h, 1)

            def down(i, q):
                j = i * Q + q
                pe.wait_ge(s_ht, j + 1 + U2)
                pe.wait_ge(s_yb, j + 1)
                pe.matmul(ps_y[:, q % U2, 0:D], lhsT=h_t[0:F1 + 1, q, :], rhs=w2[0:F1 + 1, q, :], start=True, stop=True).then_inc(s_y, 1)

            def turn(i, head=False, tail=False):
                for q in range(Q):
                    if q + 1 < Q:
                        turn_rows(i, q + 1)
                    elif not tail:
                        turn_rows(i + 1, 0)
                    up(i, q)
                    if q:
                        down(i, q - 1)
                    elif not head:
                        down(i - 1, Q - 1)

            pe.sem_inc(s_h, Q)
            pe.sem_inc(s_y, Q)
            pe.wait_ge(s_one, 1)
            turn_rows(0, 0)
            turn(0, head=True)
            with pe.Fori(0, turns - 2) as i:
                turn(i + 1)
            turn(turns - 1, tail=True)
            down(turns - 1, Q - 1)

        @block.scalar
        def _(act):
            def load(i, q):
                j = i * Q + q
                act.wait_ge(s_y, j + 1)
                act.dma_start(rows[:, q, :], K.slots1[bass.ds(j * P, P), :]).then_inc(s_in[q], 16)

            act.sem_inc(s_ht, U2)
            load(0, 0)
            load(0, 1)
            act.wait_ge(s_b, 16)

            def turn(i, tail=False):
                for q in range(Q):
                    j = i * Q + q
                    if q + 2 < Q:
                        load(i, q + 2)
                    elif not tail:
                        load(i + 1, q + 2 - Q)
                    expert = act.value_load(K.expert_at[0:1, bass.ds(j, 1)], min_val=0, max_val=E1 - 1)
                    act.wait_ge(s_h, j + 1 + Q)
                    act.wait_ge(s_y, j + 1)
                    act.activation(h_t[0:F1, q, :], ps_h[0:F1, q % U2, 0:P], ACT.Relu, bias=b1[:, bass.ds(expert, 1)]).then_inc(s_ht, 1)

            with act.Fori(0, turns - 1) as i:
                turn(i)
            turn(turns - 1, tail=True)

        @block.vector
        def _(dve):
            def turned(i, q):
                j = i * Q + q
                dve.wait_ge(s_t, j + 1)
                dve.wait_ge(s_h, j + 1)
                dve.tensor_copy(xs_t[:, q, :], ps_t[:, q % U2, 0:2 * P]).then_inc(s_xt, 1)

            def result(i, q, stored=True):
                j = i * Q + q
                dve.wait_ge(s_y, j + 1 + Q)
                if stored:
                    dve.wait_ge(s_out[q], 16 * i)
                dve.tensor_scalar(y[:, q, :], ps_y[:, q % U2, 0:D], 0.0, None, ALU.max).then_inc(s_yb, 1)

            def turn(i, tail=False):
                for q in range(Q):
                    if q + 1 < Q:
                        turned(i, q + 1)
                    elif not tail:
                        turned(i + 1, 0)
                    if isinstance(i, int) and i * Q + q == 0:
                        continue
                    back = (i, q - 1) if q else (i - 1, Q - 1)
                    result(*back, stored=not (isinstance(i, int) and back[0] == 0))

            dve.sem_inc(s_xt, U2)
            dve.sem_inc(s_yb, U2)
            dve.memset(h_t[F1:F1 + 1, :, :], 1.0).then_inc(s_one, 1)
            turned(0, 0)
            turn(0)
            turn(1)
            with dve.Fori(0, turns - 3) as i:
                turn(i + 2)
            turn(turns - 1, tail=True)
            result(turns - 1, Q - 1)

        @block.gpsimd
        def _(pool):
            st.clear_stale(pool)
            with pool.Fori(0, turns) as i:
                for q in range(Q):
                    j = i * Q + q
                    pool.wait_ge(s_yb, j + 1 + U2)
                    pool.nop(nofuse=True)
                    pool.dma_start(K.y_slots1[bass.ds(j * P, P), :], y[:, q, :]).then_inc(s_out[q], 16)
            for q in range(Q):
                pool.wait_ge(s_out[q], 16 * turns)


def combine_l1(prog, K, out):
    with Stage(prog, "join1") as st:
        y = K.xn
        s_y = [st.sem_sw(f"y{c}") for c in range(NT // U)]
        s_sum, s_out = st.sem("sum"), st.sem("out")
        block = st.block()

        @block.gpsimd
        def _(pool):
            st.clear_stale(pool)
            for t in range(NT):
                pool.indirect_dma_start(y[:, t, :], None, K.y_slots1, bass.IndirectOffsetOnAxis(ap=K.slot_to[:, t:t + 1], axis=0)).then_inc(s_y[t // U], 16)

        @block.vector
        def _(dve):
            for c in range(NT // U):
                dve.wait_ge(s_y[c], 16 * U)
                part = y[:, c * U:(c + 1) * U, :]
                dve.tensor_tensor(part, part, K.x[:, c * U:(c + 1) * U, :], ALU.add).then_inc(s_sum, 1)

        @block.sync
        def _(sp):
            for c in range(NT // U):
                sp.wait_ge(s_sum, c + 1)
                whole = U if c < NT // U - 1 else U - 1
                sp.dma_start(out[c * U * P:(c * U + whole) * P, :].rearrange("(t p) d -> p t d", p=P), y[:, c * U:c * U + whole, :]).then_inc(s_out, 16)
            sp.dma_start(out[(NT - 1) * P:N, :], y[0:NLAST, NT - 1, :]).then_inc(s_out, 16)
            sp.wait_ge(s_out, 16 * (NT // U + 1))


def stages(prog, K, A, out):
    order_edges(prog, K, A)
    edge_items(prog, K, A["x"], A["dst"])
    layer_norm(prog, K, "ln0")
    project_l0(prog, K, A)
    edge_scores_l0(prog, K, A)
    segment_softmax(prog, K, "soft0", H0, C0)
    aggregate(prog, K, "sum0", H0, H0 * (DH0 + 1), K.table0, K.acc0, blank=K.slots1)
    finish_l0(prog, K, A)
    layer_norm(prog, K, "ln1")
    route_l0(prog, K, A)
    experts_l0(prog, K, A)
    combine_l0(prog, K)
    layer_norm(prog, K, "ln2")
    linear_attention_l1(prog, K, A)
    project_l1(prog, K, A)
    for H, C, RW, table, acc in ((H1, C1, H1 * (DH1 + 1), K.table1, K.acc1),
                                 (1, C2, D + 1, K.table2, K.acc2)):
        keep = K.al[:, WS * H:WS * (2 * H + 1)].rearrange("p (s h) -> p s h", h=H + 1)
        edge_scores_l1(prog, K, f"score_h{H}", H, C)
        segment_softmax(prog, K, f"soft_h{H}", H, C, keep)
        aggregate(prog, K, f"sum_h{H}", H, RW, table, acc, keep)
        if H == H1:
            middle_l1(prog, K, A)
    finish_l1(prog, K, A)
    layer_norm(prog, K, "ln3")
    route_l1(prog, K, A)
    experts_l1(prog, K, A)
    combine_l1(prog, K, out)


class Keep:
    pass


def build(nc, A, out):
    with ExitStack() as stack:
        prog = Program(nc, stack)
        K = Keep()
        K.x = prog.sbuf("x", [P, NT, D])
        K.xn = prog.sbuf("xn", [P, NT, D])
        K.xn_t = prog.sbuf("xn_t", [P, 2, NPAD])
        K.ident = prog.sbuf("ident", [P, P])
        K.iota_row = prog.sbuf("iota_row", [P, P])
        K.iota_part = prog.sbuf("iota_part", [P, 1])
        K.eps = prog.sbuf("eps", [P, 1])
        K.src_col = prog.sbuf("src_col", [P, WS], I32)
        K.rel_col = prog.sbuf("rel_col", [P, WS])
        K.last_col = prog.sbuf("last_col", [P, WS])
        K.hi_col = prog.sbuf("hi_col", [P, WS], BF16)
        K.window = prog.sbuf("window", [P, W], I32)
        K.src_s = prog.dram("src_s", [NB, EB], I32)
        K.dst_s = prog.dram("dst_s", [NB, EB], I32)
        K.attr_s = prog.dram("attr_s", [3 * NB, EB])
        K.pair_a, K.pair_b = (prog.dram(f"pair_{n}", [NB * EB, 2], I32) for n in "ab")
        K.attr_a, K.attr_b = (prog.dram(f"attr_{n}", [NB * EB, 3]) for n in "ab")
        K.slots1 = prog.dram("slots1", [T1 * P, D])
        K.y_slots1 = prog.dram("y_slots1", [T1 * P, D])
        K.expert_at = prog.sbuf("expert_at", [P, T1], I32)
        K.slots = prog.dram("slots", [E0 * CAP, D])
        K.key_flat = prog.dram("key_flat", [WS * P + 2])
        K.attr_parts = prog.dram("attr_parts", [ENC_ROWS // 3, W * EB], BF16)
        K.edge_rows = prog.dram("edge_rows", [W // 2, 2 * 2 * EB], BF16)
        K.pen_prev = prog.dram("pen_prev", [WS * P])
        K.pen_next = prog.dram("pen_next", [WS * P])
        K.att_table = prog.dram("att_table", [NPAD, H0])
        K.table0 = prog.dram("table0", [NPAD, H0 * (DH0 + 1)])
        K.arena_a = prog.sbuf("arena_a", [P, NT * 526])
        K.arena_b = prog.sbuf("arena_b", [P, NT * H0 * (DH0 + 1)])
        K.tab0 = K.arena_b[:, :].rearrange("p (t r) -> p t r", t=NT)
        K.acc0 = K.arena_a[:, 0:NT * H0 * (DH0 + 1)].rearrange("p (t r) -> p t r", t=NT)
        K.al = prog.sbuf("al", [P, WS * (2 * H1 + 1)])
        K.slot_to = prog.sbuf("slot_to", [P, NT], I32)
        K.slot_from = prog.sbuf("slot_from", [P, NT], I32)
        K.gate = prog.sbuf("gate", [P, NT])
        K.y_slots = prog.dram("y_slots", [E0 * CAP, D])
        K.table1 = prog.dram("table1", [NPAD, H1 * (DH1 + 1)])
        K.table2 = prog.dram("table2", [NPAD, D + 1])
        width = H1 * (DH1 + 1) + H1 + 1
        K.acc1 = K.arena_a[:, 0:NT * (width + width % 2)].rearrange("p (t c) -> p t c", t=NT)
        K.acc2 = K.arena_a[:, 0:NT * (D + 3)].rearrange("p (t c) -> p t c", t=NT)
        K.tab2 = K.arena_b[:, 0:NT * (D + 1)].rearrange("p (t c) -> p t c", t=NT)
        K.att_n = prog.sbuf("att_n", [P, NT, 2 * H0])
        K.mix = prog.sbuf("mix", [P, 2, D])
        K.gath = [nc.alloc_semaphore(f"gath{q}") for q in range(5)]
        K.gathered = [0] * 5
        stages(prog, K, A, out)


def kernel(**inputs):
    import numpy as _np
    import concourse.bacc as _bacc
    from concourse import mybir as _mybir
    from concourse.bass_utils import run_bass_kernel_spmd as _run

    a = {k: _np.asarray(v) for k, v in inputs.items()}
    slots = NB * EB

    def padded(v, fill):
        return _np.concatenate([v, _np.full((slots - E,) + v.shape[1:], fill, v.dtype)])

    g0, m0, f0, g1, m1, f1 = "L0_gnn_", "L0_mix_", "L0_ffn_", "L1_gnn_", "L1_mix_", "L1_ffn_"
    A = {
        "x": a["x"],
        "src": padded(a["src"], 0).reshape(NB, EB),
        "dst": padded(a["dst"], NPAD + P).reshape(NB, EB),
        "attr": padded(a["edge_attr_3"], 0).T.reshape(3 * NB, EB),
        "pair": _np.stack([padded(a["src"], 0), padded(a["dst"], NPAD + P)], 1), "attr_rows": padded(a["edge_attr_3"], 0),
        "g0_wt": a[g0 + "W"].T, "g0_as": a[g0 + "a_src"].reshape(1, -1), "g0_ad": a[g0 + "a_dst"].reshape(1, -1),
        "g0_enc": _np.tile(_np.concatenate([a[g0 + "edge_W"].T] * 3 + [a[g0 + "edge_b"].reshape(1, -1)]), (3, 1)), "g0_b": a[g0 + "bias"].reshape(1, -1),
        "m0_wq": a[m0 + "wq"], "m0_wkt": a[m0 + "wk"].T, "m0_wvt": a[m0 + "wv"].T, "m0_wot": a[m0 + "wo"].T,
        "m0_bo": a[m0 + "bo"].reshape(1, -1),
        "m0_kg": a[m0 + "ln_k_g"].reshape(1, -1), "m0_kb": a[m0 + "ln_k_b"].reshape(1, -1),
        "m0_vg": a[m0 + "ln_v_g"].reshape(1, -1), "m0_vb": a[m0 + "ln_v_b"].reshape(1, -1),
        "f0_gw": a[f0 + "gate_w"], "f0_gb": a[f0 + "gate_b"].reshape(1, -1),
        "f0_w1": a[f0 + "w1"], "f0_b1": a[f0 + "b1"].reshape(E0, F0 // P, P).transpose(2, 0, 1).reshape(P, -1),
        "f0_w2": a[f0 + "w2"], "f0_b2": a[f0 + "b2"].reshape(1, -1),
        "g1_w1": a[g1 + "W1"], "g1_as1": a[g1 + "att_src1"].reshape(1, -1), "g1_ad1": a[g1 + "att_dst1"].reshape(1, -1),
        "g1_b1": a[g1 + "b1"].reshape(1, -1), "g1_w2": a[g1 + "W2"], "g1_as2": a[g1 + "att_src2"].reshape(1, -1),
        "g1_ad2": a[g1 + "att_dst2"].reshape(1, -1), "g1_b2": a[g1 + "b2"].reshape(1, -1),
        "m1_wqt": a[m1 + "W_qkv"][:, 0:LH * LD].T, "m1_wkv": a[m1 + "W_qkv"][:, LH * LD:], "m1_wo": a[m1 + "W_out"],
        "m1_bo": a[m1 + "b_out"].reshape(1, -1),
        "f1_rwt": a[f1 + "router_w"].T, "f1_rb": a[f1 + "router_b"].reshape(1, -1),
        "f1_w": _np.concatenate([
            a[f1 + "W1"].reshape(E1, 2, P, F1).transpose(0, 2, 1, 3).reshape(E1, P, 2 * F1),
            _np.concatenate([a[f1 + "W2"].reshape(E1, F1, D), a[f1 + "b2"].reshape(E1, 1, D),
                             _np.zeros((E1, P - F1 - 1, D), a[f1 + "W2"].dtype)], 1)], 2),
        "f1_b1": a[f1 + "b1"].reshape(E1, F1).T,
    }
    A = {k: _np.ascontiguousarray(v) for k, v in A.items()}
    nc = _bacc.Bacc("TRN2", target_bir_lowering=False, num_devices=1)
    arrays, aps = {}, {}
    for name, v in A.items():
        arrays[f"in_{name}"] = v
        aps[name] = nc.dram_tensor(f"in_{name}", v.shape, _mybir.dt.from_np(v.dtype), kind="ExternalInput").ap()
    out = nc.dram_tensor("out_0", (N, D), _mybir.dt.float32, kind="ExternalOutput").ap()
    build(nc, aps, out)
    r = _run(nc, [arrays], core_ids=[0])
    return r.results[0]["out_0"]
```
